# Optimizing a Trainium2 kernel written in Bass

```python
import numpy as np
import jax
import jax.numpy as jnp

def _softmax(x, axis=-1):
    return jax.nn.softmax(x, axis=axis)

def _gelu(x):
    return jax.nn.gelu(x, approximate=True)

def _silu(x):
    return jax.nn.silu(x)

def _sigmoid(x):
    return jax.nn.sigmoid(x)

def _layernorm(x, axis=-1, eps=1e-05):
    m = jnp.mean(x, axis=axis, keepdims=True)
    v = jnp.var(x, axis=axis, keepdims=True)
    return (x - m) / jnp.sqrt(v + eps)

def _scatter_add(tgt, idx, src, axis=0):
    return tgt.at[idx].add(src)

def _segment_sum(src, seg, n):
    return jax.ops.segment_sum(src, seg, n)
kernel_name = 'mk_adaln_d2_jaxref_r8_9d8ab7'

def setup_inputs(seed: int=0):
    np.random.seed(seed)
    _w = jnp.asarray

    def _L0_attn_setup():
        import jax, jax.numpy as jnp
        import numpy as np
        D_MODEL = 128
        N_HEADS = 16
        D_FF = 512
        D_STATE = 16
        D_CONV = 4
        EXPAND = 2
        D_INNER = D_MODEL * EXPAND
        DT_RANK = D_MODEL // 16
        BATCH = 4
        SEQ = 128

        def _ln(x, w, b):
            m = jnp.mean(x, axis=-1, keepdims=True)
            v = jnp.var(x, axis=-1, keepdims=True)
            return (x - m) / jnp.sqrt(v + 1e-05) * w + b
        key = jax.random.key(seed)
        ks = jax.random.split(key, 32)
        s = 0.02
        inp = {}
        inp['x'] = jax.random.normal(ks[0], (BATCH, SEQ, D_MODEL), jnp.float32)
        inp['ln1_w'] = jnp.ones((D_MODEL,), jnp.float32)
        inp['ln1_b'] = jnp.zeros((D_MODEL,), jnp.float32)
        inp['ln2_w'] = jnp.ones((D_MODEL,), jnp.float32)
        inp['ln2_b'] = jnp.zeros((D_MODEL,), jnp.float32)
        inp['q_w'] = jax.random.normal(ks[1], (D_MODEL, D_MODEL), jnp.float32) * s
        inp['q_b'] = jnp.zeros((D_MODEL,), jnp.float32)
        inp['k_w'] = jax.random.normal(ks[2], (D_MODEL, D_MODEL), jnp.float32) * s
        inp['k_b'] = jnp.zeros((D_MODEL,), jnp.float32)
        inp['v_w'] = jax.random.normal(ks[3], (D_MODEL, D_MODEL), jnp.float32) * s
        inp['v_b'] = jnp.zeros((D_MODEL,), jnp.float32)
        inp['o_w'] = jax.random.normal(ks[4], (D_MODEL, D_MODEL), jnp.float32) * s
        inp['o_b'] = jnp.zeros((D_MODEL,), jnp.float32)
        inp['in_proj_w'] = jax.random.normal(ks[5], (D_MODEL, 2 * D_INNER), jnp.float32) * s
        inp['conv_w'] = jax.random.normal(ks[6], (D_INNER, D_CONV), jnp.float32) * 0.2
        inp['conv_b'] = jnp.zeros((D_INNER,), jnp.float32)
        inp['x_proj_w'] = jax.random.normal(ks[7], (D_INNER, DT_RANK + 2 * D_STATE), jnp.float32) * s
        dt_std = DT_RANK ** (-0.5)
        inp['dt_w'] = jax.random.uniform(ks[8], (DT_RANK, D_INNER), jnp.float32, -dt_std, dt_std)
        dt = jnp.exp(jax.random.uniform(ks[9], (D_INNER,), jnp.float32) * (np.log(0.1) - np.log(0.001)) + np.log(0.001))
        inp['dt_b'] = dt + jnp.log(-jnp.expm1(-dt))
        A = jnp.tile(jnp.arange(1, D_STATE + 1, dtype=jnp.float32), (D_INNER, 1))
        inp['A_log'] = jnp.log(A)
        inp['D_param'] = jnp.ones((D_INNER,), jnp.float32)
        inp['ssm_out_w'] = jax.random.normal(ks[10], (D_INNER, D_MODEL), jnp.float32) * s
        inp['mix_weight'] = jnp.full((D_MODEL,), 0.5, jnp.float32)
        inp['ffn_w1'] = jax.random.normal(ks[11], (D_MODEL, D_FF), jnp.float32) * s
        inp['ffn_b1'] = jnp.zeros((D_FF,), jnp.float32)
        inp['ffn_w2'] = jax.random.normal(ks[12], (D_FF, D_MODEL), jnp.float32) * s
        inp['ffn_b2'] = jnp.zeros((D_MODEL,), jnp.float32)
        return inp
    _L0_attn_in = _L0_attn_setup()

    def _L0_ffn_setup():
        import jax, jax.numpy as jnp
        import numpy as np
        B, T, C = (2, 64, 128)
        I = 512
        E = 8
        K = 2
        key = jax.random.key(seed)
        ks = jax.random.split(key, 8)
        s = 0.02
        return {'x': jax.random.normal(ks[0], (B, T, C), jnp.float32), 'Wr1': jax.random.normal(ks[1], (C, C // 4), jnp.float32) * s, 'br1': jnp.zeros((C // 4,), jnp.float32), 'Wr2': jax.random.normal(ks[2], (C // 4, E), jnp.float32) * s, 'br2': jnp.zeros((E,), jnp.float32), 'Ws1': jax.random.normal(ks[3], (C, I), jnp.float32) * s, 'bs1': jnp.zeros((I,), jnp.float32), 'Ws2': jax.random.normal(ks[4], (I, C), jnp.float32) * s, 'bs2': jnp.zeros((C,), jnp.float32), 'We1': jax.random.normal(ks[5], (E, C, I), jnp.float32) * s, 'be1': jnp.zeros((E, I), jnp.float32), 'We2': jax.random.normal(ks[6], (E, I, C), jnp.float32) * s, 'be2': jnp.zeros((E, C), jnp.float32)}
    _L0_ffn_in = _L0_ffn_setup()
    _L0_c = _w((lambda *s: np.random.randn(*s).astype(np.float32) * 0.05)(8, 128))
    _L0_wmod = _w((lambda *s: np.random.randn(*s).astype(np.float32) * 0.05)(128, 6 * 128) * 128 ** (-0.5))

    def _L1_attn_setup():
        import jax, jax.numpy as jnp
        import numpy as np
        S, B, E = (512, 2, 128)
        H = 8
        WIN = 32

        def _band_scores(q, k_pad, seq_len, band):

            def f(o):
                ks = jax.lax.dynamic_slice_in_dim(k_pad, o, seq_len, axis=1)
                return jnp.einsum('bshd,bshd->bsh', q, ks)
            s = jax.lax.map(f, jnp.arange(band))
            return jnp.moveaxis(s, 0, -1)

        def _band_av(probs, v_pad, seq_len, band):
            bsz, _, heads, _ = probs.shape
            d = v_pad.shape[-1]

            def body(carry, o):
                vs = jax.lax.dynamic_slice_in_dim(v_pad, o, seq_len, axis=1)
                p = jax.lax.dynamic_slice_in_dim(probs, o, 1, axis=3)
                return (carry + p * vs, None)
            init = jnp.zeros((bsz, seq_len, heads, d), probs.dtype)
            out, _ = jax.lax.scan(body, init, jnp.arange(band))
            return out
        key = jax.random.key(seed)
        ks = jax.random.split(key, 7)
        val = jax.random.normal(ks[0], (S, B, E), dtype=jnp.float32)
        Wq = jax.random.normal(ks[1], (E, E), dtype=jnp.float32) * 0.02
        bq = jax.random.normal(ks[2], (E,), dtype=jnp.float32) * 0.02
        Wk = jax.random.normal(ks[3], (E, E), dtype=jnp.float32) * 0.02
        bk = jax.random.normal(ks[4], (E,), dtype=jnp.float32) * 0.02
        Wv = jax.random.normal(ks[5], (E, E), dtype=jnp.float32) * 0.02
        bv = jax.random.normal(ks[6], (E,), dtype=jnp.float32) * 0.02
        return {'val': val, 'Wq': Wq, 'bq': bq, 'Wk': Wk, 'bk': bk, 'Wv': Wv, 'bv': bv}
    _L1_attn_in = _L1_attn_setup()

    def _L1_ffn_setup():
        import jax, jax.numpy as jnp
        import numpy as np
        DIM = 128

        def _reference_tuple_inner(x, W_r, W_k, W_v, mu_r, mu_k):
            B, T, C = x.shape
            x_prev = jnp.concatenate([jnp.zeros((B, 1, C), x.dtype), x[:, :-1, :]], axis=1)
            xr = mu_r * x + (1.0 - mu_r) * x_prev
            xk = mu_k * x + (1.0 - mu_k) * x_prev
            r = jax.nn.sigmoid(jnp.einsum('btc,dc->btd', xr, W_r))
            k = jnp.einsum('btc,dc->btd', xk, W_k)
            k_act = jnp.square(jax.nn.relu(k))
            out = r * jnp.einsum('btc,dc->btd', k_act, W_v)
            new_state = x[:, -1, :]
            return (out, new_state)
        key = jax.random.key(seed)
        ks = jax.random.split(key, 6)
        B, T, C = (8, 256, DIM)
        x = jax.random.normal(ks[0], (B, T, C), dtype=jnp.float32)
        s = 1.0 / np.sqrt(C)
        W_r = jax.random.uniform(ks[1], (C, C), jnp.float32, -s, s)
        W_k = jax.random.uniform(ks[2], (C, C), jnp.float32, -s, s)
        W_v = jax.random.uniform(ks[3], (C, C), jnp.float32, -s, s)
        mu_r = jax.random.uniform(ks[4], (C,), jnp.float32)
        mu_k = jax.random.uniform(ks[5], (C,), jnp.float32)
        return {'x': x, 'W_r': W_r, 'W_k': W_k, 'W_v': W_v, 'mu_r': mu_r, 'mu_k': mu_k}
    _L1_ffn_in = _L1_ffn_setup()
    _L1_c = _w((lambda *s: np.random.randn(*s).astype(np.float32) * 0.05)(8, 128))
    _L1_wmod = _w((lambda *s: np.random.randn(*s).astype(np.float32) * 0.05)(128, 6 * 128) * 128 ** (-0.5))
    _d = {'L0_attn_x': _L0_attn_in['x'], 'L0_attn_ln1_w': _L0_attn_in['ln1_w'], 'L0_attn_ln1_b': _L0_attn_in['ln1_b'], 'L0_attn_ln2_w': _L0_attn_in['ln2_w'], 'L0_attn_ln2_b': _L0_attn_in['ln2_b'], 'L0_attn_q_w': _L0_attn_in['q_w'], 'L0_attn_q_b': _L0_attn_in['q_b'], 'L0_attn_k_w': _L0_attn_in['k_w'], 'L0_attn_k_b': _L0_attn_in['k_b'], 'L0_attn_v_w': _L0_attn_in['v_w'], 'L0_attn_v_b': _L0_attn_in['v_b'], 'L0_attn_o_w': _L0_attn_in['o_w'], 'L0_attn_o_b': _L0_attn_in['o_b'], 'L0_attn_in_proj_w': _L0_attn_in['in_proj_w'], 'L0_attn_conv_w': _L0_attn_in['conv_w'], 'L0_attn_conv_b': _L0_attn_in['conv_b'], 'L0_attn_x_proj_w': _L0_attn_in['x_proj_w'], 'L0_attn_dt_w': _L0_attn_in['dt_w'], 'L0_attn_dt_b': _L0_attn_in['dt_b'], 'L0_attn_A_log': _L0_attn_in['A_log'], 'L0_attn_D_param': _L0_attn_in['D_param'], 'L0_attn_ssm_out_w': _L0_attn_in['ssm_out_w'], 'L0_attn_mix_weight': _L0_attn_in['mix_weight'], 'L0_attn_ffn_w1': _L0_attn_in['ffn_w1'], 'L0_attn_ffn_b1': _L0_attn_in['ffn_b1'], 'L0_attn_ffn_w2': _L0_attn_in['ffn_w2'], 'L0_attn_ffn_b2': _L0_attn_in['ffn_b2'], 'L0_ffn_Wr1': _L0_ffn_in['Wr1'], 'L0_ffn_br1': _L0_ffn_in['br1'], 'L0_ffn_Wr2': _L0_ffn_in['Wr2'], 'L0_ffn_br2': _L0_ffn_in['br2'], 'L0_ffn_Ws1': _L0_ffn_in['Ws1'], 'L0_ffn_bs1': _L0_ffn_in['bs1'], 'L0_ffn_Ws2': _L0_ffn_in['Ws2'], 'L0_ffn_bs2': _L0_ffn_in['bs2'], 'L0_ffn_We1': _L0_ffn_in['We1'], 'L0_ffn_be1': _L0_ffn_in['be1'], 'L0_ffn_We2': _L0_ffn_in['We2'], 'L0_ffn_be2': _L0_ffn_in['be2'], 'L0_c': _L0_c, 'L0_wmod': _L0_wmod, 'L1_attn_Wq': _L1_attn_in['Wq'], 'L1_attn_bq': _L1_attn_in['bq'], 'L1_attn_Wk': _L1_attn_in['Wk'], 'L1_attn_bk': _L1_attn_in['bk'], 'L1_attn_Wv': _L1_attn_in['Wv'], 'L1_attn_bv': _L1_attn_in['bv'], 'L1_ffn_W_r': _L1_ffn_in['W_r'], 'L1_ffn_W_k': _L1_ffn_in['W_k'], 'L1_ffn_W_v': _L1_ffn_in['W_v'], 'L1_ffn_mu_r': _L1_ffn_in['mu_r'], 'L1_ffn_mu_k': _L1_ffn_in['mu_k'], 'L1_c': _L1_c, 'L1_wmod': _L1_wmod}
    _x0 = _d['L0_attn_x']
    _d['L0_attn_x'] = jax.random.normal(jax.random.fold_in(jax.random.key(seed), 1), (8, 512, 128), dtype=_x0.dtype)
    del _x0
    return _d

def reference(L0_attn_x, L0_attn_ln1_w, L0_attn_ln1_b, L0_attn_ln2_w, L0_attn_ln2_b, L0_attn_q_w, L0_attn_q_b, L0_attn_k_w, L0_attn_k_b, L0_attn_v_w, L0_attn_v_b, L0_attn_o_w, L0_attn_o_b, L0_attn_in_proj_w, L0_attn_conv_w, L0_attn_conv_b, L0_attn_x_proj_w, L0_attn_dt_w, L0_attn_dt_b, L0_attn_A_log, L0_attn_D_param, L0_attn_ssm_out_w, L0_attn_mix_weight, L0_attn_ffn_w1, L0_attn_ffn_b1, L0_attn_ffn_w2, L0_attn_ffn_b2, L0_ffn_Wr1, L0_ffn_br1, L0_ffn_Wr2, L0_ffn_br2, L0_ffn_Ws1, L0_ffn_bs1, L0_ffn_Ws2, L0_ffn_bs2, L0_ffn_We1, L0_ffn_be1, L0_ffn_We2, L0_ffn_be2, L0_c, L0_wmod, L1_attn_Wq, L1_attn_bq, L1_attn_Wk, L1_attn_bk, L1_attn_Wv, L1_attn_bv, L1_ffn_W_r, L1_ffn_W_k, L1_ffn_W_v, L1_ffn_mu_r, L1_ffn_mu_k, L1_c, L1_wmod):

    def _L0_attn_ref(x, ln1_w, ln1_b, ln2_w, ln2_b, q_w, q_b, k_w, k_b, v_w, v_b, o_w, o_b, in_proj_w, conv_w, conv_b, x_proj_w, dt_w, dt_b, A_log, D_param, ssm_out_w, mix_weight, ffn_w1, ffn_b1, ffn_w2, ffn_b2):
        import jax, jax.numpy as jnp
        import numpy as np
        D_MODEL = 128
        N_HEADS = 16
        D_FF = 512
        D_STATE = 16
        D_CONV = 4
        EXPAND = 2
        D_INNER = D_MODEL * EXPAND
        DT_RANK = D_MODEL // 16
        BATCH = 4
        SEQ = 128

        def _ln(x, w, b):
            m = jnp.mean(x, axis=-1, keepdims=True)
            v = jnp.var(x, axis=-1, keepdims=True)
            return (x - m) / jnp.sqrt(v + 1e-05) * w + b
        B, L, Dm = x.shape
        H = N_HEADS
        hd = Dm // H
        xn = _ln(x, ln1_w, ln1_b)
        q = (xn @ q_w + q_b).reshape(B, L, H, hd)
        k = (xn @ k_w + k_b).reshape(B, L, H, hd)
        v = (xn @ v_w + v_b).reshape(B, L, H, hd)
        scores = jnp.einsum('bqhd,bkhd->bhqk', q, k) * hd ** (-0.5)
        causal = jnp.tril(jnp.ones((L, L), bool))
        scores = jnp.where(causal[None, None], scores, -jnp.inf)
        attn = jax.nn.softmax(scores, axis=-1)
        attn_out = jnp.einsum('bhqk,bkhd->bqhd', attn, v).reshape(B, L, Dm) @ o_w + o_b
        xz = xn @ in_proj_w
        Di = xz.shape[-1] // 2
        x_ssm, z = (xz[..., :Di], xz[..., Di:])
        K = conv_w.shape[1]
        xp = jnp.pad(x_ssm, ((0, 0), (K - 1, 0), (0, 0)))
        x_c = sum((xp[:, j:j + L, :] * conv_w[:, j] for j in range(K))) + conv_b
        x_c = jax.nn.silu(x_c)
        x_dbc = x_c @ x_proj_w
        R = dt_w.shape[0]
        N = A_log.shape[1]
        dt = jax.nn.softplus(x_dbc[..., :R] @ dt_w + dt_b)
        Bm = x_dbc[..., R:R + N]
        Cm = x_dbc[..., R + N:]
        A = -jnp.exp(A_log)

        def step(h, inp):
            xt, dtt, Bt, Ct = inp
            h = jnp.exp(dtt[..., None] * A) * h + (xt * dtt)[..., None] * Bt[:, None, :]
            y = jnp.einsum('bn,bdn->bd', Ct, h)
            return (h, y)
        h0 = jnp.zeros((B, Di, N), x.dtype)
        _, ys = jax.lax.scan(step, h0, (x_c.swapaxes(0, 1), dt.swapaxes(0, 1), Bm.swapaxes(0, 1), Cm.swapaxes(0, 1)))
        y = ys.swapaxes(0, 1)
        y = (y + x_c * D_param) * jax.nn.silu(z)
        ssm_out = y @ ssm_out_w
        alpha = jax.nn.sigmoid(mix_weight)
        x = x + alpha * attn_out + (1.0 - alpha) * ssm_out
        h2 = _ln(x, ln2_w, ln2_b)
        ffn = jax.nn.gelu(h2 @ ffn_w1 + ffn_b1, approximate=False) @ ffn_w2 + ffn_b2
        return x + ffn

    def _L0_ffn_ref(x, Wr1, br1, Wr2, br2, Ws1, bs1, Ws2, bs2, We1, be1, We2, be2):
        import jax, jax.numpy as jnp
        import numpy as np
        B, T, C = (2, 64, 128)
        I = 512
        E = 8
        K = 2
        Bb, Tt, Cc = x.shape
        xf = x.reshape(-1, Cc)
        logits = jax.nn.relu(xf @ Wr1 + br1) @ Wr2 + br2
        gates = jax.nn.softmax(logits, axis=-1)
        tg, ti = jax.lax.top_k(gates, K)
        tg = jax.nn.softmax(tg / K, axis=-1)
        out = jax.nn.silu(xf @ Ws1 + bs1) @ Ws2 + bs2
        for e in range(E):
            h = jax.nn.silu(xf @ We1[e] + be1[e]) @ We2[e] + be2[e]
            w = jnp.sum(tg * (ti == e), axis=-1)
            out = out + w[:, None] * h
        return out.reshape(Bb, Tt, Cc)

    def _L1_attn_ref(val, Wq, bq, Wk, bk, Wv, bv):
        import jax, jax.numpy as jnp
        import numpy as np
        S, B, E = (512, 2, 128)
        H = 8
        WIN = 32

        def _band_scores(q, k_pad, seq_len, band):

            def f(o):
                ks = jax.lax.dynamic_slice_in_dim(k_pad, o, seq_len, axis=1)
                return jnp.einsum('bshd,bshd->bsh', q, ks)
            s = jax.lax.map(f, jnp.arange(band))
            return jnp.moveaxis(s, 0, -1)

        def _band_av(probs, v_pad, seq_len, band):
            bsz, _, heads, _ = probs.shape
            d = v_pad.shape[-1]

            def body(carry, o):
                vs = jax.lax.dynamic_slice_in_dim(v_pad, o, seq_len, axis=1)
                p = jax.lax.dynamic_slice_in_dim(probs, o, 1, axis=3)
                return (carry + p * vs, None)
            init = jnp.zeros((bsz, seq_len, heads, d), probs.dtype)
            out, _ = jax.lax.scan(body, init, jnp.arange(band))
            return out
        seq_len, bsz, embed = val.shape
        heads, w = (H, WIN)
        d = embed // heads
        band = 2 * w + 1
        x = jnp.swapaxes(val, 0, 1)
        scale = 1.0 / np.sqrt(d)
        q = (x @ Wq.T + bq) * scale
        k = x @ Wk.T + bk
        v = x @ Wv.T + bv
        mq = jnp.swapaxes(q.reshape(seq_len, bsz, heads, d), 0, 1)
        mk = jnp.swapaxes(k.reshape(seq_len, bsz, heads, d), 0, 1)
        mv = jnp.swapaxes(v.reshape(seq_len, bsz, heads, d), 0, 1)
        k_pad = jnp.pad(mk, ((0, 0), (w, w), (0, 0), (0, 0)))
        v_pad = jnp.pad(mv, ((0, 0), (w, w), (0, 0), (0, 0)))
        scores = _band_scores(mq, k_pad, seq_len, band)
        probs = jax.nn.softmax(scores, axis=-1)
        attn = _band_av(probs, v_pad, seq_len, band)
        out = jnp.swapaxes(attn, 0, 1).reshape(seq_len, bsz, embed)
        return out

    def _L1_ffn_ref(x, W_r, W_k, W_v, mu_r, mu_k):
        import jax, jax.numpy as jnp
        import numpy as np
        DIM = 128

        def _reference_tuple_inner(x, W_r, W_k, W_v, mu_r, mu_k):
            B, T, C = x.shape
            x_prev = jnp.concatenate([jnp.zeros((B, 1, C), x.dtype), x[:, :-1, :]], axis=1)
            xr = mu_r * x + (1.0 - mu_r) * x_prev
            xk = mu_k * x + (1.0 - mu_k) * x_prev
            r = jax.nn.sigmoid(jnp.einsum('btc,dc->btd', xr, W_r))
            k = jnp.einsum('btc,dc->btd', xk, W_k)
            k_act = jnp.square(jax.nn.relu(k))
            out = r * jnp.einsum('btc,dc->btd', k_act, W_v)
            new_state = x[:, -1, :]
            return (out, new_state)
        return _reference_tuple_inner(x, W_r, W_k, W_v, mu_r, mu_k)[0]
    x = L0_attn_x
    mod = (_silu(L0_c) @ L0_wmod).reshape(L0_c.shape[0], 6, 1, -1)
    sa, ca, ga, sb, cb, gb = (mod[:, 0], mod[:, 1], mod[:, 2], mod[:, 3], mod[:, 4], mod[:, 5])
    ga = (2 * (ga >= 0) - 1) * jnp.maximum(jnp.abs(ga), 0.25)
    gb = (2 * (gb >= 0) - 1) * jnp.maximum(jnp.abs(gb), 0.25)
    h = _layernorm(x, axis=-1) * (1 + ca) + sa
    x = x + ga * _L0_attn_ref(h, L0_attn_ln1_w, L0_attn_ln1_b, L0_attn_ln2_w, L0_attn_ln2_b, L0_attn_q_w, L0_attn_q_b, L0_attn_k_w, L0_attn_k_b, L0_attn_v_w, L0_attn_v_b, L0_attn_o_w, L0_attn_o_b, L0_attn_in_proj_w, L0_attn_conv_w, L0_attn_conv_b, L0_attn_x_proj_w, L0_attn_dt_w, L0_attn_dt_b, L0_attn_A_log, L0_attn_D_param, L0_attn_ssm_out_w, L0_attn_mix_weight, L0_attn_ffn_w1, L0_attn_ffn_b1, L0_attn_ffn_w2, L0_attn_ffn_b2)
    h = _layernorm(x, axis=-1) * (1 + cb) + sb
    x = x + gb * _L0_ffn_ref(h, L0_ffn_Wr1, L0_ffn_br1, L0_ffn_Wr2, L0_ffn_br2, L0_ffn_Ws1, L0_ffn_bs1, L0_ffn_Ws2, L0_ffn_bs2, L0_ffn_We1, L0_ffn_be1, L0_ffn_We2, L0_ffn_be2)
    mod = (_silu(L1_c) @ L1_wmod).reshape(L1_c.shape[0], 6, 1, -1)
    sa, ca, ga, sb, cb, gb = (mod[:, 0], mod[:, 1], mod[:, 2], mod[:, 3], mod[:, 4], mod[:, 5])
    ga = (2 * (ga >= 0) - 1) * jnp.maximum(jnp.abs(ga), 0.25)
    gb = (2 * (gb >= 0) - 1) * jnp.maximum(jnp.abs(gb), 0.25)
    h = _layernorm(x, axis=-1) * (1 + ca) + sa
    x = x + ga * _L1_attn_ref(h, L1_attn_Wq, L1_attn_bq, L1_attn_Wk, L1_attn_bk, L1_attn_Wv, L1_attn_bv)
    h = _layernorm(x, axis=-1) * (1 + cb) + sb
    x = x + gb * _L1_ffn_ref(h, L1_ffn_W_r, L1_ffn_W_k, L1_ffn_W_v, L1_ffn_mu_r, L1_ffn_mu_k)
    return x

_drawn_inputs = setup_inputs


def setup_inputs(seed=0):
    import zlib

    import numpy as np

    out = dict(_drawn_inputs(seed))
    spreads = {'L0_attn_ln1_w': (1.0, 0.2),
     'L0_attn_ln1_b': (0.0, 0.1),
     'L0_attn_ln2_w': (1.0, 0.2),
     'L0_attn_ln2_b': (0.0, 0.1),
     'L0_attn_q_b': (0.0, 0.1),
     'L0_attn_k_b': (0.0, 0.1),
     'L0_attn_v_b': (0.0, 0.1),
     'L0_attn_o_b': (0.0, 0.1),
     'L0_attn_conv_b': (0.0, 0.1),
     'L0_attn_D_param': (1.0, 0.2),
     'L0_attn_mix_weight': (0.5, 0.2),
     'L0_attn_ffn_b1': (0.0, 0.1),
     'L0_attn_ffn_b2': (0.0, 0.1),
     'L0_ffn_br1': (0.0, 0.1),
     'L0_ffn_br2': (0.0, 0.1),
     'L0_ffn_bs1': (0.0, 0.1),
     'L0_ffn_bs2': (0.0, 0.1),
     'L0_ffn_be1': (0.0, 0.1),
     'L0_ffn_be2': (0.0, 0.1)}
    factors = {}
    for name, (base, spread) in spreads.items():
        noise = np.random.default_rng([zlib.crc32(name.encode()), seed]).standard_normal(out[name].shape)
        drawn = base * np.exp(spread * noise) if base else spread * noise
        out[name] = jnp.asarray(drawn.astype(out[name].dtype))
    for name, factor in factors.items():
        out[name] = (out[name] * factor).astype(out[name].dtype)
    return out
```

```python
from contextlib import ExitStack

import concourse.bass as bass
from concourse import mybir

F32 = mybir.dt.float32
BF16 = mybir.dt.bfloat16
ALU = mybir.AluOpType
ACT = mybir.ActivationFunctionType
AX = mybir.AxisListType

P = 128
NB = 8
T = 512
EPS = 1e-5
QS = 8.0 ** -0.5
NEG = -1e30


class Op:

    def __init__(self, eng, fn, waits, step):
        self.eng, self.fn, self.waits, self.step = eng, fn, waits, step
        self.signals = False
        self.sem = None
        self.value = 0


class Program:

    def __init__(self):
        self.queues = {e: [] for e in ("pe", "dve", "act", "pool", "sp")}

    def op(self, eng, fn, *waits, sem=None, step=1):
        flat = []
        for w in waits:
            if isinstance(w, (list, tuple)):
                flat += [x for x in w if x is not None]
            elif w is not None:
                flat.append(w)
        for w in flat:
            w.signals = True
        o = Op(eng, fn, flat, step)
        if sem is not None:
            o.sem, o.value = sem, step
        self.queues[eng].append(o)
        return o

    def number(self, sems):
        for eng, q in self.queues.items():
            n = 0
            for o in q:
                if o.sem is None and o.signals:
                    n += 1
                    o.sem, o.value = sems[eng], n

    def emit(self, eng, handle):
        seen = {}
        for o in self.queues[eng]:
            need = {}
            for w in o.waits:
                if w.value > max(seen.get(id(w.sem), 0), need.get(id(w.sem), (0, None))[0]):
                    need[id(w.sem)] = (w.value, w.sem)
            for k, (v, s) in need.items():
                handle.wait_ge(s, v)
                seen[k] = v
            ins = o.fn(handle)
            if o.value:
                ins.then_inc(o.sem, o.step)


def run_together(*gens):
    live = list(gens)
    while live:
        for g in list(live):
            try:
                next(g)
            except StopIteration:
                live.remove(g)


def build(nc, d, out):
    pr = Program()
    with ExitStack() as ctx:
        def sb(name, shape, dt=F32):
            return ctx.enter_context(nc.sbuf_tensor(name, shape, dt))

        bank = [ctx.enter_context(nc.psum_tensor(f"bank{i}", [P, 512], F32)) for i in range(8)]

        def pe(fn, *w):
            return pr.op("pe", fn, *w)

        def dve(fn, *w):
            return pr.op("dve", fn, *w)

        def act(fn, *w):
            return pr.op("act", fn, *w)

        def pool(fn, *w):
            return pr.op("pool", fn, *w)

        ndma = [0]

        def dma(dst, src, *w, eng="sp"):
            s = ctx.enter_context(nc.semaphore(f"s_dma{ndma[0]}"))
            ndma[0] += 1
            return pr.op(eng, lambda e: e.dma_start(dst, src), *w, sem=s, step=16)

        def mm(o, l, r, *w, start=True, stop=True, pos=None):
            return pe(lambda e: e.matmul(o, l, r, start=start, stop=stop, tile_position=pos, skip_group_check=True), *w)

        def tr(o, i, idn, *w):
            return pe(lambda e: e.transpose(o, i, idn), *w)

        def actv(o, i, f, *w, scale=1.0, bias=0.0):
            return act(lambda e: e.activation(o, i, f, scale=scale, bias=bias), *w)

        def tt(eng, o, a, b, op, *w):
            return pr.op(eng, lambda e: e.tensor_tensor(o, a, b, op), *w)

        def ts(eng, o, a, s1, s2, op0, op1, *w):
            if s2 is None:
                return pr.op(eng, lambda e: e.tensor_scalar(o, a, s1, None, op0), *w)
            return pr.op(eng, lambda e: e.tensor_scalar(o, a, s1, s2, op0, op1), *w)

        def stt(o, a, s, b, op0, op1, *w):
            return dve(lambda e: e.scalar_tensor_tensor(out=o, in0=a, scalar=s, in1=b, op0=op0, op1=op1), *w)

        free = {}

        xT = sb("xT", [P, NB, T])
        hT = sb("hT", [P, NB, T])
        nT = sb("nT", [P, NB, T])
        big = sb("big", [P, 2, NB, 2, T])
        xc = big[:, 0]
        zg = big[:, 1]

        ident = sb("ident", [P, P])
        cmat = sb("cmat", [P, P])
        omat = sb("omat", [P, P])
        ones = sb("ones", [1, P])
        mask = sb("mask", [P, 512], BF16)
        seld = sb("seld", [P, P])
        epsc = sb("epsc", [P, 1])

        stg = nT[:, 3, :]
        vrow = stg[:, 384:512]
        vcol = sb("vcol", [P, P])
        wq = sb("wq", [P, 4, 4, 32])
        wk = sb("wk", [P, 4, 4, 32])
        wqs = stg[:, 0:256].rearrange("p (a c) -> p a c", a=2)
        wv = sb("wv", [P, P])
        wo = sb("wo", [P, 4, P])
        qb = sb("qb", [P, 4])
        kb = vcol[:, 64:68]
        On = sb("On", [P, 4, T])
        win = On[:, 0, :]
        cw = sb("cw", [P, 2, 4])
        wxp = sb("wxp", [P, 2, 40])
        wdt = sb("wdt", [8, 256])
        alog = sb("alog", [P, 2, 16])
        wso = sb("wso", [P, 2, P])
        wr1 = sb("wr1", [P, 32])
        br1 = sb("br1", [32, 1])
        wr2 = sb("wr2", [33, 8])
        bsum = sb("bsum", [33, P])
        crow = sb("crow", [16, P])
        cT = sb("cT", [P, 16])
        mod = sb("mod", [P, 2, 6, NB])
        gab = sb("gab", [P, 4, NB])
        gtmp = sb("gtmp", [P, 3, 4, NB])
        avec = sb("avec", [P, 4])
        woT = stg[:, 256:384]

        xin = xc.rearrange("p a b c -> p (a b c)")[:, 0:4096].rearrange("p (n c) -> p n c", c=P)
        xd = d["L0_attn_x"].rearrange("b (n p) c -> b p n c", p=P)
        l_x = [dma(xin[:, 4 * b:4 * b + 4, :], xd[b]) for b in range(NB)]
        ROWS = [("ln1_w", "L0_attn_ln1_w", 1), ("ln1_b", "L0_attn_ln1_b", 1), ("ln2_w", "L0_attn_ln2_w", 1),
                ("ln2_b", "L0_attn_ln2_b", 1), ("o_b", "L0_attn_o_b", 1), ("v_b", "L0_attn_v_b", 1),
                ("conv_b", "L0_attn_conv_b", 2), ("dt_b", "L0_attn_dt_b", 2), ("D", "L0_attn_D_param", 2),
                ("mix", "L0_attn_mix_weight", 1), ("ffn_b1", "L0_attn_ffn_b1", 4), ("ffn_b2", "L0_attn_ffn_b2", 1),
                ("bs1", "L0_ffn_bs1", 4), ("be1", "L0_ffn_be1", 32), ("mu_r", "L1_ffn_mu_r", 1),
                ("mu_k", "L1_ffn_mu_k", 1)]
        v0 = pool(lambda e: e.memset(vrow, 0.0))
        v1 = dve(lambda e: e.memset(vrow[64:68, :].rearrange("g (i j) -> g i j", i=4)[:, :, 8:9], 1.0), v0)
        l_rows = [v1]
        at = {"k_b": 64, "q_b": 68}
        for k in ("q_b", "k_b"):
            l_rows.append(dma(vrow[at[k]:at[k] + 4, :].rearrange("g (i j) -> g i j", i=4)[:, :, 0:8],
                              d["L0_attn_" + k].rearrange("(g i j) -> g i j", g=4, i=4), v1, eng="act"))
        n = 0
        for k, name, m in ROWS:
            src = d[name]
            src = src.rearrange("e (m c) -> (e m) c", c=P) if len(src.shape) == 2 else src.rearrange("(m c) -> m c", c=P)
            at[k] = n
            l_rows.append(dma(vrow[n:n + m, :], src, v0, eng="act"))
            n += m
        assert n <= 64
        NR = 72

        def col(k, j=0):
            return vcol[:, at[k] + j:at[k] + j + 1]

        l_c = [dma(crow[0:8, :], d["L0_c"]), dma(crow[8:16, :], d["L1_c"])]
        wm = nT[:, 0:3, :].rearrange("p a b -> p (a b)").rearrange("p (l k c) -> p l k c", l=2, k=6)
        l_wm = [dma(wm[:, 0], d["L0_wmod"].rearrange("p (k c) -> p k c", k=6)),
                dma(wm[:, 1], d["L1_wmod"].rearrange("p (k c) -> p k c", k=6))]
        l_qk = [dma(wqs[:, 0, :], d["L0_attn_q_w"]), dma(wqs[:, 1, :], d["L0_attn_k_w"])]
        l_wv = dma(wv[:], d["L0_attn_v_w"])
        l_in = dma(win, d["L0_attn_in_proj_w"])
        l_cw = dma(cw[:], d["L0_attn_conv_w"].rearrange("(h p) k -> p h k", p=P))
        l_xp = dma(wxp[:], d["L0_attn_x_proj_w"].rearrange("(h p) k -> p h k", p=P))
        l_dt = dma(wdt[:], d["L0_attn_dt_w"])
        l_al = dma(alog[:], d["L0_attn_A_log"].rearrange("(h p) k -> p h k", p=P))
        l_so = dma(wso[:], d["L0_attn_ssm_out_w"].rearrange("(h p) k -> p h k", p=P))
        l_woT = dma(woT, d["L0_attn_o_w"])

        z0 = [pool(lambda e: e.memset(wo[:], 0.0)), pool(lambda e: e.memset(wq[:], 0.0)),
              pool(lambda e: e.memset(wk[:], 0.0))]
        c_id0 = pool(lambda e: e.memset(ident[:], 0.0))
        c_id = pool(lambda e: e.affine_select(out=ident[:], in_=ident[:], compare_op=ALU.not_equal, fill=1.0, base=0,
                                              pattern=[[-1, P]], channel_multiplier=1), c_id0)
        c_om = pool(lambda e: e.memset(omat[:], 1.0 / P))
        c_cm = tt("pool", cmat[:], ident[:], omat[:], ALU.subtract, c_id, c_om)
        c_on = pool(lambda e: e.memset(ones[:], 1.0))
        c_ep = pool(lambda e: e.memset(epsc[:], EPS))
        m0 = pool(lambda e: e.memset(mask[:], 0.0))
        c_mk = pool(lambda e: e.affine_select(out=mask[:, 384:512], in_=mask[:, 384:512], compare_op=ALU.is_ge, fill=NEG,
                                              base=0, pattern=[[-1, P]], channel_multiplier=1), m0)
        sd = pool(lambda e: e.memset(seld[:], 0.0))
        sd = pool(lambda e: e.affine_select(out=seld[:].rearrange("p (i j) -> p i j", i=4),
                                            in_=seld[:].rearrange("p (i j) -> p i j", i=4), compare_op=ALU.not_equal,
                                            fill=1.0, base=-8, pattern=[[-32, 4], [0, 32]], channel_multiplier=1), sd)
        c_sel = sd
        l_wo = []
        for i in range(4):
            l_wo.append(dma(wo[32 * i:32 * i + 8, :, :],
                            d["L0_attn_o_w"].rearrange("(g i d) n -> i d g n", i=4, d=8)[i], z0))
        c_wq = [pool(lambda e, k=k, w=w: e.tensor_copy(w[:].rearrange("p g i j -> p (g i) j")[:, :, 0:8],
                                                       wqs[:, k, :].rearrange("p (h d) -> p h d", d=8)), l_qk, z0)
                for k, w in enumerate((wq, wk))]
        zb = pool(lambda e: e.memset(bsum[:], 0.0))
        l_rest = {
            "wr1": dma(wr1[:], d["L0_ffn_Wr1"]),
            "br1": dma(br1[:], d["L0_ffn_br1"].rearrange("(p o) -> p o", o=1)),
            "wr2": dma(wr2[0:32, :], d["L0_ffn_Wr2"]),
            "br2": dma(wr2[32:33, :], d["L0_ffn_br2"].rearrange("(o p) -> o p", o=1)),
            "be2": dma(bsum[0:8, :], d["L0_ffn_be2"], zb),
            "bs2": dma(bsum[32:33, :], d["L0_ffn_bs2"].rearrange("(o p) -> o p", o=1), zb),
        }

        t = tr(bank[0][:, 0:NR], vrow[0:NR, :], ident[0:NR, 0:NR], l_rows, c_id)
        c_v = actv(vcol[:, 0:NR], bank[0][:, 0:NR], ACT.Copy, t)
        c_early = [t]
        t = tr(bank[1][:, 0:16], crow[:], ident[0:16, 0:16], l_c, c_id)
        c_cT = actv(cT[:], bank[1][:, 0:16], ACT.Silu, t)
        last = None
        for l in range(2):
            for k in range(6):
                last = mm(bank[2][:, 48 * l + 8 * k:48 * l + 8 * k + 8], wm[:, l, k, :], cT[:, 8 * l:8 * l + 8], c_cT, l_wm)
        md = actv(mod[:].rearrange("p l k b -> p (l k b)"), bank[2][:, 0:96], ACT.Copy, last)
        free["wm"] = [last, md] + c_wq + c_early
        sc = [ts("dve", mod[:, :, k, :], mod[:, :, k, :], 1.0, None, ALU.add, None, md) for k in (1, 4)]
        g = mod[:].rearrange("p l (u k) b -> p l u k b", u=2)[:, :, :, 2, :]
        gt = gtmp[:].rearrange("p a (l u) b -> p a l u b", l=2)
        gv = gab[:].rearrange("p (l u) b -> p l u b", l=2)
        neg = ts("dve", gtmp[:, 0].rearrange("p (l u) b -> p l u b", l=2), g, -1.0, None, ALU.mult, None, md)
        ab = tt("dve", gt[:, 1], gt[:, 0], g, ALU.max, neg)
        sg = ts("dve", gt[:, 2], g, 0.0, 2.0, ALU.is_ge, ALU.mult, md)
        ab = ts("dve", gt[:, 0], gt[:, 1], 0.25, None, ALU.max, None, ab)
        sg = ts("dve", gt[:, 1], gt[:, 2], -1.0, None, ALU.add, None, sg, ab)
        c_g = tt("dve", gv, gt[:, 1], gt[:, 0], ALU.mult, sg, ab)
        c_mod = [c_g] + sc

        def gate(j, b):
            return gab[:, j, b:b + 1]

        sgm = actv(avec[:, 0:1], col("mix"), ACT.Sigmoid, c_v)
        om1 = ts("dve", avec[:, 1:2], avec[:, 0:1], -1.0, 1.0, ALU.mult, ALU.add, sgm)
        t = t_wo = mm(bank[3][:, 0:2], woT, vcol[:, at["v_b"]:at["v_b"] + 2], l_woT, c_v)
        t = ts("dve", avec[:, 2:3], bank[3][:, 0:1], col("o_b"), None, ALU.add, None, t)
        c_av = [om1, tt("dve", avec[:, 3:4], avec[:, 2:3], avec[:, 0:1], ALU.mult, t, sgm)]
        ea = actv(alog[:], alog[:], ACT.Exp, l_al)
        c_A = ts("dve", alog[:], alog[:], -1.0, None, ALU.mult, None, ea)
        c_qb = ts("dve", qb[:], vcol[:, 68:72], QS, None, ALU.mult, None, c_v)

        r_x = [None] * NB
        for b in range(NB):
            bk = bank[4 + b % 4]
            for j in range(4):
                t = tr(bk[:, P * j:P * j + P], xin[:, 4 * b + j, :], ident[:], l_x[b], c_id, free.get(f"b{4 + b % 4}"))
            if b % 2:
                r_x[b] = actv(xT[:, b, :], bk[:], ACT.Copy, t)
            else:
                r_x[b] = dve(lambda e, b=b, bk=bk: e.tensor_copy(xT[:, b, :], bk[:]), t)
            free[f"b{4 + b % 4}"] = [r_x[b]]
        free["xin"] = r_x

        lsq = sb("lsq", [P, 2, T])
        lrs = sb("lrs", [P, 2, T])
        for i in range(8):
            free.setdefault(f"b{i}", [c_v, c_cT, md, c_av[1]] + r_x)
        ln_n = [0]

        def layer_norm(dst, src, scale, shift, b0, *w, dst_free=None, fold=None):
            i = ln_n[0] % 2
            ln_n[0] += 1
            c = mm(bank[b0][:], cmat[:], src, c_cm, free[f"b{b0}"], *w)
            s = actv(lsq[:, i, :], bank[b0][:], ACT.Square, c, free.get(f"lsq{i}"))
            v = mm(bank[b0 + 1][:], omat[:], lsq[:, i, :], s, c_om, free[f"b{b0 + 1}"])
            free[f"lsq{i}"] = [v]
            g1 = actv(lrs[:, i, :], bank[b0 + 1][:], ACT.Ln, v, c_ep, free.get(f"lrs{i}"), bias=epsc[:])
            free[f"b{b0 + 1}"] = [g1]
            g2 = actv(lrs[:, i, :], lrs[:, i, :], ACT.Exp, g1, scale=-0.5)
            xcen, rstd = bank[b0][:], lrs[:, i, :]
            if fold:
                xcen, rstd = [a.rearrange("p (s j) -> p s j", s=fold) for a in (xcen, rstd)]
            o = stt(dst, xcen, scale, rstd, ALU.mult, ALU.mult, g2, dst_free)
            free[f"b{b0}"] = [o]
            free[f"lrs{i}"] = [o]
            return ts("pool", dst, dst, shift, None, ALU.add, None, o)

        r_h = [None] * NB
        r_n = [None] * NB
        for b in range(NB):
            r_h[b] = layer_norm(hT[:, b, :], xT[:, b, :], mod[:, 0, 1, b:b + 1], mod[:, 0, 0, b:b + 1], 2 * (b % 4),
                                r_x[b], c_mod, md)
        for b in range(NB):
            r_n[b] = layer_norm(nT[:, b, :], hT[:, b, :], col("ln1_w"), col("ln1_b"), 2 * (b % 4),
                                r_h[b], dst_free=free["wm"] + [t_wo])

        r_xc = [[None, None] for _ in range(NB)]
        r_z = [[None, None] for _ in range(NB)]
        u = 0
        for b in range(NB):
            for h in range(2):
                k = u % 8
                u += 1
                m = mm(bank[k][:], win[:, P * h:P * h + P], nT[:, b, :], l_in, r_n[b], free[f"b{k}"])
                o = xc[:, b, h, :]
                c = ts("dve", o, bank[k][:], cw[:, h, 3:4], col("conv_b", h), ALU.mult, ALU.add, m, l_cw, c_v, free["xin"])
                for j in range(1, 4):
                    c = stt(o[:, j:T], bank[k][:, 0:T - j], cw[:, h, 3 - j:4 - j], o[:, j:T], ALU.mult, ALU.add, c)
                free[f"b{k}"] = [c]
                r_xc[b][h] = actv(o, o, ACT.Silu, c)
                k = u % 8
                u += 1
                m = mm(bank[k][:], win[:, 256 + P * h:256 + P * h + P], nT[:, b, :], free[f"b{k}"])
                r_z[b][h] = actv(zg[:, b, h, :], bank[k][:], ACT.Silu, m)
                free[f"b{k}"] = [r_z[b][h]]
        free["On"] = [m]

        scr = ExitStack()

        def tmp(name, shape, dt=F32):
            return scr.enter_context(nc.sbuf_tensor(name, shape, dt))

        QT = tmp("QT", [P, 2, T])
        KT = tmp("KT", [P, 2, T])
        QTb = tmp("QTb", [P, 2, T], BF16)
        KTb = tmp("KTb", [P, 2, T], BF16)
        Vb = tmp("Vb", [P, 1, 4, 16, 32])
        Mx = tmp("Mx", [P, 2, 4, P])
        PT = tmp("PT", [P, 3, T])
        Os = tmp("Os", [P, T])
        rdn = lrs

        zi = [pool(lambda e: e.memset(Vb[:], 0.0)), pool(lambda e: e.memset(Mx[:], 0.0))]
        zi.append(pool(lambda e: e.memset(Vb[:].rearrange("p a t h j -> p (a t h) j")[:, :, 8:9], 1.0), zi[0]))

        ring = [0]

        def take():
            k = ring[0] % 3
            ring[0] += 1
            return k

        r_at = [None] * NB

        def attention(b):
            xn = nT[:, b, :]
            k = take()
            for j in range(4):
                m = mm(bank[k][:, P * j:P * j + P], xn[:, P * j:P * j + P], wv[:], r_n[b], l_wv, free[f"b{k}"])
            vv = Vb[:, 0].rearrange("p t h j -> p (t h) j")[:, :, 0:8]
            r_v = actv(vv, bank[k][:].rearrange("p (h j) -> p h j", j=8), ACT.Copy, m, zi, free.get("V"))
            free[f"b{k}"] = [r_v]
            yield
            for g in range(4):
                s = g % 2
                k = take()
                m = mm(bank[k][:], wq[:, g].rearrange("p i j -> p (i j)"), xn, c_wq, free[f"b{k}"], r_n[b])
                q1 = actv(QT[:, s, :], bank[k][:], ACT.Identity, m, c_qb, free.get(f"QT{s}"), scale=QS, bias=qb[:, g:g + 1])
                free[f"b{k}"] = [q1]
                q2 = dve(lambda e, s=s: e.tensor_copy(QTb[:, s, :], QT[:, s, :]), q1, free.get(f"QTb{s}"))
                k = take()
                m = mm(bank[k][:], wk[:, g].rearrange("p i j -> p (i j)"), xn, free[f"b{k}"])
                k1 = actv(KT[:, s, :], bank[k][:], ACT.Identity, m, c_v, free.get(f"QT{s}"), bias=kb[:, g:g + 1])
                free[f"b{k}"] = [k1]
                k2 = dve(lambda e, s=s: e.tensor_copy(KTb[:, s, :], KT[:, s, :]), k1, free.get(f"QTb{s}"))
                yield
                mxs = []
                for i in range(4):
                    for qi in range(4):
                        kc = P * (qi + 1)
                        k = take()
                        m = mm(bank[k][:, 0:kc], QTb[32 * i:32 * i + 8, s, P * qi:P * qi + P],
                               KTb[32 * i:32 * i + 8, s, 0:kc], q2, k2, free[f"b{k}"])
                        x = dve(lambda e, kc=kc, k=k, s=s, qi=qi, i=i: e.tensor_tensor_reduce(
                            bank[k][:, 0:kc], bank[k][:, 0:kc], mask[:, 512 - kc:512], 1.0, NEG, ALU.add, ALU.max,
                            Mx[:, s, qi, 32 * i + 8:32 * i + 9]), m, c_mk, zi, free.get(f"Mx{s}"))
                        free[f"b{k}"] = [x]
                        mxs.append(x)
                    yield
                free[f"QTb{s}"] = [m]
                k = take()
                for qi in range(4):
                    m = tr(bank[k][:, P * qi:P * qi + P], Mx[:, s, qi, :], ident[:], mxs, free[f"b{k}"])
                free[f"Mx{s}"] = [m]
                q3 = tt("dve", QT[:, s, :], QT[:, s, :], bank[k][:], ALU.subtract, m, q2)
                free[f"b{k}"] = [q3]
                yield
                pv = [None]

                def weigh(h4, parts, sl, ready):
                    for i, kj, off in parts:
                        n = T - P * kj
                        pv[0] = mm(bank[3][32 * i:32 * i + 32, P * kj:T], Vb[:, 0, kj, 4 * h4 + i, :],
                                   PT[:, sl, off:off + n], ready, r_v, free["b3"] if kj == 0 else None,
                                   start=(kj == 0), stop=(kj == 3), pos=(0, 32 * i))
                    free[f"PT{sl}"] = [pv[0]]

                late = []
                un = 0
                for pair in range(2):
                    a, c = 2 * pair, 2 * pair + 1
                    for parts in ([(a, 0, 0)], [(c, 0, 0)], [(a, 1, 0), (a, 3, 384)], [(c, 1, 0), (c, 3, 384)],
                                  [(a, 2, 0)], [(c, 2, 0)]):
                        k = take()
                        sl = un % 3
                        un += 1
                        for i, kj, off in parts:
                            n = T - P * kj
                            m = mm(bank[k][:, off:off + n], KT[32 * i:32 * i + 9, s, P * kj:P * kj + P],
                                   QT[32 * i:32 * i + 9, s, P * kj:T], q3, k1, free[f"b{k}"])
                        w = off + n
                        x = actv(PT[:, sl, 0:w], bank[k][:, 0:w], ACT.Exp, m, free.get(f"PT{sl}"))
                        free[f"b{k}"] = [x]
                        nd = len(parts)
                        if nd == 1:
                            v3 = PT[:, sl, 0:P].rearrange("p (a n) -> p a n", a=1)
                        else:
                            o2 = parts[1][2]
                            v3 = PT[:, sl, 0:512].rearrange("p (a n) -> p a n", n=P)[:, 0:o2 // P + 1:o2 // P, :]
                        y = pool(lambda e, v3=v3, nd=nd: e.affine_select(
                            out=v3, in_=v3, compare_op=ALU.is_ge, fill=0.0, base=0, pattern=[[0, nd], [1, P]],
                            channel_multiplier=-1), x)
                        late.append((g, parts, sl, [x, y]))
                        if len(late) > 1:
                            weigh(*late.pop(0))
                        yield
                free[f"QT{s}"] = [m]
                for w in late:
                    weigh(*w)
                o1 = actv(Os[:], bank[3][:], ACT.Copy, pv[0], free.get("Os"))
                free["b3"] = [o1]
                yield
                k = take()
                m = mm(bank[k][:], seld[:], Os[:], o1, c_sel, free[f"b{k}"])
                e1 = actv(rdn[:, s, :], bank[k][:], ACT.Ln, m, free.get(f"lrs{s}"))
                free[f"b{k}"] = [e1]
                e2 = actv(rdn[:, s, :], rdn[:, s, :], ACT.Exp, e1, scale=-1.0)
                o2 = tt("pool", On[:, g, :], Os[:], rdn[:, s, :], ALU.mult, e2, free.get("On"))
                free["Os"] = [o2]
                free[f"lrs{s}"] = [o2]
                yield
            free["V"] = [pv[0]]
            k = take()
            for g in range(4):
                m = mm(bank[k][:], wo[:, g, :], On[:, g, :], l_wo, z0, o2, free[f"b{k}"], start=(g == 0), stop=(g == 3))
            free["On"] = [m]
            a = ts("pool", hT[:, b, :], hT[:, b, :], avec[:, 3:4], None, ALU.add, None, r_n[b], c_av)
            r_at[b] = stt(hT[:, b, :], bank[k][:], avec[:, 0:1], hT[:, b, :], ALU.mult, ALU.add, m, a)
            free[f"b{k}"] = [r_at[b]]

        bc = tmp("bc", [P, 4, 32])
        sp1 = lsq
        dtv = tmp("dtv", [P, 2, T])
        dtxT = tmp("dtxT", [P, 4, 256])
        dBx = tmp("dBx", [P, 2, 4, 256])
        dA = tmp("dA", [P, 2, T])
        hst = tmp("hst", [P, 4, T])
        yT = tmp("yT", [P, 4, 256])
        sp2 = yT[:].rearrange("p a b -> p (a b)").rearrange("p (h t) -> p h t", h=2)
        dtr = sp2[0:8, 1, :]
        r_sm = [None] * NB

        def state_space(b):
            xcb, zb = xc[:, b], zg[:, b]
            for h in range(2):
                m = mm(bank[4][0:8, :], wxp[:, h, 0:8], xcb[:, h, :], l_xp, r_xc[b][h], free["b4"], start=(h == 0), stop=(h == 1))
            for j in range(4):
                for h in range(2):
                    m2 = mm(bank[5][:, 32 * j:32 * j + 32], xcb[:, h, P * j:P * j + P], wxp[:, h, 8:40], free["b5"],
                            start=(h == 0), stop=(h == 1))
            e1 = actv(dtr, bank[4][0:8, :], ACT.Copy, m, free.get("yT"), free.get("sp"))
            e2 = dve(lambda e: e.tensor_copy(bc[:].rearrange("p a b -> p (a b)"), bank[5][:, 0:P]), m2, free.get("bc"))
            free["b4"] = [e1]
            free["b5"] = [e2]
            yield
            r_dt = []
            for h in range(2):
                k = 4 + h
                m = mm(bank[k][:], wdt[:, P * h:P * h + P], dtr, e1, l_dt, free[f"b{k}"])
                a1 = actv(sp1[:, h, :], bank[k][:], ACT.Abs, m, c_v, free.get("sp"), free.get(f"lsq{h}"), bias=col("dt_b", h))
                a2 = actv(sp1[:, h, :], sp1[:, h, :], ACT.Exp, a1, scale=-1.0)
                a3 = actv(sp1[:, h, :], sp1[:, h, :], ACT.Ln, a2, bias=1.0)
                v1 = ts("dve", sp2[:, h, :], bank[k][:], col("dt_b", h), 0.0, ALU.add, ALU.max, a1, free.get("sp"), free.get("yT"))
                free[f"b{k}"] = [a1, v1]
                v2 = tt("pool", dtv[:, h, :], sp1[:, h, :], sp2[:, h, :], ALU.add, a3, v1, free.get("dtv"))
                v3 = tt("pool", sp2[:, h, :], dtv[:, h, :], xcb[:, h, :], ALU.mult, v2)
                r_dt.append(v2)
                yield
                for j in range(4):
                    m = tr(bank[k][:, P * j:P * j + P], sp2[:, h, P * j:P * j + P], ident[:], v3, free[f"b{k}"])
                x = dve(lambda e, h=h, k=k: e.tensor_copy(dtxT[:, :, P * h:P * h + P],
                                                          bank[k][:].rearrange("p (j c) -> p j c", j=4)), m, free.get("dtxT"))
                free[f"b{k}"] = [x]
                yield
            free["sp"] = [m, v2]
            r_dx = x
            y_last = [None] * 4

            def accumulate(n, hs):
                for half in range(2):
                    k = 6 + half
                    for jj in range(2):
                        for h in range(2):
                            j = 2 * half + jj
                            m = tr(bank[k][:, 256 * jj + P * h:256 * jj + P * h + P], hst[:, hs[h][0], P * j:P * j + P],
                                   ident[:], hs[h][1], free[f"b{k}"])
                    for jj in range(2):
                        j = 2 * half + jj
                        src = bank[k][:, 256 * jj:256 * jj + 256]
                        if n == 0:
                            y = ts("dve", yT[:, j, :], src, bc[:, j, 16:17], None, ALU.mult, None, m, free.get("sp"))
                        else:
                            y = stt(yT[:, j, :], src, bc[:, j, 16 + n:17 + n], yT[:, j, :], ALU.mult, ALU.add, m, y_last[j])
                        y_last[j] = y
                    free[f"b{k}"] = [y]
                for h in range(2):
                    free[f"hst{hs[h][0]}"] = [m]

            pend = None
            for n in range(16):
                sl = n % 2
                dx = tt("pool", dBx[:, sl], dtxT[:], bc[:, :, n:n + 1].broadcast_to([P, 4, 256]), ALU.mult,
                        r_dx, e2, free.get(f"dBx{sl}"))
                yield
                hs = []
                for h in range(2):
                    a = 2 * sl + h
                    k = 4 + h
                    x = actv(dA[:, h, :], dtv[:, h, :], ACT.Exp, r_dt[h], c_A, free.get(f"dA{h}"), scale=alog[:, h, n:n + 1])
                    for j in range(4):
                        m = tr(bank[k][:, P * j:P * j + P], dBx[:, sl, j, P * h:P * h + P], ident[:], dx, free[f"b{k}"])
                    sc = dve(lambda e, a=a, k=k, h=h: e.tensor_tensor_scan(hst[:, a, :], dA[:, h, :], bank[k][:], 0.0,
                                                                     ALU.mult, ALU.add), m, x, free.get(f"hst{a}"))
                    free[f"b{k}"] = [sc]
                    free[f"dA{h}"] = [sc]
                    hs.append((a, sc))
                free[f"dBx{sl}"] = [m]
                if pend:
                    accumulate(*pend)
                pend = (n, hs)
                yield
            accumulate(*pend)
            yield
            free["dtxT"] = [dx]
            free["dtv"] = [x]
            free["bc"] = y_last + [dx]
            ys = []
            for h in range(2):
                k = 6 + h
                for j in range(4):
                    m = tr(bank[k][:, P * j:P * j + P], yT[:, j, P * h:P * h + P], ident[:], y_last, free[f"b{k}"])
                y = stt(xcb[:, h, :], xcb[:, h, :], col("D", h), bank[k][:], ALU.mult, ALU.add, m, v3)
                free[f"b{k}"] = [y]
                ys.append(tt("pool", zb[:, h, :], zb[:, h, :], xcb[:, h, :], ALU.mult, y, r_z[b][h]))
                yield
            free["yT"] = [m]
            for h in range(2):
                m = mm(bank[4][:], wso[:, h, :], zb[:, h, :], ys[h], l_so, free["b4"], start=(h == 0), stop=(h == 1))
            while r_at[b] is None:
                yield
            r_sm[b] = stt(hT[:, b, :], bank[4][:], avec[:, 1:2], hT[:, b, :], ALU.mult, ALU.add, m, r_at[b])
            free["b4"] = [r_sm[b]]

        def all_of(f):
            for b in range(NB):
                yield from f(b)

        run_together(all_of(attention), all_of(state_space))
        scr.close()

        done4 = r_sm + [pr.queues[e][-1] for e in ("pe", "dve", "act", "pool")]
        scr = ExitStack()
        we1 = big[:, 0].rearrange("p b h t -> p (b h t)")[:, 0:4096].rearrange("p (e i) -> p e i", e=8)
        we2 = big[:, 0].rearrange("p b h t -> p (b h t)")[:, 4096:8192].rearrange("p (e k n) -> p e k n", e=8, k=4)
        l_e1 = dma(we1, d["L0_ffn_We1"].rearrange("e c i -> c e i"), done4)
        l_e2 = dma(we2, d["L0_ffn_We2"].rearrange("e (k p) n -> p e k n", p=P), done4)
        hid = tmp("hid", [P, 2, 4, T])
        w1 = tmp("w1", [P, 512])
        w2 = tmp("w2", [P, 4, P])
        ws1 = tmp("ws1", [P, 512])
        ws2 = tmp("ws2", [P, 4, P])
        l_rest["w1"] = dma(w1[:], d["L0_attn_ffn_w1"], done4)
        l_rest["w2"] = dma(w2[:], d["L0_attn_ffn_w2"].rearrange("(k p) n -> p k n", p=P), done4)
        l_rest["ws1"] = dma(ws1[:], d["L0_ffn_Ws1"], done4)
        l_rest["ws2"] = dma(ws2[:], d["L0_ffn_Ws2"].rearrange("(k p) n -> p k n", p=P), done4)
        for i in range(8):
            free[f"b{i}"] = free[f"b{i}"] + done4
        r_h2 = [layer_norm(nT[:, b, :], hT[:, b, :], col("ln2_w"), col("ln2_b"), 2 * (b % 4), r_sm[b], done4)
                for b in range(NB)]
        r_x2 = [None] * NB
        pend = []

        def ffn_down(b, gl):
            k = 6 + b % 2
            for c in range(4):
                m = mm(bank[k][:], w2[:, c, :], hid[:, b % 2, c, :], gl[c], l_rest["w2"], free[f"b{k}"], start=(c == 0), stop=(c == 3))
            free[f"hid{b % 2}"] = [m]
            a = stt(hT[:, b, :], bank[k][:], col("ffn_b2"), hT[:, b, :], ALU.add, ALU.add, m, r_h2[b])
            free[f"b{k}"] = [a]
            r_x2[b] = stt(xT[:, b, :], hT[:, b, :], gate(0, b), xT[:, b, :], ALU.mult, ALU.add, a, c_g)

        u = 0
        for b in range(NB):
            gl = []
            for c in range(4):
                k = u % 6
                u += 1
                m = mm(bank[k][:], w1[:, P * c:P * c + P], nT[:, b, :], r_h2[b], l_rest["w1"], free[f"b{k}"])
                x = actv(hid[:, b % 2, c, :], bank[k][:], ACT.Gelu, m, free.get(f"hid{b % 2}"), done4, bias=col("ffn_b1", c))
                free[f"b{k}"] = [x]
                gl.append(x)
            free[f"nT{b}"] = [m]
            pend.append((b, gl))
            if len(pend) > 1:
                ffn_down(*pend.pop(0))
        ffn_down(*pend.pop(0))

        r_h3 = [layer_norm(nT[:, b, :], xT[:, b, :], mod[:, 0, 4, b:b + 1], mod[:, 0, 3, b:b + 1], 2 * (b % 3), r_x2[b],
                           dst_free=free[f"nT{b}"]) for b in range(NB)]
        hr = tmp("hr", [33, 2, T])
        lg = tmp("lg", [P, 32, 8])
        pb_ = tmp("pb_", [P, 32, 8])
        oh = tmp("oh", [P, 32, 8])
        pk = tmp("pk", [P, 32, 8])
        wgt = tmp("wgt", [P, 32, 8])
        iot = tmp("iot", [P, 8])
        st = tmp("st", [P, 8, 32])
        iot_i = tmp("iot_i", [P, 8], mybir.dt.int32)
        h1 = dve(lambda e: e.memset(hr[32:33, :, :], 1.0), done4)
        io = pool(lambda e: e.iota(iot_i[:], pattern=[[-1, 8]], base=8, channel_multiplier=0), done4)
        io = pool(lambda e: e.tensor_copy(iot[:], iot_i[:]), io)
        for b in range(NB):
            k = b % 4
            m = mm(bank[k][0:32, :], wr1[:], nT[:, b, :], r_h3[b], l_rest["wr1"], free[f"b{k}"])
            x = ts("dve", hr[0:32, b % 2, :], bank[k][0:32, :], br1[:, 0:1], 0.0, ALU.add, ALU.max, m, l_rest["br1"],
                   free.get(f"hr{b % 2}"), done4)
            free[f"b{k}"] = [x]
            for j in range(4):
                m = mm(bank[5][:, 32 * b + 8 * j:32 * b + 8 * j + 8], hr[:, b % 2, P * j:P * j + P], wr2[:],
                       x, h1, l_rest["wr2"], l_rest["br2"], free["b5"])
            free[f"hr{b % 2}"] = [m]
        lgf = lg[:].rearrange("p t e -> p (t e)")
        x = dve(lambda e: e.tensor_copy(lgf, bank[5][:, 0:256]), m, done4)
        free["b5"] = [x]

        def bcast(a):
            return a.rearrange("p (t o) -> p t o", o=1).broadcast_to([P, 32, 8])

        def red(dst, src, op, *w):
            return dve(lambda e: e.tensor_reduce(dst, src, AX.X, op), *w)

        x = red(st[:, 0, :], lg[:], ALU.max, x)
        x = tt("dve", lg[:], lg[:], bcast(st[:, 0, :]), ALU.subtract, x)
        x = actv(pb_[:], lg[:], ACT.Exp, x)
        x = red(st[:, 1, :], pb_[:], ALU.add, x)
        x = dve(lambda e: e.reciprocal(st[:, 2, :], st[:, 1, :]), x)
        x = tt("dve", pb_[:], pb_[:], bcast(st[:, 2, :]), ALU.mult, x)
        iob = iot[:].rearrange("p (o e) -> p o e", o=1).broadcast_to([P, 32, 8])
        x = red(st[:, 3, :], pb_[:], ALU.max, x)
        y = tt("dve", oh[:], pb_[:], bcast(st[:, 3, :]), ALU.is_equal, x)
        y = tt("dve", pk[:], oh[:], iob, ALU.mult, y, io)
        y = red(st[:, 4, :], pk[:], ALU.max, y)
        y1 = tt("dve", oh[:], iob, bcast(st[:, 4, :]), ALU.is_equal, y)
        y = stt(pb_[:].rearrange("p t e -> p (t e)"), oh[:].rearrange("p t e -> p (t e)"), -4.0,
                pb_[:].rearrange("p t e -> p (t e)"), ALU.mult, ALU.add, y1)
        y = red(st[:, 5, :], pb_[:], ALU.max, y)
        z = tt("dve", pk[:], pb_[:], bcast(st[:, 5, :]), ALU.is_equal, y)
        z = tt("dve", pk[:], pk[:], iob, ALU.mult, z)
        z = red(st[:, 6, :], pk[:], ALU.max, z)
        z = tt("dve", pk[:], iob, bcast(st[:, 6, :]), ALU.is_equal, z)
        y = tt("dve", st[:, 7, :], st[:, 5, :], st[:, 3, :], ALU.subtract, y)
        y = actv(st[:, 0, :], st[:, 7, :], ACT.Exp, y, scale=0.5)
        y = ts("dve", st[:, 1, :], st[:, 0, :], 1.0, None, ALU.add, None, y)
        y = dve(lambda e: e.reciprocal(st[:, 2, :], st[:, 1, :]), y)
        y2 = tt("dve", st[:, 4, :], st[:, 0, :], st[:, 2, :], ALU.mult, y, y1)
        z = tt("dve", pk[:], pk[:], bcast(st[:, 4, :]), ALU.mult, z, y2)
        y = tt("dve", oh[:], oh[:], bcast(st[:, 2, :]), ALU.mult, y)
        r_w = tt("dve", wgt[:], oh[:], pk[:], ALU.add, y, z)
        wT = tmp("wT", [33, NB, T])
        wT0 = pool(lambda e: e.memset(wT[:], 0.0), done4)
        wT1 = dve(lambda e: e.memset(wT[32:33, :, :], 1.0), wT0)
        r_wT = []
        for b in range(NB):
            k = b % 4
            for j in range(4):
                m = tr(bank[k][0:8, P * j:P * j + P], wgt[:, 4 * b + j, :], ident[:], r_w, free[f"b{k}"])
            x = actv(wT[0:8, b, :], bank[k][0:8, :], ACT.Copy, m, wT1)
            free[f"b{k}"] = [x]
            r_wT.append(x)
        acc = tmp("acc", [P, 2, 4, P])
        r_x3 = [None] * NB
        last_acc = {}

        def down(b, e, gl):
            sl = (9 * b + (e + 1) % 9) % 2
            k = 6 + sl
            for j in range(4):
                for c in range(4):
                    r = ws2[:, c, :] if e == 8 else we2[:, e, c, :]
                    m = mm(bank[k][:, P * j:P * j + P], hid[:, sl, c, P * j:P * j + P], r, gl, l_e2, l_rest["ws2"], free[f"b{k}"],
                           start=(c == 0), stop=(c == 3 and e < 8))
                if e == 8:
                    m = mm(bank[k][:, P * j:P * j + P], wT[:, b, P * j:P * j + P], bsum[:], r_wT[b], l_rest["be2"],
                           l_rest["bs2"], wT1, start=False, stop=True)
            free[f"hid{sl}"] = [m]
            av = acc[:, b % 2]
            if e == 8:
                x = dve(lambda q: q.tensor_copy(av.rearrange("p j n -> p (j n)"), bank[k][:]), m, free.get(f"acc{b % 2}"))
                last_acc[b] = [x] * 4
            else:
                for j in range(4):
                    x = stt(av[:, j, :], bank[k][:, P * j:P * j + P], wgt[:, 4 * b + j, e:e + 1], av[:, j, :], ALU.mult,
                            ALU.add, m, last_acc[b][j], r_w)
                    last_acc[b][j] = x
            free[f"b{k}"] = [x]

        def finish(b):
            k = 5
            for j in range(4):
                m = tr(bank[k][:, P * j:P * j + P], acc[:, b % 2, j, :], ident[:], last_acc[b], free[f"b{k}"])
            free[f"acc{b % 2}"] = [m]
            r_x3[b] = stt(xT[:, b, :], bank[k][:], gate(1, b), xT[:, b, :], ALU.mult, ALU.add, m, r_h3[b])
            free[f"b{k}"] = [r_x3[b]]

        late = []
        u = 0
        for b in range(NB):
            for e in [8] + list(range(8)):
                sl = (9 * b + (e + 1) % 9) % 2
                gl = []
                for c in range(4):
                    k = u % 5
                    u += 1
                    lw = ws1[:, P * c:P * c + P] if e == 8 else we1[:, e, P * c:P * c + P]
                    bias = col("bs1", c) if e == 8 else col("be1", 4 * e + c)
                    m = mm(bank[k][:], lw, nT[:, b, :], r_h3[b], l_rest["ws1"], l_e1, free[f"b{k}"])
                    x = actv(hid[:, sl, c, :], bank[k][:], ACT.Silu, m, free.get(f"hid{sl}"), bias=bias)
                    free[f"b{k}"] = [x]
                    gl.append(x)
                late.append((b, e, gl))
                if len(late) > 1:
                    w = late.pop(0)
                    down(*w)
                    if w[1] == 7:
                        finish(w[0])
        down(*late.pop(0))
        finish(NB - 1)
        scr.close()

        done6 = r_x3 + [pr.queues[e][-1] for e in ("pe", "dve", "act", "pool")]
        scr = ExitStack()
        for i in range(8):
            free[f"b{i}"] = free[f"b{i}"] + done6
        n4 = nT[:].rearrange("p b t -> p (b t)").rearrange("p (r s t j) -> p r s t j", r=4, s=8, t=2)
        r_h4 = [layer_norm(n4[:, b // 2, :, b % 2, :], xT[:, b, :], mod[:, 1, 1, b:b + 1], mod[:, 1, 0, b:b + 1],
                           2 * (b % 4), r_x3[b], done6, fold=8)
                for b in range(NB)]
        lw0 = tmp("lw0", [P, 6, P])
        lwT = tmp("lwT", [P, 6, P])
        brow = tmp("brow", [1, 3 * P])
        W6 = ["L1_attn_Wq", "L1_attn_Wk", "L1_attn_Wv", "L1_ffn_W_r", "L1_ffn_W_k", "L1_ffn_W_v"]
        l_w6 = [dma(lw0[:, i, :], d[w], done6) for i, w in enumerate(W6)]
        l_b3 = [dma(brow[0:1, P * i:P * i + P], d[w].rearrange("(o c) -> o c", o=1), done6)
                for i, w in enumerate(["L1_attn_bq", "L1_attn_bk", "L1_attn_bv"])]
        for i in range(6):
            m = tr(bank[i // 4][:, P * (i % 4):P * (i % 4) + P], lw0[:, i, :], ident[:], l_w6, free[f"b{i // 4}"])
        lwf = lwT[:].rearrange("p a b -> p (a b)")
        c_lw = [actv(lwf[:, 0:512], bank[0][:], ACT.Copy, m, done6), actv(lwf[:, 512:768], bank[1][:, 0:256], ACT.Copy, m, done6)]
        free["b0"] = [c_lw[0]]
        free["b1"] = [c_lw[1]]
        qkv = tmp("qkv", [P, 2, 3, 8, P])
        prod = tmp("prod", [P, 2, 8, P])
        prod2 = tmp("prod2", [P, 2, 8, P])
        scs = tmp("scs", [P, 8, 8, 8])
        mx1 = tmp("mx1", [P, 8, 8])
        ex1 = tmp("ex1", [P, 8, 8])
        sm1 = tmp("sm1", [P, 8, 8])
        oat = tmp("oat", [P, 8, P])
        r_x4 = [[r_x3[b], r_h4[b]] for b in range(NB)]
        big4 = xT[:].rearrange("p b (j t) -> p b j t", t=8)
        for pr_ in range(4):
            sl = pr_ % 2
            ev = []
            for s_ in range(8):
                k = s_ % 4
                lt = n4[:, pr_, s_].rearrange("p t j -> p (t j)")
                m = mm(bank[k][:, 0:384], lt, lwf[:, 0:384], c_lw, r_h4[2 * pr_], r_h4[2 * pr_ + 1], free[f"b{k}"],
                       start=True, stop=False)
                m = mm(bank[k][:, 0:384], ones[:], brow[:], l_b3, c_on, start=False, stop=True)
                a = actv(qkv[:, sl, 0, s_, :], bank[k][:, 0:128], ACT.Copy, m, free.get(f"qkv{sl}"), done6, scale=0.25)
                a = actv(qkv[:, sl, 1:3, s_, :], bank[k][:, 128:384].rearrange("p (a c) -> p a c", a=2), ACT.Copy, m)
                free[f"b{k}"] = [a]
                ev.append(a)
            q_, k_, v_ = qkv[:, sl, 0], qkv[:, sl, 1], qkv[:, sl, 2]
            scl = []
            for s_ in range(8):
                w = s_ % 2
                x = tt("pool", prod[:, w], q_[:, s_:s_ + 1, :].broadcast_to([P, 8, P]), k_, ALU.mult, ev, free.get(f"prod{w}"), done6)
                y = dve(lambda e, w=w, s_=s_: e.tensor_reduce(scs[:, s_], prod[:, w].rearrange("p a (h x) -> p a h x", x=16),
                                                              AX.X, ALU.add), x, free.get("scs"), done6)
                free[f"prod{w}"] = [y]
                scl.append(y)
            x = dve(lambda e: e.tensor_reduce(mx1[:], scs[:].rearrange("p s k h -> p s h k"), AX.X, ALU.max), scl,
                    free.get("mx1"), done6)
            x = ts("dve", mx1[:], mx1[:], 0.0, None, ALU.max, None, x)
            mb = mx1[:].rearrange("p s (o h) -> p s o h", o=1).broadcast_to([P, 8, 8, 8])
            for s_ in range(8):
                m1 = mx1[:, s_:s_ + 1, :].broadcast_to([P, 8, 8])
                y = tt("dve", scs[:, s_], scs[:, s_], m1, ALU.subtract, x)
            e1 = actv(scs[:].rearrange("p s k h -> p (s k h)"), scs[:].rearrange("p s k h -> p (s k h)"), ACT.Exp, y)
            e0 = actv(ex1[:], mx1[:], ACT.Exp, x, free.get("ex1"), done6, scale=-1.0)
            free["mx1"] = [e0, y]
            y = dve(lambda e: e.tensor_reduce(sm1[:], scs[:].rearrange("p s k h -> p s h k"), AX.X, ALU.add), e1, done6)
            y = stt(sm1[:].rearrange("p s h -> p (s h)"), ex1[:].rearrange("p s h -> p (s h)"), 57.0,
                    sm1[:].rearrange("p s h -> p (s h)"), ALU.mult, ALU.add, y, e0)
            free["ex1"] = [y]
            y = dve(lambda e: e.reciprocal(sm1[:], sm1[:]), y)
            for s_ in range(8):
                m1 = sm1[:, s_:s_ + 1, :].broadcast_to([P, 8, 8])
                y = tt("dve", scs[:, s_], scs[:, s_], m1, ALU.mult, y)
            ol = []
            for s_ in range(8):
                w = s_ % 2
                pe_ = scs[:, s_].rearrange("p k (h o) -> p (k h) o", o=1).broadcast_to([P, 64, 16])
                x = tt("pool", prod2[:, w].rearrange("p k (h x) -> p (k h) x", x=16), pe_,
                       v_.rearrange("p k (h x) -> p (k h) x", x=16), ALU.mult, y, free.get(f"prodv{w}"), done6)
                z = dve(lambda e, w=w, s_=s_: e.tensor_reduce(oat[:, s_, :], prod2[:, w].rearrange("p k c -> p c k"),
                                                              AX.X, ALU.add), x, free.get("oat"), done6)
                free[f"prodv{w}"] = [z]
                ol.append(z)
            free["scs"] = [x]
            free[f"qkv{sl}"] = [x]
            for half in range(2):
                k = 4 + half
                for j in range(4):
                    m = tr(bank[k][:, P * j:P * j + P], oat[:, 4 * half + j, :], ident[:], ol, free[f"b{k}"])
                for j in range(4):
                    s_ = 4 * half + j
                    dst = big4[:, s_, :, 2 * pr_:2 * pr_ + 2].rearrange("p j t -> p t j")
                    x = stt(dst, bank[k][:, P * j:P * j + P].rearrange("p (t j) -> p t j", t=2), gate(2, s_), dst,
                            ALU.mult, ALU.add, m, r_x4[s_], r_h4[s_])
                    r_x4[s_] = [x]
                free[f"b{k}"] = [x]
            free["oat"] = [m]

        att_done = [pr.queues["pe"][-1]]
        r_h5 = [layer_norm(hT[:, b, :], xT[:, b, :], mod[:, 1, 4, b:b + 1], mod[:, 1, 3, b:b + 1], 2 * (b % 3), r_x4[b], done6)
                for b in range(NB)]
        fl = zg.rearrange("p b h t -> p (b h t)")
        mu1 = tmp("mu1", [P, 2])
        xr = fl[:, 0:2048].rearrange("p (s i t) -> p s i t", s=2, i=2)
        rr = fl[:, 2048:3072].rearrange("p (s t) -> p s t", s=2)
        kk = fl[:, 3072:4096].rearrange("p (s t) -> p s t", s=2)
        oo = fl[:, 4096:5120].rearrange("p (s j c) -> p s j c", s=2, j=4)
        um = [ts("dve", mu1[:, i:i + 1], col(n_), -1.0, 1.0, ALU.mult, ALU.add, c_v, done6) for i, n_ in enumerate(("mu_r", "mu_k"))]
        stores = []
        od = out.rearrange("b (n p) c -> b p n c", p=P)
        u = 0
        for b in range(NB):
            s = b % 2
            mixd = []
            for i, n_ in enumerate(("mu_r", "mu_k")):
                x = actv(xr[:, s, i, :], hT[:, b, :], ACT.Copy, r_h5[b], free.get(f"xr{s}"), done6, scale=col(n_))
                x = stt(xr[:, s, i, 1:T], hT[:, b, 0:T - 1], mu1[:, i:i + 1], xr[:, s, i, 1:T], ALU.mult, ALU.add, x, um)
                mixd.append(x)
            ks = [(u + i) % 6 for i in range(3)]
            u += 3
            m = mm(bank[ks[0]][:], lwT[:, 3, :], xr[:, s, 0, :], mixd[0], c_lw, free[f"b{ks[0]}"])
            r1 = actv(rr[:, s, :], bank[ks[0]][:], ACT.Sigmoid, m, free.get(f"rr{s}"), done6)
            free[f"b{ks[0]}"] = [r1]
            m = mm(bank[ks[1]][:], lwT[:, 4, :], xr[:, s, 1, :], mixd[1], free[f"b{ks[1]}"])
            free[f"xr{s}"] = [m]
            k1 = actv(kk[:, s, :], bank[ks[1]][:], ACT.Relu, m, free.get(f"kk{s}"), done6)
            free[f"b{ks[1]}"] = [k1]
            k2 = tt("pool", kk[:, s, :], kk[:, s, :], kk[:, s, :], ALU.mult, k1)
            m = mm(bank[ks[2]][:], lwT[:, 5, :], kk[:, s, :], k2, free[f"b{ks[2]}"])
            free[f"kk{s}"] = [m]
            x = tt("dve", rr[:, s, :], bank[ks[2]][:], rr[:, s, :], ALU.mult, m, r1)
            free[f"b{ks[2]}"] = [x]
            x = stt(xT[:, b, :], rr[:, s, :], gate(3, b), xT[:, b, :], ALU.mult, ALU.add, x, r_x4[b], r_h5[b])
            free[f"rr{s}"] = [x]
            k = 6 + s
            for j in range(4):
                m = tr(bank[k][:, P * j:P * j + P], xT[:, b, P * j:P * j + P], ident[:], x, free[f"b{k}"])
            y = actv(oo[:, s].rearrange("p a c -> p (a c)"), bank[k][:], ACT.Copy, m, free.get(f"oo{s}"), done6)
            free[f"b{k}"] = [y]
            w = dma(od[b], oo[:, s], y)
            free[f"oo{s}"] = [w]
            stores.append(w)

        sems = {e: ctx.enter_context(nc.semaphore(f"s_{e}")) for e in pr.queues}
        pr.number(sems)
        block = ctx.enter_context(nc.Block())

        @block.tensor
        def _(e):
            pr.emit("pe", e)

        @block.vector
        def _(e):
            pr.emit("dve", e)

        @block.scalar
        def _(e):
            pr.emit("act", e)

        @block.gpsimd
        def _(e):
            pr.emit("pool", e)

        @block.sync
        def _(e):
            pr.emit("sp", e)
            for w in stores:
                e.wait_ge(w.sem, w.value)
        scr.close()


_INS = ['L0_attn_x', 'L0_attn_ln1_w', 'L0_attn_ln1_b', 'L0_attn_ln2_w', 'L0_attn_ln2_b', 'L0_attn_q_w', 'L0_attn_q_b',
        'L0_attn_k_w', 'L0_attn_k_b', 'L0_attn_v_w', 'L0_attn_v_b', 'L0_attn_o_w', 'L0_attn_o_b', 'L0_attn_in_proj_w',
        'L0_attn_conv_w', 'L0_attn_conv_b', 'L0_attn_x_proj_w', 'L0_attn_dt_w', 'L0_attn_dt_b', 'L0_attn_A_log',
        'L0_attn_D_param', 'L0_attn_ssm_out_w', 'L0_attn_mix_weight', 'L0_attn_ffn_w1', 'L0_attn_ffn_b1',
        'L0_attn_ffn_w2', 'L0_attn_ffn_b2', 'L0_ffn_Wr1', 'L0_ffn_br1', 'L0_ffn_Wr2', 'L0_ffn_br2', 'L0_ffn_Ws1',
        'L0_ffn_bs1', 'L0_ffn_Ws2', 'L0_ffn_bs2', 'L0_ffn_We1', 'L0_ffn_be1', 'L0_ffn_We2', 'L0_ffn_be2', 'L0_c',
        'L0_wmod', 'L1_attn_Wq', 'L1_attn_bq', 'L1_attn_Wk', 'L1_attn_bk', 'L1_attn_Wv', 'L1_attn_bv', 'L1_ffn_W_r',
        'L1_ffn_W_k', 'L1_ffn_W_v', 'L1_ffn_mu_r', 'L1_ffn_mu_k', 'L1_c', 'L1_wmod']


def kernel(**inputs):
    import numpy as _np
    import concourse.bacc as _bacc
    from concourse import mybir as _mybir
    from concourse.bass_utils import run_bass_kernel_spmd as _run

    nc = _bacc.Bacc("TRN2", target_bir_lowering=False, num_devices=1)
    arrays, args = {}, {}
    for name in _INS:
        a = _np.ascontiguousarray(inputs[name])
        arrays[f"in_{name}_dram"] = a
        args[name] = nc.dram_tensor(f"in_{name}_dram", a.shape, _mybir.dt.from_np(a.dtype), kind="ExternalInput").ap()
    out = nc.dram_tensor("out_0_dram", (8, 512, 128), _mybir.dt.float32, kind="ExternalOutput").ap()
    build(nc, args, out)
    r = _run(nc, [arrays], core_ids=[0])
    return r.results[0]["out_0_dram"]
```

```python
from contextlib import ExitStack

import concourse.bass as bass
from concourse import mybir

F32 = mybir.dt.float32
BF16 = mybir.dt.bfloat16
ALU = mybir.AluOpType
ACT = mybir.ActivationFunctionType
AX = mybir.AxisListType

P = 128
NB = 8
T = 512
EPS = 1e-5
QS = 8.0 ** -0.5
NEG = -1e30
SSM_RATE = 24.5


class Op:

    def __init__(self, eng, fn, waits, step):
        self.eng, self.fn, self.waits, self.step = eng, fn, waits, step
        self.signals = False
        self.sem = None
        self.value = 0


class Program:

    def __init__(self):
        self.queues = {e: [] for e in ("pe", "dve", "act", "pool", "sp")}

    def op(self, eng, fn, *waits, sem=None, step=1):
        flat = []
        for w in waits:
            if isinstance(w, (list, tuple)):
                flat += [x for x in w if x is not None]
            elif w is not None:
                flat.append(w)
        for w in flat:
            w.signals = True
        o = Op(eng, fn, flat, step)
        if sem is not None:
            o.sem, o.value = sem, step
        self.queues[eng].append(o)
        return o

    def number(self, sems):
        for eng, q in self.queues.items():
            n = 0
            for o in q:
                if o.sem is None and o.signals:
                    n += 1
                    o.sem, o.value = sems[eng], n

    def emit(self, eng, handle):
        seen = {}
        for o in self.queues[eng]:
            need = {}
            for w in o.waits:
                if w.value > max(seen.get(id(w.sem), 0), need.get(id(w.sem), (0, None))[0]):
                    need[id(w.sem)] = (w.value, w.sem)
            for k, (v, s) in need.items():
                handle.wait_ge(s, v)
                seen[k] = v
            ins = o.fn(handle)
            if o.value:
                ins.then_inc(o.sem, o.step)


def run_together(lead, pieces, *others):
    due = [0.0] * len(others)
    for _ in lead:
        for i, (g, n, _) in enumerate(others):
            due[i] += n / pieces
            while due[i] >= 1:
                due[i] -= 1
                next(g, None)
    for g, _, whole in others:
        if whole:
            for _ in g:
                pass


def build(nc, d, out):
    pr = Program()
    with ExitStack() as ctx:
        def sb(name, shape, dt=F32):
            return ctx.enter_context(nc.sbuf_tensor(name, shape, dt))

        bank = [ctx.enter_context(nc.psum_tensor(f"bank{i}", [P, 512], F32)) for i in range(8)]

        def pe(fn, *w):
            return pr.op("pe", fn, *w)

        def dve(fn, *w):
            return pr.op("dve", fn, *w)

        def act(fn, *w):
            return pr.op("act", fn, *w)

        def pool(fn, *w):
            return pr.op("pool", fn, *w)

        ndma = [0]

        def dma(dst, src, *w, eng="sp"):
            s = ctx.enter_context(nc.semaphore(f"s_dma{ndma[0]}"))
            ndma[0] += 1
            return pr.op(eng, lambda e: e.dma_start(dst, src), *w, sem=s, step=16)

        def mm(o, l, r, *w, start=True, stop=True, pos=None):
            return pe(lambda e: e.matmul(o, l, r, start=start, stop=stop, tile_position=pos, skip_group_check=True), *w)

        def tr(o, i, idn, *w):
            return pe(lambda e: e.transpose(o, i, idn), *w)

        def actv(o, i, f, *w, scale=1.0, bias=0.0):
            return act(lambda e: e.activation(o, i, f, scale=scale, bias=bias), *w)

        def table(name, *w):
            return act(lambda e: e.preload_act_table_set(name), *w)

        def tt(eng, o, a, b, op, *w):
            return pr.op(eng, lambda e: e.tensor_tensor(o, a, b, op), *w)

        def ts(eng, o, a, s1, s2, op0, op1, *w):
            if s2 is None:
                return pr.op(eng, lambda e: e.tensor_scalar(o, a, s1, None, op0), *w)
            return pr.op(eng, lambda e: e.tensor_scalar(o, a, s1, s2, op0, op1), *w)

        def stt(o, a, s, b, op0, op1, *w):
            return dve(lambda e: e.scalar_tensor_tensor(out=o, in0=a, scalar=s, in1=b, op0=op0, op1=op1), *w)

        free = {}

        hT = sb("hT", [P, NB, T])
        nT = sb("nT", [P, NB, T])
        big = sb("big", [P, 2, NB, 2, T])
        xc = big[:, 0]
        zg = big[:, 1]

        ident = sb("ident", [P, P])
        cmat = sb("cmat", [P, P])
        omat = sb("omat", [P, P])
        ones = sb("ones", [1, P])
        mask = sb("mask", [P, 512], BF16)
        seld = sb("seld", [P, P])
        epsc = sb("epsc", [P, 1])

        stg = nT[:, 3, :]
        vrow = stg[:, 384:512]
        vcol = sb("vcol", [P, P])
        wqk = sb("wqk", [P, 2, P])
        wv = sb("wv", [P, P])
        wo = sb("wo", [P, 4, P])
        qbs = sb("qbs", [P, 1])
        On = sb("On", [P, 2, T])
        win = On[:, 0, :]
        cw = sb("cw", [P, 2, 4])
        wxp = sb("wxp", [P, 2, 40])
        wdt = sb("wdt", [8, 256])
        alog = sb("alog", [P, 2, 16])
        wso = sb("wso", [P, 2, P])
        wr1 = sb("wr1", [P, 32])
        br1 = sb("br1", [32, 1])
        wr2 = sb("wr2", [33, 8])
        bsum = sb("bsum", [33, P])
        crow = stg[0:16, 0:P]
        cT = sb("cT", [P, 16])
        mod = sb("mod", [P, 2, 6, NB])
        gab = sb("gab", [P, 4, NB])
        gtmp = sb("gtmp", [P, 3, 4, NB])
        avec = sb("avec", [P, 4])
        woT = stg[:, 256:384]

        xin = xc.rearrange("p a b c -> p (a b c)")[:, 0:4096].rearrange("p (n c) -> p n c", c=P)
        xd = d["L0_attn_x"].rearrange("b (n p) c -> b p n c", p=P)
        l_x = [dma(xin[:, 4 * b:4 * b + 4, :], xd[b]) for b in range(NB)]
        ROWS = [("ln1_w", "L0_attn_ln1_w", 1), ("ln1_b", "L0_attn_ln1_b", 1), ("ln2_w", "L0_attn_ln2_w", 1),
                ("ln2_b", "L0_attn_ln2_b", 1), ("o_b", "L0_attn_o_b", 1), ("v_b", "L0_attn_v_b", 1),
                ("conv_b", "L0_attn_conv_b", 2), ("dt_b", "L0_attn_dt_b", 2), ("D", "L0_attn_D_param", 2),
                ("mix", "L0_attn_mix_weight", 1), ("ffn_b1", "L0_attn_ffn_b1", 4), ("ffn_b2", "L0_attn_ffn_b2", 1),
                ("bs1", "L0_ffn_bs1", 4), ("be1", "L0_ffn_be1", 32), ("mu_r", "L1_ffn_mu_r", 1),
                ("mu_k", "L1_ffn_mu_k", 1), ("q_b", "L0_attn_q_b", 1), ("k_b", "L0_attn_k_b", 1)]
        v0 = pool(lambda e: e.memset(vrow, 0.0))
        l_rows = [v0]
        at = {}
        n = 0
        for k, name, m in ROWS:
            src = d[name]
            src = src.rearrange("e (m c) -> (e m) c", c=P) if len(src.shape) == 2 else src.rearrange("(m c) -> m c", c=P)
            at[k] = n
            l_rows.append(dma(vrow[n:n + m, :], src, v0, eng="act"))
            n += m
        NR = n

        def col(k, j=0):
            return vcol[:, at[k] + j:at[k] + j + 1]

        l_c = [dma(crow[0:8, :], d["L0_c"]), dma(crow[8:16, :], d["L1_c"])]
        wm = nT[:, 0:3, :].rearrange("p a b -> p (a b)").rearrange("p (l k c) -> p l k c", l=2, k=6)
        l_wm = [dma(wm[:, 0], d["L0_wmod"].rearrange("p (k c) -> p k c", k=6)),
                dma(wm[:, 1], d["L1_wmod"].rearrange("p (k c) -> p k c", k=6))]
        l_qk = [dma(wqk[:, 0, :], d["L0_attn_q_w"]), dma(wqk[:, 1, :], d["L0_attn_k_w"])]
        l_wv = dma(wv[:], d["L0_attn_v_w"])
        l_in = dma(win, d["L0_attn_in_proj_w"])
        l_cw = dma(cw[:], d["L0_attn_conv_w"].rearrange("(h p) k -> p h k", p=P))
        l_xp = dma(wxp[:], d["L0_attn_x_proj_w"].rearrange("(h p) k -> p h k", p=P))
        l_dt = dma(wdt[:], d["L0_attn_dt_w"])
        l_al = dma(alog[:], d["L0_attn_A_log"].rearrange("(h p) k -> p h k", p=P))
        l_so = dma(wso[:], d["L0_attn_ssm_out_w"].rearrange("(h p) k -> p h k", p=P))
        l_woT = dma(woT, d["L0_attn_o_w"])

        z0 = [pool(lambda e: e.memset(wo[:], 0.0))]
        c_id0 = pool(lambda e: e.memset(ident[:], 0.0))
        c_id = pool(lambda e: e.affine_select(out=ident[:], in_=ident[:], compare_op=ALU.not_equal, fill=1.0, base=0,
                                              pattern=[[-1, P]], channel_multiplier=1), c_id0)
        c_om = pool(lambda e: e.memset(omat[:], 1.0 / P))
        c_cm = tt("pool", cmat[:], ident[:], omat[:], ALU.subtract, c_id, c_om)
        c_on = pool(lambda e: e.memset(ones[:], 1.0))
        c_ep = pool(lambda e: e.memset(epsc[:], EPS))
        m0 = pool(lambda e: e.memset(mask[:], 0.0))
        c_mk = pool(lambda e: e.affine_select(out=mask[:, 384:512], in_=mask[:, 384:512], compare_op=ALU.is_ge, fill=NEG,
                                              base=0, pattern=[[-1, P]], channel_multiplier=1), m0)
        sd = pool(lambda e: e.memset(seld[:], 0.0))
        sd = pool(lambda e: e.affine_select(out=seld[:].rearrange("p (i j) -> p i j", i=4),
                                            in_=seld[:].rearrange("p (i j) -> p i j", i=4), compare_op=ALU.not_equal,
                                            fill=1.0, base=-8, pattern=[[-32, 4], [0, 32]], channel_multiplier=1), sd)
        c_sel = sd
        l_wo = []
        for i in range(4):
            l_wo.append(dma(wo[32 * i:32 * i + 8, :, :],
                            d["L0_attn_o_w"].rearrange("(g i d) n -> i d g n", i=4, d=8)[i], z0))
        zb = pool(lambda e: e.memset(bsum[:], 0.0))
        l_rest = {
            "wr1": dma(wr1[:], d["L0_ffn_Wr1"]),
            "br1": dma(br1[:], d["L0_ffn_br1"].rearrange("(p o) -> p o", o=1)),
            "wr2": dma(wr2[0:32, :], d["L0_ffn_Wr2"]),
            "br2": dma(wr2[32:33, :], d["L0_ffn_br2"].rearrange("(o p) -> o p", o=1)),
            "be2": dma(bsum[0:8, :], d["L0_ffn_be2"], zb),
            "bs2": dma(bsum[32:33, :], d["L0_ffn_bs2"].rearrange("(o p) -> o p", o=1), zb),
        }

        t = tr(bank[0][:, 0:NR], vrow[0:NR, :], ident[0:NR, 0:NR], l_rows, c_id)
        c_v = actv(vcol[:, 0:NR], bank[0][:, 0:NR], ACT.Copy, t)
        c_early = [t]
        t = tr(bank[1][:, 0:16], crow, ident[0:16, 0:16], l_c, c_id)
        c_cT = actv(cT[:], bank[1][:, 0:16], ACT.Silu, t)
        last = None
        for l in range(2):
            for k in range(6):
                last = mm(bank[2][:, 48 * l + 8 * k:48 * l + 8 * k + 8], wm[:, l, k, :], cT[:, 8 * l:8 * l + 8], c_cT, l_wm)
        md = actv(mod[:].rearrange("p l k b -> p (l k b)"), bank[2][:, 0:96], ACT.Copy, last)
        free["wm"] = [last, md] + c_early
        sc = [ts("dve", mod[:, :, k, :], mod[:, :, k, :], 1.0, None, ALU.add, None, md) for k in (1, 4)]
        g = mod[:].rearrange("p l (u k) b -> p l u k b", u=2)[:, :, :, 2, :]
        gt = gtmp[:].rearrange("p a (l u) b -> p a l u b", l=2)
        gv = gab[:].rearrange("p (l u) b -> p l u b", l=2)
        neg = ts("dve", gtmp[:, 0].rearrange("p (l u) b -> p l u b", l=2), g, -1.0, None, ALU.mult, None, md)
        ab = tt("dve", gt[:, 1], gt[:, 0], g, ALU.max, neg)
        sg = ts("dve", gt[:, 2], g, 0.0, 2.0, ALU.is_ge, ALU.mult, md)
        ab = ts("dve", gt[:, 0], gt[:, 1], 0.25, None, ALU.max, None, ab)
        sg = ts("dve", gt[:, 1], gt[:, 2], -1.0, None, ALU.add, None, sg, ab)
        c_g = tt("dve", gv, gt[:, 1], gt[:, 0], ALU.mult, sg, ab)
        c_mod = [c_g] + sc

        def gate(j, b):
            return gab[:, j, b:b + 1]

        sgm = actv(avec[:, 0:1], col("mix"), ACT.Sigmoid, c_v)
        om1 = ts("dve", avec[:, 1:2], avec[:, 0:1], -1.0, 1.0, ALU.mult, ALU.add, sgm)
        t = t_wo = mm(bank[3][:, 0:2], woT, vcol[:, at["v_b"]:at["v_b"] + 2], l_woT, c_v)
        t = ts("dve", avec[:, 2:3], bank[3][:, 0:1], col("o_b"), None, ALU.add, None, t)
        c_av = [om1, tt("dve", avec[:, 3:4], avec[:, 2:3], avec[:, 0:1], ALU.mult, t, sgm)]
        ea = actv(alog[:], alog[:], ACT.Exp, l_al)
        c_A = ts("dve", alog[:], alog[:], -1.0, None, ALU.mult, None, ea)
        c_qb = ts("dve", qbs[:], col("q_b"), QS, None, ALU.mult, None, c_v)

        r_x = [None] * NB
        for b in range(NB):
            bk = bank[4 + b % 4]
            for j in range(4):
                t = tr(bk[:, P * j:P * j + P], xin[:, 4 * b + j, :], ident[:], l_x[b], c_id, free.get(f"b{4 + b % 4}"))
            if b % 2:
                r_x[b] = actv(hT[:, b, :], bk[:], ACT.Copy, t)
            else:
                r_x[b] = dve(lambda e, b=b, bk=bk: e.tensor_copy(hT[:, b, :], bk[:]), t)
            free[f"b{4 + b % 4}"] = [r_x[b]]
        free["xin"] = r_x

        lsq = sb("lsq", [P, 2, T])
        lrs = sb("lrs", [P, 2, T])
        for i in range(8):
            free.setdefault(f"b{i}", [c_v, c_cT, md, c_av[1]] + r_x)
        ln_n = [0]

        def layer_norm(dst, src, scale, shift, b0, *w, dst_free=None, fold=None):
            i = ln_n[0] % 2
            ln_n[0] += 1
            c = mm(bank[b0][:], cmat[:], src, c_cm, free[f"b{b0}"], *w)
            s = actv(lsq[:, i, :], bank[b0][:], ACT.Square, c, free.get(f"lsq{i}"))
            v = mm(bank[b0 + 1][:], omat[:], lsq[:, i, :], s, c_om, free[f"b{b0 + 1}"])
            free[f"lsq{i}"] = [v]
            g1 = actv(lrs[:, i, :], bank[b0 + 1][:], ACT.Ln, v, c_ep, free.get(f"lrs{i}"), bias=epsc[:])
            free[f"b{b0 + 1}"] = [g1]
            g2 = actv(lrs[:, i, :], lrs[:, i, :], ACT.Exp, g1, scale=-0.5)
            xcen, rstd = bank[b0][:], lrs[:, i, :]
            if fold:
                xcen, rstd = [a.rearrange("p (s j) -> p s j", s=fold) for a in (xcen, rstd)]
            o = stt(dst, xcen, scale, rstd, ALU.mult, ALU.mult, g2, dst_free)
            free[f"b{b0}"] = [o]
            free[f"lrs{i}"] = [o]
            return ts("pool", dst, dst, shift, None, ALU.add, None, o)

        table("natural_log_exp_and_others")
        r_h = [None] * NB
        r_n = [None] * NB
        for b in range(NB):
            r_h[b] = layer_norm(hT[:, b, :], hT[:, b, :], mod[:, 0, 1, b:b + 1], mod[:, 0, 0, b:b + 1], 2 * (b % 4),
                                r_x[b], c_mod, md)
        for b in range(NB):
            r_n[b] = layer_norm(nT[:, b, :], hT[:, b, :], col("ln1_w"), col("ln1_b"), 2 * (b % 4),
                                r_h[b], dst_free=free["wm"] + [t_wo])

        r_xc = [[None, None] for _ in range(NB)]
        r_z = [[None, None] for _ in range(NB)]
        u = 0
        for b in range(NB):
            for h in range(2):
                k = u % 8
                u += 1
                m = mm(bank[k][:], win[:, P * h:P * h + P], nT[:, b, :], l_in, r_n[b], free[f"b{k}"])
                o = xc[:, b, h, :]
                c = ts("dve", o, bank[k][:], cw[:, h, 3:4], col("conv_b", h), ALU.mult, ALU.add, m, l_cw, c_v, free["xin"])
                for j in range(1, 4):
                    c = stt(o[:, j:T], bank[k][:, 0:T - j], cw[:, h, 3 - j:4 - j], o[:, j:T], ALU.mult, ALU.add, c)
                free[f"b{k}"] = [c]
                r_xc[b][h] = actv(o, o, ACT.Silu, c)
                k = u % 8
                u += 1
                m = mm(bank[k][:], win[:, 256 + P * h:256 + P * h + P], nT[:, b, :], free[f"b{k}"])
                r_z[b][h] = actv(zg[:, b, h, :], bank[k][:], ACT.Silu, m)
                free[f"b{k}"] = [r_z[b][h]]
        free["On0"] = [m]

        table("natural_log_exp_and_others")
        scr = ExitStack()

        def tmp(name, shape, dt=F32):
            return scr.enter_context(nc.sbuf_tensor(name, shape, dt))

        QK = tmp("QK", [P, 2, 3, 4, T], BF16)
        Vb = tmp("Vb", [P, 2, 4, 16, 32])
        Mx = tmp("Mx", [P, 2, 4, 8])
        mrow = tmp("mrow", [8, 2, T], BF16)
        qf = tmp("qf", [P, T])
        part = tmp("part", [P, 3, T], BF16)
        PT = tmp("PT", [P, 3, T])
        Os = tmp("Os", [P, T])
        rdn = lrs
        parts_d = [nc.dram_tensor(f"parts{i}", (2, 3, P, T), BF16, kind="Internal").ap() for i in range(2)]
        s_pw = [ctx.enter_context(nc.semaphore(f"s_pw{i}")) for i in range(2)]
        s_pr = [ctx.enter_context(nc.semaphore(f"s_pr{i}")) for i in range(3)]
        s_mr = [ctx.enter_context(nc.semaphore(f"s_mr{i}")) for i in range(2)]
        count = {}

        def dmas(sem, pairs, *w, eng="sp"):
            count[id(sem)] = count.get(id(sem), 0) + 16 * len(pairs)
            ops = [pr.op(eng, lambda e, a=a, c=c: e.dma_start(a, c), *w, sem=sem, step=16) for a, c in pairs]
            for o in ops:
                o.value = count[id(sem)]
            return ops[-1]

        zi = [pool(lambda e: e.memset(Vb[:], 0.0)), pool(lambda e: e.memset(mrow[:], 1.0))]
        zi.append(pool(lambda e: e.memset(Vb[:].rearrange("p a t h j -> p (a t h) j")[:, :, 8:9], 1.0), zi[0]))
        s_on = ctx.enter_context(nc.semaphore("s_on"))
        r_one = dmas(s_on, [(QK[64 * p + 48:64 * p + 49, 1, r, a, :], mrow[0:1, 0, :])
                            for p in range(2) for r in range(3) for a in range(4)], zi[1])

        ring = [0]

        def take():
            k = ring[0] % 3
            ring[0] += 1
            return k

        r_at = [None] * NB
        r_parts, r_v, r_qk, r_mr = {}, {}, {}, {}
        h_last = [[r_n[b]] for b in range(NB)]

        def project(b):
            xn = nT[:, b, :]
            prev = None
            for i, bias in ((0, qbs[:, 0:1]), (1, col("k_b"))):
                k = take()
                m = mm(bank[k][:], wqk[:, i, :], xn, l_qk, free[f"b{k}"], r_n[b])
                q1 = actv(qf[:], bank[k][:], ACT.Identity, m, c_qb, c_v, free.get("qf"), scale=QS if i == 0 else 1.0, bias=bias)
                free[f"b{k}"] = [q1]
                h1 = dve(lambda e: e.tensor_copy(part[:, 0, :], qf[:]), q1, free.get("part"))
                yield
                m1 = tt("dve", qf[:], qf[:], part[:, 0, :], ALU.subtract, h1)
                h2 = dve(lambda e: e.tensor_copy(part[:, 1, :], qf[:]), m1, free.get("part"))
                yield
                h3 = tt("pool", part[:, 2, :], qf[:], part[:, 1, :], ALU.subtract, h2, free.get("part"))
                free["qf"] = [h3]
                prev = dmas(s_pw[b % 2], [(parts_d[b % 2][i].rearrange("k c t -> c k t"), part[:])], h1, h2, h3,
                            free.get(f"pd{b % 2}"))
                free["part"] = [prev]
                yield
            r_parts[b] = prev
            k = take()
            for j in range(4):
                m = mm(bank[k][:, P * j:P * j + P], xn[:, P * j:P * j + P], wv[:], r_n[b], l_wv, free[f"b{k}"])
            vv = Vb[:, b % 2].rearrange("p t h j -> p (t h) j")[:, :, 0:8]
            r_v[b] = actv(vv, bank[k][:].rearrange("p (h j) -> p h j", j=8), ACT.Copy, m, zi, free.get(f"V{b % 2}"))
            free[f"b{k}"] = [r_v[b]]
            yield

        def fetch(u):
            b, hf, s = u // 2, u % 2, u % 3
            pairs = []
            for i in range(2):
                src = parts_d[b % 2][i].rearrange("k (f a p d) t -> f p k d a t", f=2, a=4, p=2)[hf]
                plan = [(0, 0), (1, 0), (2, 0), (3, 1), (4, 1), (5, 2)] if i == 0 else \
                    [(0, 0), (1, 1), (2, 2), (3, 0), (4, 1), (5, 0)]
                for p in range(2):
                    for r, k in plan:
                        pairs.append((QK[64 * p + 8 * r:64 * p + 8 * r + 8, i, s, :, :], src[p, k]))
            r_qk[u] = dmas(s_pr[s], pairs, r_parts[b], free.get(f"QK{s}"))
            if hf == 1:
                free[f"pd{b % 2}"] = [r_qk[u]]

        def maxima(u):
            b, s, s2 = u // 2, u % 3, u % 2
            mxs = []
            for h in range(8):
                a, p = h // 2, h % 2
                for qi in range(4):
                    kc = P * (qi + 1)
                    k = take()
                    m = mm(bank[k][:, 0:kc], QK[64 * p:64 * p + 48, 0, s, a, P * qi:P * qi + P],
                           QK[64 * p:64 * p + 48, 1, s, a, 0:kc], r_qk[u], free[f"b{k}"])
                    x = dve(lambda e, kc=kc, k=k, h=h, qi=qi: e.tensor_tensor_reduce(
                        bank[k][:, 0:kc], bank[k][:, 0:kc], mask[:, 512 - kc:512], 1.0, NEG, ALU.add, ALU.max,
                        Mx[:, s2, qi, h:h + 1]), m, c_mk, free.get(f"Mx{s2}"))
                    free[f"b{k}"] = [x]
                    mxs.append(x)
                    yield
            k = take()
            for qi in range(4):
                m = tr(bank[k][0:8, P * qi:P * qi + P], Mx[:, s2, qi, :], ident[:], mxs, free[f"b{k}"])
            free[f"Mx{s2}"] = [m]
            x = actv(mrow[:, s2, :], bank[k][0:8, :], ACT.Copy, m, r_one, free.get(f"mrow{s2}"), scale=-1.0)
            free[f"b{k}"] = [x]
            r_mr[u] = dmas(s_mr[s2], [(QK[64 * (h % 2) + 48:64 * (h % 2) + 49, 0, s, h // 2, :], mrow[h:h + 1, s2, :])
                                      for h in range(8)], x)
            free[f"mrow{s2}"] = [r_mr[u]]
            yield

        late = []
        later = []
        tick = [0]

        def weigh(b, g, parts, sl, ready):
            k = 3 + g % 2
            for i, kj, off in parts:
                n = T - P * kj
                m = mm(bank[k][32 * i:32 * i + 32, P * kj:T], Vb[:, b % 2, kj, 4 * g + i, :],
                       PT[:, sl, off:off + n], ready, r_v[b], free[f"b{k}"] if kj == 0 else None,
                       start=(kj == 0), stop=(kj == 3), pos=(0, 32 * i))
            free[f"PT{sl}"] = [m]
            return m

        def normalise(b, g, m):
            gg = g % 2
            o1 = actv(Os[:], bank[3 + gg][:], ACT.Copy, m, free.get("Os"))
            free[f"b{3 + gg}"] = [o1]
            yield
            yield
            k = take()
            m = mm(bank[k][:], seld[:], Os[:], o1, c_sel, free[f"b{k}"])
            e1 = actv(rdn[:, gg, :], bank[k][:], ACT.Ln, m, free.get(f"lrs{gg}"))
            free[f"b{k}"] = [e1]
            e2 = actv(rdn[:, gg, :], rdn[:, gg, :], ACT.Exp, e1, scale=-1.0)
            o2 = tt("pool", On[:, gg, :], Os[:], rdn[:, gg, :], ALU.mult, e2, free.get(f"On{gg}"))
            free["Os"] = [o2]
            free[f"lrs{gg}"] = [o2]
            r_on[g] = o2
            for _ in range(4):
                yield
            if gg == 0:
                return
            k = take()
            for j in range(2):
                m = mm(bank[k][:], wo[:, g - 1 + j, :], On[:, j, :], l_wo, z0, r_on[g - 1 + j], free[f"b{k}"],
                       start=(j == 0), stop=(j == 1))
                free[f"On{j}"] = [m]
            if g == 1:
                h_last[b] = [ts("pool", hT[:, b, :], hT[:, b, :], avec[:, 3:4], None, ALU.add, None, h_last[b], c_av)]
            h_last[b] = [stt(hT[:, b, :], bank[k][:], avec[:, 0:1], hT[:, b, :], ALU.mult, ALU.add, m, h_last[b])]
            free[f"b{k}"] = h_last[b]

        r_on = {}

        def settle(n):
            while len(late) > n:
                b, g, parts, sl, ready, end = late.pop(0)
                m = weigh(b, g, parts, sl, ready)
                if end:
                    if g == 3:
                        free[f"V{b % 2}"] = [m]
                    later.append(normalise(b, g, m))
            for x in list(later):
                if next(x, 0) == 0:
                    later.remove(x)

        def attend(u):
            b, hf, s = u // 2, u % 2, u % 3
            for gg in range(2):
                g = 2 * hf + gg
                units = [[(i, 0, 0)] for i in range(4)] + [[(i, 1, 0), (i, 3, 384)] for i in range(4)] + \
                    [[(i, 2, 0), (i + 2, 2, 256)] for i in range(2)]
                for parts in units:
                    k = take()
                    sl = pts[0] % 3
                    pts[0] += 1
                    for i, kj, off in parts:
                        n = T - P * kj
                        p, a = i % 2, 2 * gg + i // 2
                        m = mm(bank[k][:, off:off + n], QK[64 * p:64 * p + 49, 1, s, a, P * kj:P * kj + P],
                               QK[64 * p:64 * p + 49, 0, s, a, P * kj:T], r_mr[u], r_qk[u], r_one, free[f"b{k}"])
                    x = actv(PT[:, sl, :], bank[k][:], ACT.Exp, m, free.get(f"PT{sl}"))
                    free[f"b{k}"] = [x]
                    if len(parts) == 1:
                        v3 = PT[:, sl, 0:P]
                        pat = [[1, P]]
                    else:
                        o2 = parts[1][2]
                        v3 = PT[:, sl, 0:512].rearrange("p (a n) -> p a n", n=P)[:, 0:o2 // P + 1:o2 // P, :]
                        pat = [[0, 2], [1, P]]
                    y = pool(lambda e, v3=v3, pat=pat: e.affine_select(
                        out=v3, in_=v3, compare_op=ALU.is_ge, fill=0.0, base=0, pattern=pat,
                        channel_multiplier=-1), x)
                    late.append((b, g, parts, sl, [x, y], parts is units[-1]))
                    settle(2)
                    yield
            free[f"QK{s}"] = [m]

        pts = [0]
        bc = tmp("bc", [P, 4, 32])
        sp1 = lsq
        dtv = tmp("dtv", [P, 2, T])
        dtxT = tmp("dtxT", [P, 4, 256])
        dBx = tmp("dBx", [P, 2, 4, 256])
        dA = tmp("dA", [P, 2, T])
        hst = tmp("hst", [P, 4, T])
        yT = tmp("yT", [P, 4, 256])
        sp2 = yT[:].rearrange("p a b -> p (a b)").rearrange("p (h t) -> p h t", h=2)
        dtr = sp2[0:8, 1, :]
        ring2 = [0]

        def take2():
            k = 5 + ring2[0] % 3
            ring2[0] += 1
            return k

        def state_space(b):
            xcb, zb = xc[:, b], zg[:, b]
            k, k2 = take2(), take2()
            for h in range(2):
                m = mm(bank[k][0:8, :], wxp[:, h, 0:8], xcb[:, h, :], l_xp, r_xc[b][h], free[f"b{k}"], start=(h == 0), stop=(h == 1))
            for j in range(4):
                for h in range(2):
                    m2 = mm(bank[k2][:, 32 * j:32 * j + 32], xcb[:, h, P * j:P * j + P], wxp[:, h, 8:40], free[f"b{k2}"],
                            start=(h == 0), stop=(h == 1))
            e1 = actv(dtr, bank[k][0:8, :], ACT.Copy, m, free.get("yT"), free.get("sp"))
            e2 = dve(lambda e: e.tensor_copy(bc[:].rearrange("p a b -> p (a b)"), bank[k2][:, 0:P]), m2, free.get("bc"))
            free[f"b{k}"] = [e1]
            free[f"b{k2}"] = [e2]
            yield
            yield
            r_dt, dxs = [], []
            ks = []
            for h in range(2):
                k = take2()
                ks.append(k)
                m = mm(bank[k][:], wdt[:, P * h:P * h + P], dtr, e1, l_dt, free[f"b{k}"])
                a1 = actv(sp1[:, h, :], bank[k][:], ACT.Abs, m, c_v, free.get("sp"), free.get(f"lsq{h}"), bias=col("dt_b", h))
                a2 = actv(sp1[:, h, :], sp1[:, h, :], ACT.Exp, a1, scale=-1.0)
                a3 = actv(sp1[:, h, :], sp1[:, h, :], ACT.Ln, a2, bias=1.0)
                v1 = ts("dve", sp2[:, h, :], bank[k][:], col("dt_b", h), 0.0, ALU.add, ALU.max, a1, free.get("sp"), free.get("yT"))
                free[f"b{k}"] = [a1, v1]
                v2 = tt("pool", dtv[:, h, :], sp1[:, h, :], sp2[:, h, :], ALU.add, a3, v1, free.get("dtv"))
                v3 = tt("pool", sp2[:, h, :], dtv[:, h, :], xcb[:, h, :], ALU.mult, v2)
                r_dt.append(v2)
                dxs.append(v3)
                yield
            yield
            yield
            r_dx = []
            for h in range(2):
                k = take2()
                for j in range(4):
                    m = tr(bank[k][:, P * j:P * j + P], sp2[:, h, P * j:P * j + P], ident[:], dxs[h], free[f"b{k}"])
                x = dve(lambda e, h=h, k=k: e.tensor_copy(dtxT[:, :, P * h:P * h + P],
                                                          bank[k][:].rearrange("p (j c) -> p j c", j=4)), m, free.get("dtxT"))
                free[f"b{k}"] = [x]
                r_dx.append(x)
                yield
            free["sp"] = [m, v2]
            y_last = [None] * 4

            def accumulate(n, hs):
                for half in range(2):
                    k = take2()
                    for jj in range(2):
                        for h in range(2):
                            j = 2 * half + jj
                            m = tr(bank[k][:, 256 * jj + P * h:256 * jj + P * h + P], hst[:, hs[h][0], P * j:P * j + P],
                                   ident[:], hs[h][1], free[f"b{k}"])
                    for jj in range(2):
                        j = 2 * half + jj
                        src = bank[k][:, 256 * jj:256 * jj + 256]
                        if n == 0:
                            y = ts("dve", yT[:, j, :], src, bc[:, j, 16:17], None, ALU.mult, None, m, free.get("sp"))
                        else:
                            y = stt(yT[:, j, :], src, bc[:, j, 16 + n:17 + n], yT[:, j, :], ALU.mult, ALU.add, m, y_last[j])
                        y_last[j] = y
                    free[f"b{k}"] = [y]
                for h in range(2):
                    free[f"hst{hs[h][0]}"] = [m]

            def spread(n):
                sl = n % 2
                return tt("pool", dBx[:, sl], dtxT[:], bc[:, :, n:n + 1].broadcast_to([P, 4, 256]), ALU.mult,
                          r_dx, e2, free.get(f"dBx{sl}"))

            pend = None
            dx = spread(0)
            yield
            yield
            for n in range(16):
                sl = n % 2
                hs = []
                now = dx
                for h in range(2):
                    a = 2 * sl + h
                    k = take2()
                    x = actv(dA[:, h, :], dtv[:, h, :], ACT.Exp, r_dt[h], c_A, free.get(f"dA{h}"), scale=alog[:, h, n:n + 1])
                    for j in range(4):
                        m = tr(bank[k][:, P * j:P * j + P], dBx[:, sl, j, P * h:P * h + P], ident[:], now, free[f"b{k}"])
                    sc = dve(lambda e, a=a, k=k, h=h: e.tensor_tensor_scan(hst[:, a, :], dA[:, h, :], bank[k][:], 0.0,
                                                                          ALU.mult, ALU.add), m, x, free.get(f"hst{a}"))
                    free[f"b{k}"] = [sc]
                    free[f"dA{h}"] = [sc]
                    hs.append((a, sc))
                free[f"dBx{sl}"] = [m]
                if n < 15:
                    dx = spread(n + 1)
                yield
                if pend:
                    accumulate(*pend)
                    yield
                pend = (n, hs)
            accumulate(*pend)
            yield
            free["dtxT"] = [dx]
            free["dtv"] = [x]
            free["bc"] = y_last + [dx]
            ys = []
            for h in range(2):
                k = take2()
                for j in range(4):
                    m = tr(bank[k][:, P * j:P * j + P], yT[:, j, P * h:P * h + P], ident[:], y_last, free[f"b{k}"])
                y = stt(xcb[:, h, :], xcb[:, h, :], col("D", h), bank[k][:], ALU.mult, ALU.add, m, dxs[h])
                free[f"b{k}"] = [y]
                ys.append(tt("pool", zb[:, h, :], zb[:, h, :], xcb[:, h, :], ALU.mult, y, r_z[b][h]))
                yield
            free["yT"] = [m]
            yield
            k = take2()
            for h in range(2):
                m = mm(bank[k][:], wso[:, h, :], zb[:, h, :], ys[h], l_so, free[f"b{k}"], start=(h == 0), stop=(h == 1))
            h_last[b] = [stt(hT[:, b, :], bank[k][:], avec[:, 1:2], hT[:, b, :], ALU.mult, ALU.add, m, h_last[b])]
            free[f"b{k}"] = h_last[b]
            yield

        def chain(*gens):
            for x in gens:
                yield from x

        def drain(gen):
            for _ in gen:
                pass

        def prepare(u):
            if u % 2 == 0:
                yield from project(u // 2)
            fetch(u)
            yield

        NU = 2 * NB
        ssm = chain(*[state_space(b) for b in range(NB)])
        drain(prepare(0))
        run_together(maxima(0), 33, (prepare(1), 1, True), (ssm, 8, False))
        for u in range(NU):
            others = [(ssm, SSM_RATE, False)]
            if u + 1 < NU:
                others.append((maxima(u + 1), 43, True))
            if u + 2 < NU:
                others.append((prepare(u + 2), 18 if u % 2 == 0 else 20, True))
            run_together(attend(u), 20, *others)
        while late or later:
            settle(0)
        drain(ssm)
        r_sm = [h_last[b][0] for b in range(NB)]
        scr.close()

        xT = sb("xT", [P, NB, T])
        done4 = r_sm + [pr.queues[e][-1] for e in ("pe", "dve", "act", "pool")]
        scr = ExitStack()
        we1 = big[:, 0].rearrange("p b h t -> p (b h t)")[:, 0:4096].rearrange("p (e i) -> p e i", e=8)
        we2 = big[:, 0].rearrange("p b h t -> p (b h t)")[:, 4096:8192].rearrange("p (e k n) -> p e k n", e=8, k=4)
        l_e1 = dma(we1, d["L0_ffn_We1"].rearrange("e c i -> c e i"), done4)
        l_e2 = dma(we2, d["L0_ffn_We2"].rearrange("e (k p) n -> p e k n", p=P), done4)
        hid = tmp("hid", [P, 2, 4, T])
        xin2 = tmp("xin2", [P, 2, 4, P])
        w1 = tmp("w1", [P, 512])
        w2 = tmp("w2", [P, 4, P])
        ws1 = tmp("ws1", [P, 512])
        ws2 = tmp("ws2", [P, 4, P])
        l_rest["w1"] = dma(w1[:], d["L0_attn_ffn_w1"], done4)
        l_rest["w2"] = dma(w2[:], d["L0_attn_ffn_w2"].rearrange("(k p) n -> p k n", p=P), done4)
        l_rest["ws1"] = dma(ws1[:], d["L0_ffn_Ws1"], done4)
        l_rest["ws2"] = dma(ws2[:], d["L0_ffn_Ws2"].rearrange("(k p) n -> p k n", p=P), done4)
        for i in range(8):
            free[f"b{i}"] = free[f"b{i}"] + done4
        r_h2 = [layer_norm(nT[:, b, :], hT[:, b, :], col("ln2_w"), col("ln2_b"), 2 * (b % 4), r_sm[b], done4)
                for b in range(NB)]
        r_x2 = [None] * NB
        pend = []

        def ffn_down(b, gl):
            k = 6 + b % 2
            for c in range(4):
                m = mm(bank[k][:], w2[:, c, :], hid[:, b % 2, c, :], gl[c], l_rest["w2"], free[f"b{k}"], start=(c == 0), stop=(c == 3))
            free[f"hid{b % 2}"] = [m]
            a = stt(hT[:, b, :], bank[k][:], col("ffn_b2"), hT[:, b, :], ALU.add, ALU.add, m, r_h2[b])
            l = dma(xin2[:, b % 2], xd[b], free.get(f"xin2{b % 2}"), done4)
            for j in range(4):
                m = tr(bank[k][:, P * j:P * j + P], xin2[:, b % 2, j, :], ident[:], l, a)
            free[f"xin2{b % 2}"] = [m]
            r_x2[b] = stt(xT[:, b, :], hT[:, b, :], gate(0, b), bank[k][:], ALU.mult, ALU.add, m, a, c_g, done4)
            free[f"b{k}"] = [r_x2[b]]

        u = 0
        for b in range(NB):
            gl = []
            for c in range(4):
                k = u % 6
                u += 1
                m = mm(bank[k][:], w1[:, P * c:P * c + P], nT[:, b, :], r_h2[b], l_rest["w1"], free[f"b{k}"])
                x = actv(hid[:, b % 2, c, :], bank[k][:], ACT.Gelu, m, free.get(f"hid{b % 2}"), done4, bias=col("ffn_b1", c))
                free[f"b{k}"] = [x]
                gl.append(x)
            free[f"nT{b}"] = [m]
            pend.append((b, gl))
            if len(pend) > 1:
                ffn_down(*pend.pop(0))
        ffn_down(*pend.pop(0))

        table("natural_log_exp_and_others")
        r_h3 = [layer_norm(nT[:, b, :], xT[:, b, :], mod[:, 0, 4, b:b + 1], mod[:, 0, 3, b:b + 1], 2 * (b % 3), r_x2[b],
                           dst_free=free[f"nT{b}"]) for b in range(NB)]
        hr = tmp("hr", [33, 2, T])
        lg = tmp("lg", [P, 32, 8])
        pb_ = tmp("pb_", [P, 32, 8])
        oh = tmp("oh", [P, 32, 8])
        pk = tmp("pk", [P, 32, 8])
        wgt = tmp("wgt", [P, 32, 8])
        iot = tmp("iot", [P, 8])
        st = tmp("st", [P, 8, 32])
        iot_i = tmp("iot_i", [P, 8], mybir.dt.int32)
        h1 = dve(lambda e: e.memset(hr[32:33, :, :], 1.0), done4)
        io = pool(lambda e: e.iota(iot_i[:], pattern=[[-1, 8]], base=8, channel_multiplier=0), done4)
        io = pool(lambda e: e.tensor_copy(iot[:], iot_i[:]), io)
        for b in range(NB):
            k = b % 4
            m = mm(bank[k][0:32, :], wr1[:], nT[:, b, :], r_h3[b], l_rest["wr1"], free[f"b{k}"])
            x = ts("dve", hr[0:32, b % 2, :], bank[k][0:32, :], br1[:, 0:1], 0.0, ALU.add, ALU.max, m, l_rest["br1"],
                   free.get(f"hr{b % 2}"), done4)
            free[f"b{k}"] = [x]
            for j in range(4):
                m = mm(bank[5][:, 32 * b + 8 * j:32 * b + 8 * j + 8], hr[:, b % 2, P * j:P * j + P], wr2[:],
                       x, h1, l_rest["wr2"], l_rest["br2"], free["b5"])
            free[f"hr{b % 2}"] = [m]
        lgf = lg[:].rearrange("p t e -> p (t e)")
        x = dve(lambda e: e.tensor_copy(lgf, bank[5][:, 0:256]), m, done4)
        free["b5"] = [x]

        def bcast(a):
            return a.rearrange("p (t o) -> p t o", o=1).broadcast_to([P, 32, 8])

        def red(dst, src, op, *w):
            return dve(lambda e: e.tensor_reduce(dst, src, AX.X, op), *w)

        x = red(st[:, 0, :], lg[:], ALU.max, x)
        x = tt("dve", lg[:], lg[:], bcast(st[:, 0, :]), ALU.subtract, x)
        x = actv(pb_[:], lg[:], ACT.Exp, x)
        x = red(st[:, 1, :], pb_[:], ALU.add, x)
        x = dve(lambda e: e.reciprocal(st[:, 2, :], st[:, 1, :]), x)
        x = tt("dve", pb_[:], pb_[:], bcast(st[:, 2, :]), ALU.mult, x)
        iob = iot[:].rearrange("p (o e) -> p o e", o=1).broadcast_to([P, 32, 8])
        x = red(st[:, 3, :], pb_[:], ALU.max, x)
        y = tt("dve", oh[:], pb_[:], bcast(st[:, 3, :]), ALU.is_equal, x)
        y = tt("dve", pk[:], oh[:], iob, ALU.mult, y, io)
        y = red(st[:, 4, :], pk[:], ALU.max, y)
        y1 = tt("dve", oh[:], iob, bcast(st[:, 4, :]), ALU.is_equal, y)
        y = stt(pb_[:].rearrange("p t e -> p (t e)"), oh[:].rearrange("p t e -> p (t e)"), -4.0,
                pb_[:].rearrange("p t e -> p (t e)"), ALU.mult, ALU.add, y1)
        y = red(st[:, 5, :], pb_[:], ALU.max, y)
        z = tt("dve", pk[:], pb_[:], bcast(st[:, 5, :]), ALU.is_equal, y)
        z = tt("dve", pk[:], pk[:], iob, ALU.mult, z)
        z = red(st[:, 6, :], pk[:], ALU.max, z)
        z = tt("dve", pk[:], iob, bcast(st[:, 6, :]), ALU.is_equal, z)
        y = tt("dve", st[:, 7, :], st[:, 5, :], st[:, 3, :], ALU.subtract, y)
        y = actv(st[:, 0, :], st[:, 7, :], ACT.Exp, y, scale=0.5)
        y = ts("dve", st[:, 1, :], st[:, 0, :], 1.0, None, ALU.add, None, y)
        y = dve(lambda e: e.reciprocal(st[:, 2, :], st[:, 1, :]), y)
        y2 = tt("dve", st[:, 4, :], st[:, 0, :], st[:, 2, :], ALU.mult, y, y1)
        z = tt("dve", pk[:], pk[:], bcast(st[:, 4, :]), ALU.mult, z, y2)
        y = tt("dve", oh[:], oh[:], bcast(st[:, 2, :]), ALU.mult, y)
        r_w = tt("dve", wgt[:], oh[:], pk[:], ALU.add, y, z)
        wT = tmp("wT", [33, NB, T])
        wT0 = pool(lambda e: e.memset(wT[:], 0.0), done4)
        wT1 = dve(lambda e: e.memset(wT[32:33, :, :], 1.0), wT0)
        r_wT = []
        for b in range(NB):
            k = b % 4
            for j in range(4):
                m = tr(bank[k][0:8, P * j:P * j + P], wgt[:, 4 * b + j, :], ident[:], r_w, free[f"b{k}"])
            x = actv(wT[0:8, b, :], bank[k][0:8, :], ACT.Copy, m, wT1)
            free[f"b{k}"] = [x]
            r_wT.append(x)
        acc = tmp("acc", [P, 2, 4, P])
        r_x3 = [None] * NB
        last_acc = {}

        def down(b, e, gl):
            sl = (9 * b + (e + 1) % 9) % 2
            k = 6 + sl
            for j in range(4):
                for c in range(4):
                    r = ws2[:, c, :] if e == 8 else we2[:, e, c, :]
                    m = mm(bank[k][:, P * j:P * j + P], hid[:, sl, c, P * j:P * j + P], r, gl, l_e2, l_rest["ws2"], free[f"b{k}"],
                           start=(c == 0), stop=(c == 3 and e < 8))
                if e == 8:
                    m = mm(bank[k][:, P * j:P * j + P], wT[:, b, P * j:P * j + P], bsum[:], r_wT[b], l_rest["be2"],
                           l_rest["bs2"], wT1, start=False, stop=True)
            free[f"hid{sl}"] = [m]
            av = acc[:, b % 2]
            if e == 8:
                x = dve(lambda q: q.tensor_copy(av.rearrange("p j n -> p (j n)"), bank[k][:]), m, free.get(f"acc{b % 2}"))
                last_acc[b] = [x] * 4
            else:
                for j in range(4):
                    x = stt(av[:, j, :], bank[k][:, P * j:P * j + P], wgt[:, 4 * b + j, e:e + 1], av[:, j, :], ALU.mult,
                            ALU.add, m, last_acc[b][j], r_w)
                    last_acc[b][j] = x
            free[f"b{k}"] = [x]

        def finish(b):
            k = 5
            for j in range(4):
                m = tr(bank[k][:, P * j:P * j + P], acc[:, b % 2, j, :], ident[:], last_acc[b], free[f"b{k}"])
            free[f"acc{b % 2}"] = [m]
            r_x3[b] = stt(xT[:, b, :], bank[k][:], gate(1, b), xT[:, b, :], ALU.mult, ALU.add, m, r_h3[b])
            free[f"b{k}"] = [r_x3[b]]

        late = []
        u = 0
        for b in range(NB):
            for e in [8] + list(range(8)):
                sl = (9 * b + (e + 1) % 9) % 2
                gl = []
                for c in range(4):
                    k = u % 5
                    u += 1
                    lw = ws1[:, P * c:P * c + P] if e == 8 else we1[:, e, P * c:P * c + P]
                    bias = col("bs1", c) if e == 8 else col("be1", 4 * e + c)
                    m = mm(bank[k][:], lw, nT[:, b, :], r_h3[b], l_rest["ws1"], l_e1, free[f"b{k}"])
                    x = actv(hid[:, sl, c, :], bank[k][:], ACT.Silu, m, free.get(f"hid{sl}"), bias=bias)
                    free[f"b{k}"] = [x]
                    gl.append(x)
                late.append((b, e, gl))
                if len(late) > 1:
                    w = late.pop(0)
                    down(*w)
                    if w[1] == 7:
                        finish(w[0])
        down(*late.pop(0))
        finish(NB - 1)
        scr.close()

        done6 = r_x3 + [pr.queues[e][-1] for e in ("pe", "dve", "act", "pool")]
        scr = ExitStack()
        for i in range(8):
            free[f"b{i}"] = free[f"b{i}"] + done6
        table("natural_log_exp_and_others")
        n4 = nT[:].rearrange("p b t -> p (b t)").rearrange("p (r s t j) -> p r s t j", r=4, s=8, t=2)
        r_h4 = [layer_norm(n4[:, b // 2, :, b % 2, :], xT[:, b, :], mod[:, 1, 1, b:b + 1], mod[:, 1, 0, b:b + 1],
                           2 * (b % 4), r_x3[b], done6, fold=8)
                for b in range(NB)]
        lw0 = tmp("lw0", [P, 6, P])
        lwT = tmp("lwT", [P, 6, P])
        brow = tmp("brow", [1, 3 * P])
        W6 = ["L1_attn_Wq", "L1_attn_Wk", "L1_attn_Wv", "L1_ffn_W_r", "L1_ffn_W_k", "L1_ffn_W_v"]
        l_w6 = [dma(lw0[:, i, :], d[w], done6) for i, w in enumerate(W6)]
        l_b3 = [dma(brow[0:1, P * i:P * i + P], d[w].rearrange("(o c) -> o c", o=1), done6)
                for i, w in enumerate(["L1_attn_bq", "L1_attn_bk", "L1_attn_bv"])]
        for i in range(6):
            m = tr(bank[i // 4][:, P * (i % 4):P * (i % 4) + P], lw0[:, i, :], ident[:], l_w6, free[f"b{i // 4}"])
        lwf = lwT[:].rearrange("p a b -> p (a b)")
        c_lw = [actv(lwf[:, 0:512], bank[0][:], ACT.Copy, m, done6), actv(lwf[:, 512:768], bank[1][:, 0:256], ACT.Copy, m, done6)]
        free["b0"] = [c_lw[0]]
        free["b1"] = [c_lw[1]]
        qkv = tmp("qkv", [P, 2, 3, 8, P])
        prod = tmp("prod", [P, 2, 8, P])
        prod2 = tmp("prod2", [P, 2, 8, P])
        scs = tmp("scs", [P, 8, 8, 8])
        mx1 = tmp("mx1", [P, 8, 8])
        ex1 = tmp("ex1", [P, 8, 8])
        sm1 = tmp("sm1", [P, 8, 8])
        oat = tmp("oat", [P, 8, P])
        r_x4 = [[r_x3[b], r_h4[b]] for b in range(NB)]
        big4 = xT[:].rearrange("p b (j t) -> p b j t", t=8)
        for pr_ in range(4):
            sl = pr_ % 2
            ev = []
            for s_ in range(8):
                k = s_ % 4
                lt = n4[:, pr_, s_].rearrange("p t j -> p (t j)")
                m = mm(bank[k][:, 0:384], lt, lwf[:, 0:384], c_lw, r_h4[2 * pr_], r_h4[2 * pr_ + 1], free[f"b{k}"],
                       start=True, stop=False)
                m = mm(bank[k][:, 0:384], ones[:], brow[:], l_b3, c_on, start=False, stop=True)
                a = actv(qkv[:, sl, 0, s_, :], bank[k][:, 0:128], ACT.Copy, m, free.get(f"qkv{sl}"), done6, scale=0.25)
                a = actv(qkv[:, sl, 1:3, s_, :], bank[k][:, 128:384].rearrange("p (a c) -> p a c", a=2), ACT.Copy, m)
                free[f"b{k}"] = [a]
                ev.append(a)
            q_, k_, v_ = qkv[:, sl, 0], qkv[:, sl, 1], qkv[:, sl, 2]
            scl = []
            for s_ in range(8):
                w = s_ % 2
                x = tt("pool", prod[:, w], q_[:, s_:s_ + 1, :].broadcast_to([P, 8, P]), k_, ALU.mult, ev, free.get(f"prod{w}"), done6)
                y = dve(lambda e, w=w, s_=s_: e.tensor_reduce(scs[:, s_], prod[:, w].rearrange("p a (h x) -> p a h x", x=16),
                                                              AX.X, ALU.add), x, free.get("scs"), done6)
                free[f"prod{w}"] = [y]
                scl.append(y)
            x = dve(lambda e: e.tensor_reduce(mx1[:], scs[:].rearrange("p s k h -> p s h k"), AX.X, ALU.max), scl,
                    free.get("mx1"), done6)
            x = ts("dve", mx1[:], mx1[:], 0.0, None, ALU.max, None, x)
            mb = mx1[:].rearrange("p s (o h) -> p s o h", o=1).broadcast_to([P, 8, 8, 8])
            for s_ in range(8):
                m1 = mx1[:, s_:s_ + 1, :].broadcast_to([P, 8, 8])
                y = tt("dve", scs[:, s_], scs[:, s_], m1, ALU.subtract, x)
            e1 = actv(scs[:].rearrange("p s k h -> p (s k h)"), scs[:].rearrange("p s k h -> p (s k h)"), ACT.Exp, y)
            e0 = actv(ex1[:], mx1[:], ACT.Exp, x, free.get("ex1"), done6, scale=-1.0)
            free["mx1"] = [e0, y]
            y = dve(lambda e: e.tensor_reduce(sm1[:], scs[:].rearrange("p s k h -> p s h k"), AX.X, ALU.add), e1, done6)
            y = stt(sm1[:].rearrange("p s h -> p (s h)"), ex1[:].rearrange("p s h -> p (s h)"), 57.0,
                    sm1[:].rearrange("p s h -> p (s h)"), ALU.mult, ALU.add, y, e0)
            free["ex1"] = [y]
            y = dve(lambda e: e.reciprocal(sm1[:], sm1[:]), y)
            for s_ in range(8):
                m1 = sm1[:, s_:s_ + 1, :].broadcast_to([P, 8, 8])
                y = tt("dve", scs[:, s_], scs[:, s_], m1, ALU.mult, y)
            ol = []
            for s_ in range(8):
                w = s_ % 2
                pe_ = scs[:, s_].rearrange("p k (h o) -> p (k h) o", o=1).broadcast_to([P, 64, 16])
                x = tt("pool", prod2[:, w].rearrange("p k (h x) -> p (k h) x", x=16), pe_,
                       v_.rearrange("p k (h x) -> p (k h) x", x=16), ALU.mult, y, free.get(f"prodv{w}"), done6)
                z = dve(lambda e, w=w, s_=s_: e.tensor_reduce(oat[:, s_, :], prod2[:, w].rearrange("p k c -> p c k"),
                                                              AX.X, ALU.add), x, free.get("oat"), done6)
                free[f"prodv{w}"] = [z]
                ol.append(z)
            free["scs"] = [x]
            free[f"qkv{sl}"] = [x]
            for half in range(2):
                k = 4 + half
                for j in range(4):
                    m = tr(bank[k][:, P * j:P * j + P], oat[:, 4 * half + j, :], ident[:], ol, free[f"b{k}"])
                for j in range(4):
                    s_ = 4 * half + j
                    dst = big4[:, s_, :, 2 * pr_:2 * pr_ + 2].rearrange("p j t -> p t j")
                    x = stt(dst, bank[k][:, P * j:P * j + P].rearrange("p (t j) -> p t j", t=2), gate(2, s_), dst,
                            ALU.mult, ALU.add, m, r_x4[s_], r_h4[s_])
                    r_x4[s_] = [x]
                free[f"b{k}"] = [x]
            free["oat"] = [m]

        att_done = [pr.queues["pe"][-1]]
        r_h5 = [layer_norm(hT[:, b, :], xT[:, b, :], mod[:, 1, 4, b:b + 1], mod[:, 1, 3, b:b + 1], 2 * (b % 3), r_x4[b], done6)
                for b in range(NB)]
        fl = zg.rearrange("p b h t -> p (b h t)")
        mu1 = tmp("mu1", [P, 2])
        xr = fl[:, 0:2048].rearrange("p (s i t) -> p s i t", s=2, i=2)
        rr = fl[:, 2048:3072].rearrange("p (s t) -> p s t", s=2)
        kk = fl[:, 3072:4096].rearrange("p (s t) -> p s t", s=2)
        oo = fl[:, 4096:5120].rearrange("p (s j c) -> p s j c", s=2, j=4)
        um = [ts("dve", mu1[:, i:i + 1], col(n_), -1.0, 1.0, ALU.mult, ALU.add, c_v, done6) for i, n_ in enumerate(("mu_r", "mu_k"))]
        stores = []
        od = out.rearrange("b (n p) c -> b p n c", p=P)
        u = 0
        for b in range(NB):
            s = b % 2
            mixd = []
            for i, n_ in enumerate(("mu_r", "mu_k")):
                x = actv(xr[:, s, i, :], hT[:, b, :], ACT.Copy, r_h5[b], free.get(f"xr{s}"), done6, scale=col(n_))
                x = stt(xr[:, s, i, 1:T], hT[:, b, 0:T - 1], mu1[:, i:i + 1], xr[:, s, i, 1:T], ALU.mult, ALU.add, x, um)
                mixd.append(x)
            ks = [(u + i) % 6 for i in range(3)]
            u += 3
            m = mm(bank[ks[0]][:], lwT[:, 3, :], xr[:, s, 0, :], mixd[0], c_lw, free[f"b{ks[0]}"])
            r1 = actv(rr[:, s, :], bank[ks[0]][:], ACT.Sigmoid, m, free.get(f"rr{s}"), done6)
            free[f"b{ks[0]}"] = [r1]
            m = mm(bank[ks[1]][:], lwT[:, 4, :], xr[:, s, 1, :], mixd[1], free[f"b{ks[1]}"])
            free[f"xr{s}"] = [m]
            k1 = actv(kk[:, s, :], bank[ks[1]][:], ACT.Relu, m, free.get(f"kk{s}"), done6)
            free[f"b{ks[1]}"] = [k1]
            k2 = tt("pool", kk[:, s, :], kk[:, s, :], kk[:, s, :], ALU.mult, k1)
            m = mm(bank[ks[2]][:], lwT[:, 5, :], kk[:, s, :], k2, free[f"b{ks[2]}"])
            free[f"kk{s}"] = [m]
            x = tt("dve", rr[:, s, :], bank[ks[2]][:], rr[:, s, :], ALU.mult, m, r1)
            free[f"b{ks[2]}"] = [x]
            x = stt(xT[:, b, :], rr[:, s, :], gate(3, b), xT[:, b, :], ALU.mult, ALU.add, x, r_x4[b], r_h5[b])
            free[f"rr{s}"] = [x]
            k = 6 + s
            for j in range(4):
                m = tr(bank[k][:, P * j:P * j + P], xT[:, b, P * j:P * j + P], ident[:], x, free[f"b{k}"])
            y = actv(oo[:, s].rearrange("p a c -> p (a c)"), bank[k][:], ACT.Copy, m, free.get(f"oo{s}"), done6)
            free[f"b{k}"] = [y]
            w = dma(od[b], oo[:, s], y)
            free[f"oo{s}"] = [w]
            stores.append(w)

        sems = {e: ctx.enter_context(nc.semaphore(f"s_{e}")) for e in pr.queues}
        pr.number(sems)
        block = ctx.enter_context(nc.Block())

        @block.tensor
        def _(e):
            pr.emit("pe", e)

        @block.vector
        def _(e):
            pr.emit("dve", e)

        @block.scalar
        def _(e):
            pr.emit("act", e)

        @block.gpsimd
        def _(e):
            pr.emit("pool", e)

        @block.sync
        def _(e):
            pr.emit("sp", e)
            for w in stores:
                e.wait_ge(w.sem, w.value)
        scr.close()


_INS = ['L0_attn_x', 'L0_attn_ln1_w', 'L0_attn_ln1_b', 'L0_attn_ln2_w', 'L0_attn_ln2_b', 'L0_attn_q_w', 'L0_attn_q_b',
        'L0_attn_k_w', 'L0_attn_k_b', 'L0_attn_v_w', 'L0_attn_v_b', 'L0_attn_o_w', 'L0_attn_o_b', 'L0_attn_in_proj_w',
        'L0_attn_conv_w', 'L0_attn_conv_b', 'L0_attn_x_proj_w', 'L0_attn_dt_w', 'L0_attn_dt_b', 'L0_attn_A_log',
        'L0_attn_D_param', 'L0_attn_ssm_out_w', 'L0_attn_mix_weight', 'L0_attn_ffn_w1', 'L0_attn_ffn_b1',
        'L0_attn_ffn_w2', 'L0_attn_ffn_b2', 'L0_ffn_Wr1', 'L0_ffn_br1', 'L0_ffn_Wr2', 'L0_ffn_br2', 'L0_ffn_Ws1',
        'L0_ffn_bs1', 'L0_ffn_Ws2', 'L0_ffn_bs2', 'L0_ffn_We1', 'L0_ffn_be1', 'L0_ffn_We2', 'L0_ffn_be2', 'L0_c',
        'L0_wmod', 'L1_attn_Wq', 'L1_attn_bq', 'L1_attn_Wk', 'L1_attn_bk', 'L1_attn_Wv', 'L1_attn_bv', 'L1_ffn_W_r',
        'L1_ffn_W_k', 'L1_ffn_W_v', 'L1_ffn_mu_r', 'L1_ffn_mu_k', 'L1_c', 'L1_wmod']


def kernel(**inputs):
    import numpy as _np
    import concourse.bacc as _bacc
    from concourse import mybir as _mybir
    from concourse.bass_utils import run_bass_kernel_spmd as _run

    nc = _bacc.Bacc("TRN2", target_bir_lowering=False, num_devices=1)
    arrays, args = {}, {}
    for name in _INS:
        a = _np.ascontiguousarray(inputs[name])
        arrays[f"in_{name}_dram"] = a
        args[name] = nc.dram_tensor(f"in_{name}_dram", a.shape, _mybir.dt.from_np(a.dtype), kind="ExternalInput").ap()
    out = nc.dram_tensor("out_0_dram", (8, 512, 128), _mybir.dt.float32, kind="ExternalOutput").ap()
    build(nc, args, out)
    r = _run(nc, [arrays], core_ids=[0])
    return r.results[0]["out_0_dram"]
```

```python
from contextlib import ExitStack

import concourse.bass as bass
from concourse import mybir

F32 = mybir.dt.float32
BF16 = mybir.dt.bfloat16
F32R = mybir.dt.float32r
ALU = mybir.AluOpType
ACT = mybir.ActivationFunctionType
AX = mybir.AxisListType

P = 128
NB = 8
T = 512
EPS = 1e-5
QS = 8.0 ** -0.5
NEG = -1e30
SSM_RATE = 16
NPT = 6
LAG = 4
BEHIND = 1
ROUTE = 40
S4 = 13
OFF = 22
LEAD = 8
SECOND = (2,)
START = 6


class Op:

    def __init__(self, eng, fn, waits, step):
        self.eng, self.fn, self.waits, self.step = eng, fn, waits, step
        self.signals = False
        self.sem = None
        self.value = 0


class Program:

    def __init__(self):
        self.queues = {e: [] for e in ("pe", "dve", "act", "pool", "sp")}

    def op(self, eng, fn, *waits, sem=None, step=1):
        flat, todo = [], list(waits)
        while todo:
            w = todo.pop(0)
            if isinstance(w, (list, tuple)):
                todo += w
            elif w is not None:
                flat.append(w)
        for w in flat:
            w.signals = True
        o = Op(eng, fn, flat, step)
        if sem is not None:
            o.sem, o.value = sem, step
        self.queues[eng].append(o)
        return o

    def number(self, sems):
        for eng, q in self.queues.items():
            n = 0
            for o in q:
                if o.sem is None and o.signals:
                    n += 1
                    o.sem, o.value = sems[eng], n

    def emit(self, eng, handle):
        seen = {}
        for o in self.queues[eng]:
            need = {}
            for w in o.waits:
                if w.value > max(seen.get(id(w.sem), 0), need.get(id(w.sem), (0, None))[0]):
                    need[id(w.sem)] = (w.value, w.sem)
            for k, (v, s) in need.items():
                handle.wait_ge(s, v)
                seen[k] = v
            ins = o.fn(handle)
            if o.value:
                ins.then_inc(o.sem, o.step)


def run_together(lead, pieces, *others):
    due = [0.0] * len(others)
    for _ in lead:
        for i, (g, n, _) in enumerate(others):
            due[i] += n / pieces
            while due[i] >= 1:
                due[i] -= 1
                next(g, None)
    for g, _, whole in others:
        if whole:
            for _ in g:
                pass


def staggered(n, *stages):
    for t in range(n + len(stages) - 1):
        for i in range(len(stages)):
            if 0 <= t - i < n:
                stages[i](t - i)


def build(nc, d, out):
    pr = Program()
    with ExitStack() as ctx:
        def sb(name, shape, dt=F32):
            return ctx.enter_context(nc.sbuf_tensor(name, shape, dt))

        bank = [ctx.enter_context(nc.psum_tensor(f"bank{i}", [P, 512], F32)) for i in range(8)]

        def pe(fn, *w):
            return pr.op("pe", fn, *w)

        def dve(fn, *w):
            return pr.op("dve", fn, *w)

        def act(fn, *w):
            return pr.op("act", fn, *w)

        def pool(fn, *w):
            return pr.op("pool", fn, *w)

        ndma = [0]

        def dma(dst, src, *w, eng="sp"):
            s = ctx.enter_context(nc.semaphore(f"s_dma{ndma[0]}"))
            ndma[0] += 1
            return pr.op(eng, lambda e: e.dma_start(dst, src), *w, sem=s, step=16)

        def mm(o, l, r, *w, start=True, stop=True, pos=None):
            return pe(lambda e: e.matmul(o, l, r, start=start, stop=stop, tile_position=pos, skip_group_check=True), *w)

        def tr(o, i, idn, *w):
            return pe(lambda e: e.transpose(o, i, idn), *w)

        def actv(o, i, f, *w, scale=1.0, bias=0.0):
            return act(lambda e: e.activation(o, i, f, scale=scale, bias=bias), *w)

        def table(name, *w):
            return act(lambda e: e.preload_act_table_set(name), *w)

        def tt(eng, o, a, b, op, *w):
            return pr.op(eng, lambda e: e.tensor_tensor(o, a, b, op), *w)

        def ts(eng, o, a, s1, s2, op0, op1, *w):
            if s2 is None:
                return pr.op(eng, lambda e: e.tensor_scalar(o, a, s1, None, op0), *w)
            return pr.op(eng, lambda e: e.tensor_scalar(o, a, s1, s2, op0, op1), *w)

        def stt(o, a, s, b, op0, op1, *w):
            return dve(lambda e: e.scalar_tensor_tensor(out=o, in0=a, scalar=s, in1=b, op0=op0, op1=op1), *w)

        free = {}

        hT = sb("hT", [P, NB, T])
        nT = sb("nT", [P, NB, T])

        ident = sb("ident", [P, P])
        cmat = sb("cmat", [P, P])
        omat = sb("omat", [P, P])
        ones = sb("ones", [1, P])
        mask = sb("mask", [P, 512], BF16)
        seld = sb("seld", [P, P])
        epsc = sb("epsc", [P, 1])

        stg = nT[:, 3, :]
        vrow = stg[:, 384:512]
        vcol = sb("vcol", [P, P])
        wqk0 = nT[:, 3, 0:256].rearrange("p (i c) -> p i c", i=2)
        wqk = sb("wqk", [P, 2, P])
        wv = sb("wv", [P, P])
        wo = sb("wo", [P, 4, P])
        qbs = sb("qbs", [P, 1])
        On = sb("On", [P, 2, T])
        win = sb("win", [P, T])[:]
        cw = sb("cw", [P, 2, 4])
        wxp = sb("wxp", [P, 2, 40])
        wdt = sb("wdt", [8, 256])
        alog = sb("alog", [P, 2, 16])
        wso = sb("wso", [P, 2, P])
        wr1 = sb("wr1", [P, 32])
        br1 = sb("br1", [32, 1])
        wr2 = sb("wr2", [33, 8])
        bsum = sb("bsum", [97, P])
        crow = nT[0:16, 4, 0:P]
        cT = sb("cT", [P, 16])
        mod = sb("mod", [P, 2, 6, NB])
        gab = sb("gab", [P, 4, NB])
        gtmp = sb("gtmp", [P, 3, 4, NB])
        avec = sb("avec", [P, 4])
        lsq = sb("lsq", [P, 2, T])
        lrs = sb("lrs", [P, 2, T])
        scr0 = ExitStack()
        xc = scr0.enter_context(nc.sbuf_tensor("xc", [P, 2, 2, T], F32))
        zg = scr0.enter_context(nc.sbuf_tensor("zg", [P, 2, 2, T], F32))
        hst = scr0.enter_context(nc.sbuf_tensor("hst", [P, 8, T], F32))
        woT = stg[:, 256:384]

        xin = hst[:].rearrange("p a t -> p (a t)").rearrange("p (n c) -> p n c", c=P)
        xd = d["L0_attn_x"].rearrange("b (n p) c -> b p n c", p=P)
        l_c = [dma(crow[0:8, :], d["L0_c"]), dma(crow[8:16, :], d["L1_c"])]
        wm = nT[:, 0:3, :].rearrange("p a b -> p (a b)").rearrange("p (l k c) -> p l k c", l=2, k=6)
        l_wm = [dma(wm[:, 0], d["L0_wmod"].rearrange("p (k c) -> p k c", k=6)),
                dma(wm[:, 1], d["L1_wmod"].rearrange("p (k c) -> p k c", k=6))]
        l_x = [dma(xin[:, 4 * b:4 * b + 4, :], xd[b]) for b in range(NB)]
        ROWS = [("q_b", "L0_attn_q_b", 1), ("k_b", "L0_attn_k_b", 1), ("ln1_w", "L0_attn_ln1_w", 1), ("ln1_b", "L0_attn_ln1_b", 1), ("ln2_w", "L0_attn_ln2_w", 1),
                ("ln2_b", "L0_attn_ln2_b", 1), ("o_b", "L0_attn_o_b", 1), ("v_b", "L0_attn_v_b", 1),
                ("conv_b", "L0_attn_conv_b", 2), ("dt_b", "L0_attn_dt_b", 2), ("D", "L0_attn_D_param", 2),
                ("mix", "L0_attn_mix_weight", 1), ("ffn_b1", "L0_attn_ffn_b1", 4), ("ffn_b2", "L0_attn_ffn_b2", 1),
                ("bs1", "L0_ffn_bs1", 4), ("be1", "L0_ffn_be1", 32), ("mu_r", "L1_ffn_mu_r", 1),
                ("mu_k", "L1_ffn_mu_k", 1)]
        v0 = pool(lambda e: e.memset(vrow, 0.0))
        l_rows = [v0]
        qkb = nT[0:2, 4, P:2 * P]
        l_qkb = []
        at = {}
        n = 0
        for k, name, m in ROWS:
            src = d[name]
            src = src.rearrange("e (m c) -> (e m) c", c=P) if len(src.shape) == 2 else src.rearrange("(m c) -> m c", c=P)
            at[k] = n
            if k in ("q_b", "k_b"):
                l_qkb.append(dma(qkb[n:n + 1, :], src, eng="act"))
            else:
                l_rows.append(dma(vrow[n:n + m, :], src, l_rows[0:3], eng="act"))
            n += m
            if n == 2:
                l_rows += [dve(lambda e, f=f: e.tensor_copy(
                    vrow[0:2, 64 * f:64 * f + 64].rearrange("c (q a) -> c q a", a=4),
                    qkb[:, 64 * f:64 * f + 64].rearrange("c (a q) -> c q a", a=4)), l_qkb, v0) for f in range(2)]
        NR = n

        def col(k, j=0):
            return vcol[:, at[k] + j:at[k] + j + 1]

        l_qk0 = [dma(wqk0[:, 0, :], d["L0_attn_q_w"]), dma(wqk0[:, 1, :], d["L0_attn_k_w"])]
        l_qk = [pool(lambda e, i=i, f=f: e.tensor_copy(
            wqk[:, i, 64 * f:64 * f + 64].rearrange("c (q a) -> c q a", a=4),
            wqk0[:, i, 64 * f:64 * f + 64].rearrange("c (a q) -> c q a", a=4)), l_qk0) for i in range(2) for f in range(2)]
        l_wv = dma(wv[:], d["L0_attn_v_w"])
        l_in = dma(win, d["L0_attn_in_proj_w"])
        l_cw = dma(cw[:], d["L0_attn_conv_w"].rearrange("(h p) k -> p h k", p=P))
        l_xp = dma(wxp[:], d["L0_attn_x_proj_w"].rearrange("(h p) k -> p h k", p=P))
        l_dt = dma(wdt[:], d["L0_attn_dt_w"])
        l_al = dma(alog[:], d["L0_attn_A_log"].rearrange("(h p) k -> p h k", p=P))
        l_so = dma(wso[:], d["L0_attn_ssm_out_w"].rearrange("(h p) k -> p h k", p=P))
        l_woT = dma(woT, d["L0_attn_o_w"])

        z0 = [pool(lambda e: e.memset(wo[:], 0.0))]
        c_id0 = pool(lambda e: e.memset(ident[:], 0.0))
        c_id = pool(lambda e: e.affine_select(out=ident[:], in_=ident[:], compare_op=ALU.not_equal, fill=1.0, base=0,
                                              pattern=[[-1, P]], channel_multiplier=1), c_id0)
        c_om = pool(lambda e: e.memset(omat[:], 1.0 / P))
        c_cm = tt("pool", cmat[:], ident[:], omat[:], ALU.subtract, c_id, c_om)
        c_on = pool(lambda e: e.memset(ones[:], 1.0))
        c_ep = pool(lambda e: e.memset(epsc[:], EPS))
        m0 = pool(lambda e: e.memset(mask[:], 0.0))
        c_mk = pool(lambda e: e.affine_select(out=mask[:, 384:512], in_=mask[:, 384:512], compare_op=ALU.is_ge, fill=NEG,
                                              base=0, pattern=[[-1, P]], channel_multiplier=1), m0)
        sd = pool(lambda e: e.memset(seld[:], 0.0))
        sd = pool(lambda e: e.affine_select(out=seld[:].rearrange("p (i j) -> p i j", i=4),
                                            in_=seld[:].rearrange("p (i j) -> p i j", i=4), compare_op=ALU.not_equal,
                                            fill=1.0, base=-8, pattern=[[-32, 4], [0, 32]], channel_multiplier=1), sd)
        c_sel = sd
        l_wo = []
        for i in range(4):
            l_wo.append(dma(wo[32 * i:32 * i + 8, :, :],
                            d["L0_attn_o_w"].rearrange("(g i d) n -> i d g n", i=4, d=8)[i], z0))
        zb = pool(lambda e: e.memset(bsum[:], 0.0))
        l_rest = {
            "wr1": dma(wr1[:], d["L0_ffn_Wr1"]),
            "br1": dma(br1[:], d["L0_ffn_br1"].rearrange("(p o) -> p o", o=1)),
            "wr2": dma(wr2[0:32, :], d["L0_ffn_Wr2"]),
            "br2": dma(wr2[32:33, :], d["L0_ffn_br2"].rearrange("(o p) -> o p", o=1)),
            "be2": dma(bsum[64:72, :], d["L0_ffn_be2"], zb),
            "bs2": dma(bsum[96:97, :], d["L0_ffn_bs2"].rearrange("(o p) -> o p", o=1), zb),
        }

        t = tr(bank[0][:, 0:NR], vrow[0:NR, :], ident[0:NR, 0:NR], l_rows, c_id)
        c_v = actv(vcol[:, 0:NR], bank[0][:, 0:NR], ACT.Copy, t)
        c_early = [t]
        t = tr(bank[1][:, 0:16], crow, ident[0:16, 0:16], l_c, c_id)
        c_cT = actv(cT[:], bank[1][:, 0:16], ACT.Silu, t)
        last = None
        for l in range(2):
            for k in range(6):
                last = mm(bank[2][:, 48 * l + 8 * k:48 * l + 8 * k + 8], wm[:, l, k, :], cT[:, 8 * l:8 * l + 8], c_cT, l_wm)
        md = actv(mod[:].rearrange("p l k b -> p (l k b)"), bank[2][:, 0:96], ACT.Copy, last)
        free["wm"] = [last, md] + c_early
        sc = [ts("dve", mod[:, :, k, :], mod[:, :, k, :], 1.0, None, ALU.add, None, md) for k in (1, 4)]
        g = mod[:].rearrange("p l (u k) b -> p l u k b", u=2)[:, :, :, 2, :]
        gt = gtmp[:].rearrange("p a (l u) b -> p a l u b", l=2)
        gv = gab[:].rearrange("p (l u) b -> p l u b", l=2)
        neg = ts("dve", gtmp[:, 0].rearrange("p (l u) b -> p l u b", l=2), g, -1.0, None, ALU.mult, None, md)
        ab = tt("dve", gt[:, 1], gt[:, 0], g, ALU.max, neg)
        sg = ts("dve", gt[:, 2], g, 0.0, 2.0, ALU.is_ge, ALU.mult, md)
        ab = ts("dve", gt[:, 0], gt[:, 1], 0.25, None, ALU.max, None, ab)
        sg = ts("dve", gt[:, 1], gt[:, 2], -1.0, None, ALU.add, None, sg, ab)
        c_g = tt("dve", gv, gt[:, 1], gt[:, 0], ALU.mult, sg, ab)
        c_mod = [c_g] + sc

        def gate(j, b):
            return gab[:, j, b:b + 1]

        sgm = actv(avec[:, 0:1], col("mix"), ACT.Sigmoid, c_v)
        om1 = ts("dve", avec[:, 1:2], avec[:, 0:1], -1.0, 1.0, ALU.mult, ALU.add, sgm)
        t = t_wo = mm(bank[3][:, 0:2], woT, vcol[:, at["v_b"]:at["v_b"] + 2], l_woT, c_v)
        t = ts("dve", avec[:, 2:3], bank[3][:, 0:1], col("o_b"), None, ALU.add, None, t)
        c_av = [om1, tt("dve", avec[:, 3:4], avec[:, 2:3], avec[:, 0:1], ALU.mult, t, sgm)]
        ea = actv(alog[:], alog[:], ACT.Exp, l_al)
        c_A = ts("dve", alog[:], alog[:], -1.0, None, ALU.mult, None, ea)
        c_qb = ts("dve", qbs[:], col("q_b"), QS, None, ALU.mult, None, c_v)

        r_x = [None] * NB
        for b in range(NB):
            bk = bank[4 + b % 4]
            for j in range(4):
                t = tr(bk[:, P * j:P * j + P], xin[:, 4 * b + j, :], ident[:], l_x[b], c_id, free.get(f"b{4 + b % 4}"))
            if b % 2:
                r_x[b] = actv(hT[:, b, :], bk[:], ACT.Copy, t)
            else:
                r_x[b] = dve(lambda e, b=b, bk=bk: e.tensor_copy(hT[:, b, :], bk[:]), t)
            free[f"b{4 + b % 4}"] = [r_x[b]]
            free[f"hst{b}"] = [t]

        for i in range(8):
            free.setdefault(f"b{i}", [c_v, c_cT, md, c_av[1]] + r_x)
        ln_n = [0]

        def norm_start(dst, src, scale, shift, banks, *w, dst_free=None, fold=None, squares=None):
            b0, b1 = banks
            i = ln_n[0] % 2
            ln_n[0] += 1
            c = mm(bank[b0][:], cmat[:], src, c_cm, free[f"b{b0}"], *w)
            sq, key = squares or (lsq[:, i, :], f"lsq{i}")
            s = actv(sq, bank[b0][:], ACT.Square, c, free.get(key))

            def finish():
                v = mm(bank[b1][:], omat[:], sq, s, c_om, free[f"b{b1}"])
                free[key] = [v]
                g1 = actv(lrs[:, i, :], bank[b1][:], ACT.Ln, v, c_ep, free.get(f"lrs{i}"), bias=epsc[:])
                free[f"b{b1}"] = [g1]
                g2 = actv(lrs[:, i, :], lrs[:, i, :], ACT.Exp, g1, scale=-0.5)
                xcen, rstd = bank[b0][:], lrs[:, i, :]
                if fold:
                    xcen, rstd = [a.rearrange("p (s j) -> p s j", s=fold) for a in (xcen, rstd)]
                o = stt(dst, xcen, scale, rstd, ALU.mult, ALU.mult, g2, dst_free)
                free[f"b{b0}"] = [o]
                free[f"lrs{i}"] = [o]
                return ts("dve" if i else "pool", dst, dst, shift, None, ALU.add, None, o)

            return finish

        def norms(calls):
            before = None
            for keep, at_, args, more in calls:
                f = norm_start(*args, **more)
                if before:
                    before[0][before[1]] = before[2]()
                before = keep, at_, f
                yield
            before[0][before[1]] = before[2]()

        def layer_norms(calls):
            done = [None] * NB
            for _ in norms([(done, i, args, more) for i, (args, more) in enumerate(calls)]):
                pass
            return done

        BK = ((0, 4), (1, 5), (2, 6), (3, 7))
        table("natural_log_exp_and_others")
        r_h = [None] * NB
        r_n = [None] * NB

        class First:

            def __init__(self, b, l, banks):
                self.b, self.l, self.banks = b, l, banks

            def call(self):
                b = self.b
                if self.l == 0:
                    return r_h, b, (hT[:, b, :], hT[:, b, :], mod[:, 0, 1, b:b + 1], mod[:, 0, 0, b:b + 1], self.banks,
                                    r_x[b], c_mod, md), {}
                return r_n, b, (nT[:, b, :], hT[:, b, :], col("ln1_w"), col("ln1_b"), self.banks, r_h[b]), \
                    {"dst_free": free["wm"] + [t_wo] + l_qk}

        def first_norms(order):
            banks = ((0, 4), (1, 5), (2, 4), (3, 5))
            return norms(First(b, l, banks[i % 4]).call() for i, (b, l) in enumerate(order))

        for _ in first_norms(((0, 0), (1, 0), (0, 1))):
            pass

        table("natural_log_exp_and_others")
        scr = ExitStack()

        def tmp(name, shape, dt=F32):
            return scr.enter_context(nc.sbuf_tensor(name, shape, dt))

        QK = tmp("QK", [P, 2, 3, 4, T], BF16)
        Vb = tmp("Vb", [P, 2, 4, 168])
        Mx = tmp("Mx", [P, 2, 4, 8])
        mrow = tmp("mrow", [8, 2, T], BF16)
        qf = tmp("qf", [P, T])
        part = tmp("part", [P, 3, T], BF16)
        PT = tmp("PT", [P, NPT, T])
        Os = tmp("Os", [P, T])
        rdn = lrs
        parts_d = [nc.dram_tensor(f"parts{i}", (2, 3, P, T), BF16, kind="Internal").ap() for i in range(2)]
        s_pw = [ctx.enter_context(nc.semaphore(f"s_pw{i}")) for i in range(2)]
        s_pr = [ctx.enter_context(nc.semaphore(f"s_pr{i}")) for i in range(3)]
        s_mr = [ctx.enter_context(nc.semaphore(f"s_mr{i}")) for i in range(2)]
        count = {}

        def dmas(sem, pairs, *w, eng="sp"):
            count[id(sem)] = count.get(id(sem), 0) + 16 * len(pairs)
            ops = [pr.op(eng, lambda e, a=a, c=c: e.dma_start(a, c), *w, sem=sem, step=16) for a, c in pairs]
            for o in ops:
                o.value = count[id(sem)]
            return ops[-1]

        zi = [pool(lambda e: e.memset(Vb[:], 0.0)), pool(lambda e: e.memset(mrow[:], 1.0))]
        zi.append(pool(lambda e: e.memset(Vb[:, :, :, 0:144].rearrange("p a t (h j) -> p (a t) h j", j=9)[:, :, :, 8:9], 1.0), zi[0]))
        s_on = ctx.enter_context(nc.semaphore("s_on"))
        r_one = dmas(s_on, [(QK[64 * p + 48:64 * p + 49, 1], mrow[0:1, 0:1, :].broadcast_to([1, 12, T])) for p in range(2)], zi[1])

        ring = [0]

        ring = [0, 1, 2, 5]

        def take():
            ring.append(ring.pop(0))
            return ring[-1]

        r_parts, r_v, r_qk, r_mr = {}, {}, {}, {}
        h_last = [None] * NB

        def project(b):
            xn = nT[:, b, :]
            prev = None
            for i, bias in ((0, qbs[:, 0:1]), (1, col("k_b"))):
                k = take()
                m = mm(bank[k][:], wqk[:, i, :], xn, l_qk, free[f"b{k}"], r_n[b])
                q1 = actv(qf[:], bank[k][:], ACT.Identity, m, c_qb, c_v, free.get("qf"), scale=QS if i == 0 else 1.0, bias=bias)
                free[f"b{k}"] = [q1]
                h1 = dve(lambda e: e.tensor_copy(part[:, 0, :], qf[:]), q1, free.get("part"))
                yield
                m1 = tt("dve", qf[:], qf[:], part[:, 0, :], ALU.subtract, h1)
                h2 = dve(lambda e: e.tensor_copy(part[:, 1, :], qf[:]), m1, free.get("part"))
                yield
                h3 = tt("pool", part[:, 2, :], qf[:], part[:, 1, :], ALU.subtract, h2, free.get("part"))
                free["qf"] = [h3]
                prev = dmas(s_pw[b % 2], [(parts_d[b % 2][i].rearrange("k c t -> c k t"), part[:])], h1, h2, h3,
                            free.get(f"pd{b % 2}"))
                free["part"] = [prev]
                yield
            r_parts[b] = prev

        def values_of(b):
            xn = nT[:, b, :]
            k = take()
            for j in range(4):
                m = mm(bank[k][:, P * j:P * j + P], xn[:, P * j:P * j + P], wv[:], r_n[b], l_wv, free[f"b{k}"])
            vv = Vb[:, b % 2, :, 0:144].rearrange("p t (h j) -> p t h j", j=9)[:, :, :, 0:8]
            r_v[b] = actv(vv, bank[k][:].rearrange("p (t h j) -> p t h j", t=4, j=8), ACT.Copy, m, zi, free.get(f"V{b % 2}"))
            free[f"b{k}"] = [r_v[b]]
            yield

        def fetch(u):
            b, hf, s = u // 2, u % 2, u % 3
            pairs = []
            for i in range(2):
                src = parts_d[b % 2][i].rearrange("k (f p d a) t -> f p k d (a t)", f=2, a=4, p=2)[hf]
                for p in range(2):
                    for r, n, k in ((0, 3, 0), (3, 2, 1), (5, 1, 2)):
                        x = src[p, k:k + 1].broadcast_to([n, 8, 4 * T]) if i == 0 else src[p, 0:n]
                        pairs.append((QK[64 * p + 8 * r:64 * p + 8 * (r + n), i, s].rearrange("p a t -> p (a t)"), x))
            r_qk[u] = dmas(s_pr[s], pairs, r_parts[b], free.get(f"QK{s}"))
            if hf == 1:
                free[f"pd{b % 2}"] = [r_qk[u]]

        def maxima(u):
            b, s, s2 = u // 2, u % 3, u % 2
            mxs = []
            for p, a in ((0, 0), (1, 0), (0, 2), (1, 2)):
                for unit in ([(a, 0, 0), (a, 2, P)], [(a, 3, 0)], [(a, 1, 0), (a + 1, 1, 2 * P)], [(a + 1, 0, 0), (a + 1, 2, P)],
                             [(a + 1, 3, 0)]):
                    k = take()
                    for a, qi, off in unit:
                        kc = P * (qi + 1)
                        m = mm(bank[k][:, off:off + kc], QK[64 * p:64 * p + 48, 0, s, a, P * qi:P * qi + P],
                               QK[64 * p:64 * p + 48, 1, s, a, 0:kc], r_qk[u], free[f"b{k}"])
                    for a, qi, off in unit:
                        kc = P * (qi + 1)
                        x = dve(lambda e, o=bank[k][:, off:off + kc], kc=kc, h=4 * p + a, qi=qi: e.tensor_tensor_reduce(
                            o, o, mask[:, 512 - kc:512], 1.0, NEG, ALU.add, ALU.max, Mx[:, s2, qi, h:h + 1]),
                            m, c_mk, free.get(f"Mx{s2}"))
                        mxs.append(x)
                    free[f"b{k}"] = [x]
                    yield
            k = take()
            for qi in range(4):
                m = tr(bank[k][0:8, P * qi:P * qi + P], Mx[:, s2, qi, :], ident[:], mxs, free[f"b{k}"])
            free[f"Mx{s2}"] = [m]
            x = actv(mrow[:, s2, :], bank[k][0:8, :], ACT.Copy, m, r_one, free.get(f"mrow{s2}"), scale=-1.0)
            free[f"b{k}"] = [x]
            r_mr[u] = dmas(s_mr[s2], [(QK[64 * p + 48:64 * p + 49, 0, s], mrow[4 * p:4 * p + 4, s2, :]) for p in range(2)], x)
            free[f"mrow{s2}"] = [r_mr[u]]
            yield

        late = []
        later = []
        tick = [0]

        def weigh(b, g, parts, sl, ready):
            k = 3 + g % 2
            for i, kj, off in parts:
                n = T - P * kj
                m = mm(bank[k][32 * i:32 * i + 32, P * kj:T], Vb[:, b % 2, kj, 36 * g + 9 * i:36 * g + 9 * i + 32],
                       PT[:, sl, off:off + n], ready, r_v[b], free[f"b{k}"] if kj == 0 else None,
                       start=(kj == 0), stop=(kj == 3), pos=(0, 32 * i))
            free[f"PT{sl}"] = [m]
            return m

        def normalise(b, g, m):
            gg = g % 2
            o1 = actv(Os[:], bank[3 + gg][:], ACT.Copy, m, free.get("Os"))
            free[f"b{3 + gg}"] = [o1]
            yield
            yield
            k = take()
            m = mm(bank[k][:], seld[:], Os[:], o1, c_sel, free[f"b{k}"])
            e1 = actv(rdn[:, gg, :], bank[k][:], ACT.Ln, m, free.get(f"lrs{gg}"))
            free[f"b{k}"] = [e1]
            e2 = actv(rdn[:, gg, :], rdn[:, gg, :], ACT.Exp, e1, scale=-1.0)
            o2 = tt("pool", On[:, gg, :], Os[:], rdn[:, gg, :], ALU.mult, e2, free.get(f"On{gg}"))
            free["Os"] = [o2]
            free[f"lrs{gg}"] = [o2]
            r_on[g] = o2
            for _ in range(4):
                yield
            if gg == 0:
                return
            k = take()
            for j in range(2):
                m = mm(bank[k][:], wo[:, g - 1 + j, :], On[:, j, :], l_wo, z0, r_on[g - 1 + j], free[f"b{k}"],
                       start=(j == 0), stop=(j == 1))
                free[f"On{j}"] = [m]
            if g == 1:
                h_last[b] = [ts("pool", hT[:, b, :], hT[:, b, :], avec[:, 3:4], None, ALU.add, None, h_last[b] or r_n[b], c_av)]
            h_last[b] = [stt(hT[:, b, :], bank[k][:], avec[:, 0:1], hT[:, b, :], ALU.mult, ALU.add, m, h_last[b] or r_n[b])]
            free[f"b{k}"] = h_last[b]

        r_on = {}

        def settle(n):
            while len(late) > n:
                b, g, parts, sl, ready, end = late.pop(0)
                m = weigh(b, g, parts, sl, ready)
                if end:
                    if g == 3:
                        free[f"V{b % 2}"] = [m]
                    later.append(normalise(b, g, m))
            for x in list(later):
                if next(x, 0) == 0:
                    later.remove(x)

        def attend(u):
            b, hf, s = u // 2, u % 2, u % 3
            for gg in range(2):
                g = 2 * hf + gg
                units = [[(i, 0, 0)] for i in range(4)] + [[(i, 1, 0), (i, 3, 384)] for i in range(4)] + \
                    [[(i, 2, 0), (i + 2, 2, 256)] for i in range(2)]
                for parts in units:
                    k = take()
                    sl = pts[0] % NPT
                    pts[0] += 1
                    for i, kj, off in parts:
                        n = T - P * kj
                        p, a = i % 2, 2 * gg + i // 2
                        m = mm(bank[k][:, off:off + n], QK[64 * p:64 * p + 49, 1, s, a, P * kj:P * kj + P],
                               QK[64 * p:64 * p + 49, 0, s, a, P * kj:T], r_mr[u], r_qk[u], r_one, free[f"b{k}"])
                    x = actv(PT[:, sl, :], bank[k][:], ACT.Exp, m, free.get(f"PT{sl}"))
                    free[f"b{k}"] = [x]
                    if len(parts) == 1:
                        v3 = PT[:, sl, 0:P]
                        pat = [[1, P]]
                    else:
                        o2 = parts[1][2]
                        v3 = PT[:, sl, 0:512].rearrange("p (a n) -> p a n", n=P)[:, 0:o2 // P + 1:o2 // P, :]
                        pat = [[0, 2], [1, P]]
                    y = pool(lambda e, v3=v3, pat=pat: e.affine_select(
                        out=v3, in_=v3, compare_op=ALU.is_ge, fill=0.0, base=0, pattern=pat,
                        channel_multiplier=-1), x)
                    late.append((b, g, parts, sl, [x, y], parts is units[-1]))
                    settle(LAG)
                    yield
            free[f"QK{s}"] = [m]

        pts = [0]
        bc = tmp("bc", [P, 2, 4, 16])
        Bb = tmp("Bb", [P, 4, T])
        B_d = [nc.dram_tensor(f"b{i}_dram", (16, T), F32, kind="Internal").ap() for i in range(2)]
        s_bw = [ctx.enter_context(nc.semaphore(f"s_bw{i}")) for i in range(2)]
        s_br = [ctx.enter_context(nc.semaphore(f"s_br{i}")) for i in range(4)]
        slots = [0]
        sp1 = lsq
        dtv = tmp("dtv", [P, 2, 2, T])
        dtx = tmp("dtx", [P, 2, 2, T])
        dBx = tmp("dBx", [P, 4, 2, T])
        dA = tmp("dA", [P, 4, T])
        yT = tmp("yT", [P, 4, 256])
        sp2 = tmp("sp2", [P, 2, T])
        dtr = tmp("dtr", [24, T])[:]
        ring2 = [0]

        def take2():
            k = 6 + ring2[0] % 2
            ring2[0] += 1
            return k

        r_xc = [[None, None] for _ in range(NB)]
        r_z = [[None, None] for _ in range(NB)]

        def branches(b):
            s, cs, zs = b % 2, [], []
            while r_n[b] is None:
                yield
            for h in range(2):
                k = take2()
                m = mm(bank[k][:], win[:, P * h:P * h + P], nT[:, b, :], l_in, r_n[b], free[f"b{k}"])
                o = xc[:, s, h, :]
                x = actv(sp2[:, h, :], bank[k][:], ACT.Copy, m, free.get(f"sp{h}"))
                c = actv(o, bank[k][:], ACT.Identity, m, l_cw, c_v, free.get(f"xc{s}"), scale=cw[:, h, 3:4], bias=col("conv_b", h))
                free[f"b{k}"] = [c]
                yield
                for j in range(1, 4):
                    c = stt(o[:, j:T], sp2[:, h, 0:T - j], cw[:, h, 3 - j:4 - j], o[:, j:T], ALU.mult, ALU.add, c, x)
                free[f"sp{h}"] = [c]
                cs.append(c)
                yield
                k = take2()
                m = mm(bank[k][:], win[:, 256 + P * h:256 + P * h + P], nT[:, b, :], free[f"b{k}"])
                z = actv(zg[:, s, h, :], bank[k][:], ACT.Copy, m, free.get(f"zg{s}"))
                free[f"b{k}"] = [z]
                zs.append(z)
                yield
            xs = xc[:, s].rearrange("p h t -> p (h t)")
            r_xc[b] = [actv(xs, xs, ACT.Silu, cs)] * 2
            zs_ = zg[:, s].rearrange("p h t -> p (h t)")
            r_z[b] = [actv(zs_, zs_, ACT.Silu, zs)] * 2
            table("natural_log_exp_and_others")
            yield

        ssm_of = [None] * NB

        def steps_of(b):
            xcb, pb = xc[:, b % 2], b % 2
            k, k2 = take2(), take2()
            for h in range(2):
                m = mm(bank[k][0:24, :], wxp[:, h, 0:24], xcb[:, h, :], l_xp, r_xc[b][h], free[f"b{k}"], start=(h == 0), stop=(h == 1))
            for j in range(4):
                for h in range(2):
                    m2 = mm(bank[k2][:, 16 * j:16 * j + 16], xcb[:, h, P * j:P * j + P], wxp[:, h, 24:40], free[f"b{k2}"],
                            start=(h == 0), stop=(h == 1))
            e1 = actv(dtr, bank[k][0:24, :], ACT.Copy, m, free.get("dtr"))
            e2 = dve(lambda e: e.tensor_copy(bc[:, pb].rearrange("p a b -> p (a b)"), bank[k2][:, 0:64]), m2, free.get(f"bc{pb}"))
            free[f"b{k}"] = [e1]
            free[f"b{k2}"] = [e2]
            r_B = dmas(s_bw[pb], [(B_d[pb], dtr[8:24])], e1, free.get(f"B_d{pb}"))
            yield
            yield
            r_dt, dxs = [], []
            for h in range(2):
                k = take2()
                m = mm(bank[k][:], wdt[:, P * h:P * h + P], dtr[0:8], e1, l_dt, free[f"b{k}"])
                a1 = actv(sp1[:, h, :], bank[k][:], ACT.Abs, m, c_v, free.get(f"sp{h}"), free.get(f"lsq{h}"), bias=col("dt_b", h))
                v1 = actv(sp2[:, h, :], bank[k][:], ACT.Relu, a1, free.get(f"sp{h}"), bias=col("dt_b", h))
                free[f"b{k}"] = [v1]
                a2 = actv(sp1[:, h, :], sp1[:, h, :], ACT.Exp, a1, scale=-1.0)
                a3 = actv(sp1[:, h, :], sp1[:, h, :], ACT.Ln, a2, bias=1.0)
                v2 = tt("pool", dtv[:, pb, h, :], sp1[:, h, :], sp2[:, h, :], ALU.add, a3, v1, free.get(f"dtv{pb}"))
                v3 = tt("pool", dtx[:, pb, h, :], dtv[:, pb, h, :], xcb[:, h, :], ALU.mult, v2, free.get(f"dtx{pb}"))
                free[f"sp{h}"] = [v2]
                r_dt.append(v2)
                dxs.append(v3)
                yield
            free["dtr"] = [m, r_B]
            ssm_of[b] = {"bc": e2, "B": r_B, "dt": r_dt, "dx": dxs, "y": [None] * 4}

        def spread(g):
            b, n = divmod(g, 16)
            sl = g % 4
            st_ = ssm_of[b]
            st_["row", n] = dmas(s_br[sl], [(Bb[:, sl, :], B_d[b % 2][n:n + 1, :].broadcast_to([P, T]))], st_["B"],
                                 free.get(f"Bb{sl}"))
            free[f"B_d{b % 2}"] = [st_["row", n]]

        def weight(g):
            b, n = divmod(g, 16)
            sl = g % 4
            st_ = ssm_of[b]
            x = [tt("pool", dBx[:, sl, h], dtx[:, b % 2, h], Bb[:, sl], ALU.mult, st_["dx"][h], st_["row", n],
                    free.get(f"dBx{sl}{h}")) for h in range(2)]
            st_["in", n] = x
            free[f"Bb{sl}"] = x
            if n == 15:
                free[f"dtx{b % 2}"] = x

        def decay(g):
            b, n = divmod(g, 16)
            xs = []
            for h in range(2):
                i = 2 * (g % 2) + h
                xs.append(actv(dA[:, i, :], dtv[:, b % 2, h, :], ACT.Exp, ssm_of[b]["dt"][h], c_A, free.get(f"dA{i}"),
                               scale=alog[:, h, n:n + 1]))
            ssm_of[b]["decay", n] = xs
            if n == 15:
                free[f"dtv{b % 2}"] = xs

        def scan(g):
            b, n = divmod(g, 16)
            st_ = ssm_of[b]
            st_["h", n] = []
            for h in range(2):
                a, i = 2 * (g % 4) + h, 2 * (g % 2) + h
                x = dve(lambda e, a=a, i=i, h=h: e.tensor_tensor_scan(
                    hst[:, a, :], dA[:, i, :], dBx[:, g % 4, h, :], 0.0, ALU.mult, ALU.add), st_["in", n][h],
                    st_["decay", n][h], free.get(f"hst{a}"))
                free[f"dA{i}"] = [x]
                free[f"dBx{g % 4}{h}"] = [x]
                st_["h", n].append(x)

        def accumulate(g):
            b, n = divmod(g, 16)
            st_ = ssm_of[b]
            y_last, a = st_["y"], 2 * (g % 4)
            for half in range(2):
                k = take2()
                for jj in range(2):
                    for h in range(2):
                        j = 2 * half + jj
                        m = tr(bank[k][:, 256 * jj + P * h:256 * jj + P * h + P], hst[:, a + h, P * j:P * j + P],
                               ident[:], st_["h", n][h], free[f"b{k}"])
                for jj in range(2):
                    j = 2 * half + jj
                    src = bank[k][:, 256 * jj:256 * jj + 256]
                    cn = bc[:, b % 2, j, n:n + 1]
                    if n == 0:
                        y = actv(yT[:, j, :], src, ACT.Copy, m, free.get("yT"), st_["bc"], scale=cn)
                    else:
                        y = stt(yT[:, j, :], src, cn, yT[:, j, :], ALU.mult, ALU.add, m, y_last[j])
                    y_last[j] = y
                free[f"b{k}"] = [y]
            for h in range(2):
                free[f"hst{a + h}"] = [m]

        def finish(b):
            xcb, zb, st_ = xc[:, b % 2], zg[:, b % 2], ssm_of[b]
            free[f"bc{b % 2}"] = st_["y"]
            ys = []
            for h in range(2):
                k = take2()
                for j in range(4):
                    m = tr(bank[k][:, P * j:P * j + P], yT[:, j, P * h:P * h + P], ident[:], st_["y"], free[f"b{k}"])
                y = stt(xcb[:, h, :], xcb[:, h, :], col("D", h), bank[k][:], ALU.mult, ALU.add, m, st_["dx"][h])
                free[f"b{k}"] = [y]
                ys.append(tt("pool", zb[:, h, :], zb[:, h, :], xcb[:, h, :], ALU.mult, y, r_z[b][h]))
            free["yT"] = [m]
            free[f"xc{b % 2}"] = ys
            yield
            yield
            yield
            k = take2()
            for h in range(2):
                m = mm(bank[k][:], wso[:, h, :], zb[:, h, :], ys[h], l_so, free[f"b{k}"], start=(h == 0), stop=(h == 1))
            h_last[b] = [stt(hT[:, b, :], bank[k][:], avec[:, 1:2], hT[:, b, :], ALU.mult, ALU.add, m, h_last[b] or r_n[b])]
            free[f"b{k}"] = h_last[b]
            free[f"zg{b % 2}"] = [m]
            yield

        def mamba():
            yield from branches(0)
            yield from steps_of(0)
            for g in range(4):
                spread(g)
            weight(0)
            weight(1)
            decay(0)
            yield
            beside = iter(())
            behind = iter(())
            for g in range(16 * NB + BEHIND):
                b, n = divmod(g, 16)
                if b < NB:
                    if n == START and b + 1 < NB:
                        beside = chain(branches(b + 1), steps_of(b + 1))
                    if n == 11:
                        drain(beside)
                    for ahead, f in ((4, spread), (2, weight), (1, decay)):
                        if g + ahead < 16 * NB:
                            f(g + ahead)
                    scan(g)
                    next(beside, None)
                    next(behind, None)
                    yield
                if g >= BEHIND:
                    accumulate(g - BEHIND)
                    next(beside, None)
                    yield
                    if (g - BEHIND) % 16 == 15:
                        drain(behind)
                        behind = finish((g - BEHIND) // 16)
                        next(behind)
            drain(behind)

        def chain(*gens):
            for x in gens:
                yield from x

        def drain(gen):
            for _ in gen:
                pass

        def first(gen, n):
            for _ in range(n):
                next(gen, None)
                yield

        def prepare(u):
            if u + 2 < NU:
                fetch(u + 2)
            yield
            if u % 2 == 0 and u // 2 + 1 < NB:
                yield from values_of(u // 2 + 1)
            if u % 2 == 1 and (u + 3) // 2 < NB:
                yield from project((u + 3) // 2)

        NU = 2 * NB
        ssm = mamba()
        drain(project(0))
        fetch(0)
        run_together(first_norms([(1, 1)] + [(b, l) for l in range(2) for b in range(2, NB)]), 12, (ssm, 6, False))
        fetch(1)
        run_together(maxima(0), 21, (chain(values_of(0), project(1)), 8, True), (ssm, OFF, False))
        tops = chain(*[maxima(u) for u in range(1, NU)])
        run_together(first(tops, LEAD), LEAD, (ssm, SSM_RATE * LEAD / 20, False))
        for u in range(NU):
            run_together(attend(u), 20, (ssm, SSM_RATE, False), (tops, 21, False), (prepare(u), 8, True))
        while late or later:
            settle(0)
        drain(ssm)
        r_sm = [h_last[b][0] for b in range(NB)]
        scr.close()
        scr0.close()

        xT = sb("xT", [P, NB, T])
        lwT = sb("lwT", [P, 6, P])
        lwf = lwT[:].rearrange("p a b -> p (a b)")
        brow = sb("brow", [1, 3 * P])
        done4 = r_sm + [pr.queues[e][-1] for e in ("pe", "dve", "act", "pool")]
        scr = ExitStack()
        xin2 = tmp("xin2", [P, 2, 4, P])
        we1h = tmp("we1h", [P, 10, 512], F32R)
        we1l = tmp("we1l", [P, 10, 512], F32R)
        we2h = tmp("we2h", [P, 10, 4, P], F32R)
        we2l = tmp("we2l", [P, 10, 4, P], F32R)
        stage = tmp("stage", [P, 6, 512])
        r_we = [None] * 10

        def split_weights(i, e):
            s1, s2 = stage[:, 2 * (i % 3), :], stage[:, 2 * (i % 3) + 1, :].rearrange("p (k n) -> p k n", k=4)
            a1, a2 = {9: (d["L0_attn_ffn_w1"], d["L0_attn_ffn_w2"]), 8: (d["L0_ffn_Ws1"], d["L0_ffn_Ws2"])}.get(e) or \
                (d["L0_ffn_We1"][e], d["L0_ffn_We2"][e])
            ld = [dma(s1, a1, done4, free.get(f"stage{i % 3}")),
                  dma(s2, a2.rearrange("(k p) n -> p k n", p=P), done4, free.get(f"stage{i % 3}"))]
            x1 = dve(lambda q: q.tensor_copy(we1h[:, e, :], s1), ld, done4)
            x2 = dve(lambda q: q.tensor_copy(we2h[:, e], s2), ld, done4)
            x1 = tt("pool", we1l[:, e, :], s1, we1h[:, e, :].bitcast(F32), ALU.subtract, x1)
            x2 = tt("pool", we2l[:, e], s2, we2h[:, e].bitcast(F32), ALU.subtract, x2)
            free[f"stage{i % 3}"] = r_we[e] = [x1, x2]

        for i in range(8):
            free[f"b{i}"] = free[f"b{i}"] + done4
        r_h2 = layer_norms([((nT[:, b, :], hT[:, b, :], col("ln2_w"), col("ln2_b"), BK[b % 4], r_sm[b], done4), {})
                            for b in range(NB)])
        split_weights(0, 9)
        r_x2 = [None] * NB
        x3 = tmp("x3", [P, 2, 2, T], F32R)
        hh = tmp("hh", [P, 6, T], F32R)
        hl = tmp("hl", [P, 6, T], F32R)
        full = lsq

        def pass3(o, a, b, first, last, *w):
            mm(o, a[0], b[0], *w, start=first, stop=False)
            mm(o, a[0], b[1], start=False, stop=False)
            return mm(o, a[1], b[0], start=False, stop=last)

        units = [0]
        r_split = {}

        def split(b, *w):
            x = dve(lambda e, b=b: e.tensor_copy(x3[:, b % 2, 0, :], nT[:, b, :]), w, free.get(f"x3{b % 2}"), done4)
            y = tt("dve", x3[:, b % 2, 1, :], nT[:, b, :], x3[:, b % 2, 0, :].bitcast(F32), ALU.subtract, x)
            free[f"nT{b}"] = [y]
            r_split[b] = [x, y]

        def up(b, e, i, c):
            k, sl = c, (4 * i + c) % 6
            f = c % 2
            cs = slice(P * c, P * c + P)
            m = pass3(bank[k][:], (we1h[:, e, cs], we1l[:, e, cs]), (x3[:, b % 2, 0, :], x3[:, b % 2, 1, :]),
                      True, True, r_split[b], r_we[e], free[f"b{k}"])
            free[f"x3{b % 2}"] = [m]
            bias = col("ffn_b1", c) if e == 9 else col("bs1", c) if e == 8 else col("be1", 4 * e + c)
            fn = ACT.Gelu if e == 9 else ACT.Silu
            x = actv(full[:, f, :], bank[k][:], fn, m, free.get(f"lsq{f}"), bias=bias)
            if c in SECOND and e < 9:
                y = dve(lambda q: q.tensor_copy(hh[:, sl, :], full[:, f, :]), x, free.get(f"hh{sl}"))
                free[f"b{k}"] = [x]
            else:
                y = actv(hh[:, sl, :], bank[k][:], fn, m, free.get(f"hh{sl}"), bias=bias)
                free[f"b{k}"] = [y]
            z = tt("dve", hl[:, sl, :], full[:, f, :], hh[:, sl, :].bitcast(F32), ALU.subtract, x, y, free.get(f"hh{sl}"))
            free[f"lsq{f}"] = [z]
            return [y, z]

        def down(b, e, i, c, ready):
            sl, o = (4 * i + c) % 6, 6 + i % 2
            m = pass3(bank[o][:], (we2h[:, e, c, :], we2l[:, e, c, :]), (hh[:, sl, :], hl[:, sl, :]),
                      c == 0, c == 3, ready, free[f"b{o}"])
            free[f"hh{sl}"] = [m]
            return m

        queue = []

        def expert(b, e, end, *w):
            cur, prev = None, queue.pop(0) if queue else None
            if b is not None:
                cur = (b, e, units[0], end, [])
                units[0] += 1
            for c in range(4):
                if cur:
                    cur[4].append(up(b, e, cur[2], c))
                if prev:
                    m = down(prev[0], prev[1], prev[2], c, prev[4][c])
                yield
            if prev:
                prev[3](prev[0], prev[1], 6 + prev[2] % 2, m)
            if cur:
                queue.append(cur)

        def ffn_end(b, e, k, m):
            a = stt(hT[:, b, :], bank[k][:], col("ffn_b2"), hT[:, b, :], ALU.add, ALU.add, m, r_h2[b])
            free[f"b{k}"] = [a]
            r_x2[b] = stt(xT[:, b, :], hT[:, b, :], gate(0, b), xT[:, b, :], ALU.mult, ALU.add, a, c_g, r_xT[b])

        r_xT = [None] * NB
        l_x2 = {}

        def load_x(b):
            l_x2[b] = dma(xin2[:, b % 2], xd[b], free.get(f"xin2{b % 2}"), done4)

        load_x(0)
        split(0, r_h2[0])
        for b in range(NB):
            if b + 1 < NB:
                load_x(b + 1)
                split(b + 1, r_h2[b + 1])
            k = 4 + b % 2
            for j in range(4):
                m = tr(bank[k][:, P * j:P * j + P], xin2[:, b % 2, j, :], ident[:], l_x2[b], free[f"b{k}"])
            free[f"xin2{b % 2}"] = [m]
            r_xT[b] = actv(xT[:, b, :], bank[k][:], ACT.Copy, m, done4)
            free[f"b{k}"] = [r_xT[b]]
            drain(expert(b, 9, ffn_end))
            if b < 4:
                split_weights(b + 1, (8, 0, 1, 2)[b])
        drain(expert(None, None, None))

        table("natural_log_exp_and_others")
        hr = On[0:33]
        lg = tmp("lg", [P, 32, 8])
        pb_, oh, pk, wgt = [a.rearrange("p (t e) -> p t e", e=8) for w in (win, wo[:].rearrange("p a b -> p (a b)"))
                            for a in (w[:, 0:256], w[:, 256:512])]
        iot = tmp("iot", [P, 8])
        st = wso[:].rearrange("p a (b t) -> p (a b) t", t=32)
        iot_i = tmp("iot_i", [P, 8], mybir.dt.int32)
        h1 = dve(lambda e: e.memset(hr[32:33, :, :], 1.0), done4)
        io = pool(lambda e: e.iota(iot_i[:], pattern=[[-1, 8]], base=8, channel_multiplier=0), done4)
        io = pool(lambda e: e.tensor_copy(iot[:], iot_i[:]), io)
        def bcast(a):
            return a.rearrange("p (t o) -> p t o", o=1).broadcast_to([P, 32, 8])

        def red(dst, src, op, *w):
            return dve(lambda e: e.tensor_reduce(dst, src, AX.X, op), *w)

        wT, wrow = hT[64:97], hT[0:1]
        r_wT = []

        r_h3 = [None] * NB
        r_log = []
        wT1 = dve(lambda e: e.memset(wT[32:33, :, :], 1.0), r_x2)

        def logits():
            hid = {}
            for b in range(NB + 1):
                while b < NB and r_h3[min(b + 2, NB - 1)] is None:
                    yield
                if b < NB:
                    m = mm(bank[7][0:32, :], wr1[:], nT[:, b, :], r_h3[b], l_rest["wr1"], free["b7"])
                    hid[b] = ts("dve", hr[0:32, b % 2, :], bank[7][0:32, :], br1[:, 0:1], 0.0, ALU.add, ALU.max, m,
                                l_rest["br1"], free.get(f"hr{b % 2}"), done4)
                    free["b7"] = [hid[b]]
                if b:
                    s = (b - 1) % 2
                    for j in range(4):
                        o = 32 * b - 32 + 8 * j
                        m = mm(bank[5][:, o:o + 8], hr[:, s, P * j:P * j + P], wr2[:], hid[b - 1], h1, l_rest["wr2"],
                               l_rest["br2"], free["b5"])
                    free[f"hr{s}"] = [m]
                yield
            r_log.append(m)

        run_together(norms([(r_h3, b, (nT[:, b, :], xT[:, b, :], mod[:, 0, 4, b:b + 1], mod[:, 0, 3, b:b + 1],
                                       ((0, 4), (1, 6), (2, 4), (3, 6))[b % 4], r_x2[b]), {"dst_free": free[f"nT{b}"]})
                            for b in range(NB)]), 8, (logits(), 8, True))

        def route():
            m = r_log[0]
            lgf = lg[:].rearrange("p t e -> p (t e)")
            x = dve(lambda e: e.tensor_copy(lgf, bank[5][:, 0:256]), m, done4)
            yield
            free["b5"] = [x]

            x = red(st[:, 0, :], lg[:], ALU.max, x)
            yield
            x = tt("dve", lg[:], lg[:], bcast(st[:, 0, :]), ALU.subtract, x)
            yield
            x = actv(pb_[:], lg[:], ACT.Exp, x)
            yield
            x = red(st[:, 1, :], pb_[:], ALU.add, x)
            yield
            x = dve(lambda e: e.reciprocal(st[:, 2, :], st[:, 1, :]), x)
            yield
            x = tt("dve", pb_[:], pb_[:], bcast(st[:, 2, :]), ALU.mult, x)
            yield
            iob = iot[:].rearrange("p (o e) -> p o e", o=1).broadcast_to([P, 32, 8])
            x = red(st[:, 3, :], pb_[:], ALU.max, x)
            yield
            y = tt("dve", oh[:], pb_[:], bcast(st[:, 3, :]), ALU.is_equal, x)
            yield
            y = tt("dve", pk[:], oh[:], iob, ALU.mult, y, io)
            yield
            y = red(st[:, 4, :], pk[:], ALU.max, y)
            yield
            y1 = tt("dve", oh[:], iob, bcast(st[:, 4, :]), ALU.is_equal, y)
            yield
            y = stt(pb_[:].rearrange("p t e -> p (t e)"), oh[:].rearrange("p t e -> p (t e)"), -4.0,
                    pb_[:].rearrange("p t e -> p (t e)"), ALU.mult, ALU.add, y1)
            y = red(st[:, 5, :], pb_[:], ALU.max, y)
            yield
            z = tt("dve", pk[:], pb_[:], bcast(st[:, 5, :]), ALU.is_equal, y)
            yield
            z = tt("dve", pk[:], pk[:], iob, ALU.mult, z)
            yield
            z = red(st[:, 6, :], pk[:], ALU.max, z)
            yield
            z = tt("dve", pk[:], iob, bcast(st[:, 6, :]), ALU.is_equal, z)
            yield
            y = tt("dve", st[:, 7, :], st[:, 5, :], st[:, 3, :], ALU.subtract, y)
            yield
            y = actv(st[:, 0, :], st[:, 7, :], ACT.Exp, y, scale=0.5)
            yield
            y = ts("dve", st[:, 1, :], st[:, 0, :], 1.0, None, ALU.add, None, y)
            yield
            y = dve(lambda e: e.reciprocal(st[:, 2, :], st[:, 1, :]), y)
            yield
            y2 = tt("dve", st[:, 4, :], st[:, 0, :], st[:, 2, :], ALU.mult, y, y1)
            yield
            z = tt("dve", pk[:], pk[:], bcast(st[:, 4, :]), ALU.mult, z, y2)
            yield
            y = tt("dve", oh[:], oh[:], bcast(st[:, 2, :]), ALU.mult, y)
            yield
            r_w = tt("dve", wgt[:], oh[:], pk[:], ALU.add, y, z)
            yield
            r_wT.clear()
            for b in range(NB):
                k = 4
                for j in range(4):
                    m = tr(bank[k][0:8, P * j:P * j + P], wgt[:, 4 * b + j, :], ident[:], r_w, free[f"b{k}"])
                x = actv(wT[0:8, b, :], bank[k][0:8, :], ACT.Copy, m, wT1)
                free[f"b{k}"] = [x]
                r_wT.append(x)
                yield

        prd = lrs
        acc = stage[:, 0:2, :]
        wbc = stage[:, 2:6, :]
        r_x3 = [None] * NB
        last_acc = {}
        r_wb = {}

        def moe_end(b, e, k, m):
            if e == 8:
                x = r_xs[b] = stt(xT[:, b, :], bank[k][:], gate(1, b), xT[:, b, :], ALU.mult, ALU.add, m, r_h3[b])
            else:
                x = tt("dve", prd[:, e % 2, :], bank[k][:], wbc[:, e % 4, :], ALU.mult, m, r_wb[b, e], free.get(f"lrs{e % 2}"))
                free[f"wbc{e % 4}"] = [x]
                last_acc[b] = tt("pool", acc[:, b % 2, :], acc[:, b % 2, :], prd[:, e % 2, :], ALU.add, x, last_acc[b])
                free[f"lrs{e % 2}"] = [last_acc[b]]
            free[f"b{k}"] = [x]
            if e == 7:
                r_x3[b] = stt(xT[:, b, :], acc[:, b % 2, :], gate(1, b), xT[:, b, :], ALU.mult, ALU.add, last_acc[b], r_xs[b])
                free[f"acc{b % 2}"] = [r_x3[b]]

        r_xs = [None] * NB

        def shared():
            split(0, r_h3[0])
            for b in range(NB):
                split((b + 1) % NB, r_h3[(b + 1) % NB])
                if b < 5:
                    split_weights(b + 5, b + 3)
                yield from expert(b, 8, moe_end)

        lw0 = xin2[:].rearrange("p a b c -> p (a b) c")[:, 0:6, :]
        l_w6 = [dma(lw0[:, i, :], d[w], free["xin20"], free["xin21"]) for i, w in enumerate(
            ["L1_attn_Wq", "L1_attn_Wk", "L1_attn_Wv", "L1_ffn_W_r", "L1_ffn_W_k", "L1_ffn_W_v"])]
        l_b3 = [dma(brow[0:1, P * i:P * i + P], d[w].rearrange("(o c) -> o c", o=1), done4)
                for i, w in enumerate(["L1_attn_bq", "L1_attn_bk", "L1_attn_bv"])]
        run_together(shared(), 32, (route(), ROUTE, True))
        for i in range(6):
            m = tr(bank[4 + i // 4][:, P * (i % 4):P * (i % 4) + P], lw0[:, i, :], ident[:], l_w6, free[f"b{4 + i // 4}"])
        c_lw = [actv(lwf[:, 0:512], bank[4][:], ACT.Copy, m, done4), actv(lwf[:, 512:768], bank[5][:, 0:256], ACT.Copy, m, done4)]
        free["b4"] = [c_lw[0]]
        free["b5"] = [c_lw[1]]
        n4 = nT[:].rearrange("p b t -> p (b t)").rearrange("p (r s t j) -> p r s t j", r=4, s=8, t=2)
        r_h4 = [None] * NB
        r_w4 = [pr.queues["dve"][-1], pr.queues["pe"][-1]]

        def norm4(b):
            return norm_start(n4[:, b // 2, :, b % 2, :], xT[:, b, :], mod[:, 1, 1, b:b + 1], mod[:, 1, 0, b:b + 1],
                              (4, 5), r_x3[b], r_w4, fold=8, squares=(win, "win"), dst_free=free[f"nT{b - b % 2}"] + free[f"nT{b - b % 2 + 1}"])

        for b in range(NB):
            k = 4 + b % 2
            m = mm(bank[k][:], bsum[64:97, :], wT[:, b, :], r_wT[b], l_rest["be2"], l_rest["bs2"], free[f"b{k}"])
            last_acc[b] = actv(acc[:, b % 2, :], bank[k][:], ACT.Copy, m, free.get(f"acc{b % 2}"), r_we)
            free[f"b{k}"] = [last_acc[b]]
            r_row = dma(wrow, wT[0:8, b, :], r_wT[b], free.get("wrow"), r_x2)
            for e in range(8):
                r_wb[b, e] = pool(lambda q, e=e: q.partition_broadcast(wbc[:, e % 4, :], wrow[0:1, e, :], P), r_row,
                                  free.get(f"wbc{e % 4}"), r_we)
                free["wrow"] = [r_wb[b, e]]
                if e == 3 and b + 1 < NB:
                    split(b + 1, r_h3[b + 1])
                if b and b % 2 == 0 and e in (1, 3):
                    half = norm4(b - 2 + e // 2)
                if b and b % 2 == 0 and e in (2, 4):
                    table("natural_log_exp_and_others")
                    r_h4[b - 3 + e // 2] = half()
                drain(expert(b, e, moe_end))
        drain(expert(None, None, None))
        scr.close()

        done6 = r_x3 + [pr.queues[e][-1] for e in ("pe", "dve", "act", "pool")]
        scr = ExitStack()
        for i in range(8):
            free[f"b{i}"] = free[f"b{i}"] + done6
        table("natural_log_exp_and_others")
        bhl = tmp("bhl", [33, 3 * P], F32R)
        onr = tmp("onr", [33, P], F32R)
        zer = tmp("zer", [33, 3 * P])
        z = dve(lambda e: e.memset(zer[:], 0.0), done6)
        x = dve(lambda e: e.tensor_copy(bhl[:], zer[:]), z)
        hi = dve(lambda e: e.tensor_copy(bhl[0:1, :], brow[:]), l_b3, x)
        lo = tt("dve", brow[:], brow[:], bhl[0:1, :].bitcast(F32), ALU.subtract, hi)
        lo = dve(lambda e: e.tensor_copy(bhl[32:33, :], brow[:]), lo, x)
        o = dve(lambda e: e.tensor_copy(onr[:], zer[:, 0:P]), z)
        c_b3 = [hi, lo, dve(lambda e: e.tensor_copy(onr[0:1, :], ones[:]), c_on, o),
                dve(lambda e: e.tensor_copy(onr[32:33, :], ones[:]), c_on, o)]
        qkv = tmp("qkv", [P, 3, 3, 8, P])
        prod = tmp("prod", [P, 9, 8, P])
        scs = tmp("scs", [P, 2, 8, 64])
        mx1 = tmp("mx1", [P, 64])
        ex1 = tmp("ex1", [P, 64])
        sm1 = tmp("sm1", [P, 64])
        r_x4 = [[r_x3[b]] for b in range(NB)]
        big4 = xT[:].rearrange("p b (j t) -> p b j t", t=8)
        ON_DVE = (1, 4, 7)
        r_qkv, r_scs, r_soft, prods = {}, {}, {}, [0, 0]

        def project4(r):
            sl = r % 3
            r_qkv[r] = []
            for s_ in range(8):
                k = s_ % 4
                lt = n4[:, r, s_].rearrange("p t j -> p (t j)")
                mm(bank[k][:, 0:384], lt, lwf[:, 0:384], c_lw, r_h4[2 * r], r_h4[2 * r + 1], free[f"b{k}"],
                   start=True, stop=False)
                m = mm(bank[k][:, 0:384], onr[:], bhl[:], c_b3, start=False, stop=True)
                a = actv(qkv[:, sl, 0, s_, :], bank[k][:, 0:128], ACT.Copy, m, free.get(f"qkv{sl}"), done6, scale=0.25)
                a = actv(qkv[:, sl, 1:3, s_, :], bank[k][:, 128:384].rearrange("p (a c) -> p a c", a=2), ACT.Copy, m)
                free[f"b{k}"] = [a]
                r_qkv[r].append(a)
                yield

        def scores4(r):
            sl = r % 3
            r_scs[r] = []
            while len(r_qkv[r]) < 8:
                yield
            for s_ in range(8):
                w = prods[0] % 4
                prods[0] += 1
                x = tt("dve" if s_ in ON_DVE else "pool", prod[:, w], qkv[:, sl, 0, s_:s_ + 1, :].broadcast_to([P, 8, P]),
                       qkv[:, sl, 1], ALU.mult, r_qkv[r], free.get(f"prod{w}"), done6)
                y = dve(lambda e, w=w, s_=s_: e.tensor_reduce(scs[:, r % 2, :, 8 * s_:8 * s_ + 8],
                                                              prod[:, w].rearrange("p a (h x) -> p a h x", x=16),
                                                              AX.X, ALU.add), x, free.get(f"scs{r % 2}"), done6)
                free[f"prod{w}"] = [y]
                r_scs[r].append(y)
                yield

        def softmax4(r):
            sc, sl = scs[:, r % 2], r % 3
            x = dve(lambda e: e.tensor_reduce(mx1[:], sc.rearrange("p k s -> p s k"), AX.X, ALU.max), r_scs[r],
                    free.get("mx1"), done6)
            x = ts("dve", mx1[:], mx1[:], 0.0, None, ALU.max, None, x)
            mb = mx1[:].rearrange("p (o s) -> p o s", o=1).broadcast_to([P, 8, 64])
            y = tt("dve", sc, sc, mb, ALU.subtract, x)
            e0 = actv(ex1[:], mx1[:], ACT.Exp, x, free.get("ex1"), done6, scale=-1.0)
            e1 = actv(sc.rearrange("p k s -> p (k s)"), sc.rearrange("p k s -> p (k s)"), ACT.Exp, y)
            free["mx1"] = [e0, y]
            yield
            y = dve(lambda e: e.tensor_reduce(sm1[:], sc.rearrange("p k s -> p s k"), AX.X, ALU.add), e1, free.get("sm1"), done6)
            yield
            y = stt(sm1[:], ex1[:], 57.0, sm1[:], ALU.mult, ALU.add, y, e0)
            free["ex1"] = [y]
            y = dve(lambda e: e.reciprocal(sm1[:], sm1[:]), y)
            sb_ = sm1[:].rearrange("p (o s) -> p o s", o=1).broadcast_to([P, 8, 64])
            y = tt("dve", sc, sc, sb_, ALU.mult, y)
            free["sm1"] = [y]
            r_soft[r] = y
            yield

        def values4(r):
            sc, sl, y = scs[:, r % 2], r % 3, r_soft[r]
            xs = []

            def add(s_, x, w):
                k = 4 + 2 * (r % 2) + s_ // 4
                j = s_ % 4
                for key in range(8):
                    m = mm(bank[k][:, P * j:P * j + P], prod[:, w, key, :], ident[:], x, free[f"b{k}"] if j == 0 else None,
                           start=(key == 0), stop=(key == 7))
                free[f"prod{w}"] = [m]
                if j == 3:
                    ends.append((k, m))

            def end(k, m):
                for j in range(4):
                    s_ = 4 * (k % 2) + j
                    dst = big4[:, s_, :, 2 * r:2 * r + 2].rearrange("p j t -> p t j")
                    x = stt(dst, bank[k][:, P * j:P * j + P].rearrange("p (t j) -> p t j", t=2), gate(2, s_), dst,
                            ALU.mult, ALU.add, m, r_x4[s_], r_h4[s_])
                    r_x4[s_] = [x]
                free[f"b{k}"] = [x]

            ends = []
            wait = []
            for s_ in range(8):
                w = 4 + prods[1] % 5
                prods[1] += 1
                pr4 = sc[:, :, 8 * s_:8 * s_ + 8].rearrange("p k (h o) -> p k h o", o=1).broadcast_to([P, 8, 8, 16])
                x = tt("dve" if s_ in ON_DVE else "pool", prod[:, w].rearrange("p k (h x) -> p k h x", x=16), pr4,
                       qkv[:, sl, 2].rearrange("p k (h x) -> p k h x", x=16), ALU.mult, y, free.get(f"prod{w}"), done6)
                xs.append(x)
                wait.append((s_, x, w))
                if len(wait) > 2:
                    add(*wait.pop(0))
                if s_ == 7:
                    end(*ends.pop(0))
                    free[f"scs{r % 2}"] = xs
                    free[f"qkv{sl}"] = xs
                yield
            for w in wait:
                add(*w)
                yield
            yield
            end(*ends.pop(0))

        drain(project4(0))
        run_together(scores4(0), 8, (project4(1), 8, True))
        drain(softmax4(0))
        for b in (6, 7):
            r_h4[b] = norm4(b)()
        rest = iter(())
        for r in range(4):
            before, rest = rest, values4(r)
            parts = [(before, 4, True)]
            if r < 3:
                parts.append((chain(scores4(r + 1), softmax4(r + 1)), S4, True))
            if r < 2:
                parts.append((project4(r + 2), 8, True))
            run_together(first(rest, 8), 8, *parts)
        drain(rest)

        att_done = [pr.queues["pe"][-1]]
        r_h5 = layer_norms([((hT[:, b, :], xT[:, b, :], mod[:, 1, 4, b:b + 1], mod[:, 1, 3, b:b + 1], BK[b % 4],
                              r_x4[b], done6), {}) for b in range(NB)])
        fl = tmp("fl", [P, 5120])
        mu1 = tmp("mu1", [P, 2])
        xr = fl[:, 0:2048].rearrange("p (s i t) -> p s i t", s=2, i=2)
        rr = fl[:, 2048:3072].rearrange("p (s t) -> p s t", s=2)
        kk = fl[:, 3072:4096].rearrange("p (s t) -> p s t", s=2)
        oo = fl[:, 4096:5120].rearrange("p (s j c) -> p s j c", s=2, j=4)
        um = [ts("dve", mu1[:, i:i + 1], col(n_), -1.0, 1.0, ALU.mult, ALU.add, c_v, done6) for i, n_ in enumerate(("mu_r", "mu_k"))]
        stores = []
        od = out.rearrange("b (n p) c -> b p n c", p=P)
        mixd, r1, k2, r_x5 = {}, {}, {}, {}

        def mix5(b):
            s = b % 2
            mixd[b] = []
            for i, n_ in enumerate(("mu_r", "mu_k")):
                x = actv(xr[:, s, i, :], hT[:, b, :], ACT.Copy, r_h5[b], free.get(f"xr{s}"), done6, scale=col(n_))
                x = stt(xr[:, s, i, 1:T], hT[:, b, 0:T - 1], mu1[:, i:i + 1], xr[:, s, i, 1:T], ALU.mult, ALU.add, x, um)
                mixd[b].append(x)

        def keys5(b):
            s = b % 2
            k = 2 * s
            m = mm(bank[k][:], lwT[:, 3, :], xr[:, s, 0, :], mixd[b][0], c_lw, free[f"b{k}"])
            r1[b] = actv(rr[:, s, :], bank[k][:], ACT.Sigmoid, m, free.get(f"rr{s}"), done6)
            free[f"b{k}"] = [r1[b]]
            k += 1
            m = mm(bank[k][:], lwT[:, 4, :], xr[:, s, 1, :], mixd[b][1], free[f"b{k}"])
            free[f"xr{s}"] = [m]
            x = actv(kk[:, s, :], bank[k][:], ACT.Relu, m, free.get(f"kk{s}"), done6)
            free[f"b{k}"] = [x]
            k2[b] = tt("pool", kk[:, s, :], kk[:, s, :], kk[:, s, :], ALU.mult, x)

        def values5(b):
            s = b % 2
            k = 4 + s
            m = mm(bank[k][:], lwT[:, 5, :], kk[:, s, :], k2[b], free[f"b{k}"])
            free[f"kk{s}"] = [m]
            x = tt("dve", rr[:, s, :], bank[k][:], rr[:, s, :], ALU.mult, m, r1[b])
            free[f"b{k}"] = [x]
            x = r_x5[b] = stt(xT[:, b, :], rr[:, s, :], gate(3, b), xT[:, b, :], ALU.mult, ALU.add, x, r_x4[b], r_h5[b])
            free[f"rr{s}"] = [x]

        def store5(b):
            s = b % 2
            k = 6 + s
            for j in range(4):
                m = tr(bank[k][:, P * j:P * j + P], xT[:, b, P * j:P * j + P], ident[:], r_x5[b], free[f"b{k}"])
            y = actv(oo[:, s].rearrange("p a c -> p (a c)"), bank[k][:], ACT.Copy, m, free.get(f"oo{s}"), done6)
            free[f"b{k}"] = [y]
            w = dma(od[b], oo[:, s], y)
            free[f"oo{s}"] = [w]
            stores.append(w)

        staggered(NB, mix5, keys5, values5, store5)

        sems = {e: ctx.enter_context(nc.semaphore(f"s_{e}")) for e in pr.queues}
        pr.number(sems)
        block = ctx.enter_context(nc.Block())

        @block.tensor
        def _(e):
            pr.emit("pe", e)

        @block.vector
        def _(e):
            pr.emit("dve", e)

        @block.scalar
        def _(e):
            pr.emit("act", e)

        @block.gpsimd
        def _(e):
            pr.emit("pool", e)

        @block.sync
        def _(e):
            pr.emit("sp", e)
            for w in stores:
                e.wait_ge(w.sem, w.value)
        scr.close()


_INS = ['L0_attn_x', 'L0_attn_ln1_w', 'L0_attn_ln1_b', 'L0_attn_ln2_w', 'L0_attn_ln2_b', 'L0_attn_q_w', 'L0_attn_q_b',
        'L0_attn_k_w', 'L0_attn_k_b', 'L0_attn_v_w', 'L0_attn_v_b', 'L0_attn_o_w', 'L0_attn_o_b', 'L0_attn_in_proj_w',
        'L0_attn_conv_w', 'L0_attn_conv_b', 'L0_attn_x_proj_w', 'L0_attn_dt_w', 'L0_attn_dt_b', 'L0_attn_A_log',
        'L0_attn_D_param', 'L0_attn_ssm_out_w', 'L0_attn_mix_weight', 'L0_attn_ffn_w1', 'L0_attn_ffn_b1',
        'L0_attn_ffn_w2', 'L0_attn_ffn_b2', 'L0_ffn_Wr1', 'L0_ffn_br1', 'L0_ffn_Wr2', 'L0_ffn_br2', 'L0_ffn_Ws1',
        'L0_ffn_bs1', 'L0_ffn_Ws2', 'L0_ffn_bs2', 'L0_ffn_We1', 'L0_ffn_be1', 'L0_ffn_We2', 'L0_ffn_be2', 'L0_c',
        'L0_wmod', 'L1_attn_Wq', 'L1_attn_bq', 'L1_attn_Wk', 'L1_attn_bk', 'L1_attn_Wv', 'L1_attn_bv', 'L1_ffn_W_r',
        'L1_ffn_W_k', 'L1_ffn_W_v', 'L1_ffn_mu_r', 'L1_ffn_mu_k', 'L1_c', 'L1_wmod']


def kernel(**inputs):
    import numpy as _np
    import concourse.bacc as _bacc
    from concourse import mybir as _mybir
    from concourse.bass_utils import run_bass_kernel_spmd as _run

    nc = _bacc.Bacc("TRN2", target_bir_lowering=False, num_devices=1)
    arrays, args = {}, {}
    for name in _INS:
        a = _np.ascontiguousarray(inputs[name])
        arrays[f"in_{name}_dram"] = a
        args[name] = nc.dram_tensor(f"in_{name}_dram", a.shape, _mybir.dt.from_np(a.dtype), kind="ExternalInput").ap()
    out = nc.dram_tensor("out_0_dram", (8, 512, 128), _mybir.dt.float32, kind="ExternalOutput").ap()
    build(nc, args, out)
    r = _run(nc, [arrays], core_ids=[0])
    return r.results[0]["out_0_dram"]
```
